# Optimizing a Trainium2 kernel written in Bass

```python
import numpy as np
import jax
import jax.numpy as jnp

def _softmax(x, axis=-1):
    return jax.nn.softmax(x, axis=axis)

def _gelu(x):
    return jax.nn.gelu(x, approximate=True)

def _silu(x):
    return jax.nn.silu(x)

def _sigmoid(x):
    return jax.nn.sigmoid(x)

def _layernorm(x, axis=-1, eps=1e-05):
    m = jnp.mean(x, axis=axis, keepdims=True)
    v = jnp.var(x, axis=axis, keepdims=True)
    return (x - m) / jnp.sqrt(v + eps)

def _scatter_add(tgt, idx, src, axis=0):
    return tgt.at[idx].add(src)

def _segment_sum(src, seg, n):
    return jax.ops.segment_sum(src, seg, n)
kernel_name = 'mk_vit_tower_postln_d1_tok_img768_r4_9e1d5a'

def setup_inputs(seed: int=0):
    np.random.seed(seed)
    _w = jnp.asarray

    def _rec_inputs():
        import jax
        import jax.numpy as jnp
        _rk = jax.random.key(seed)
        x = -0.000596345 + 1.00056 * jax.random.normal(jax.random.fold_in(_rk, 1), (16, 3, 64, 64), jnp.float32)
        return x
    x = _rec_inputs()

    def _L0_tok_setup():
        import jax, jax.numpy as jnp
        import numpy as np
        B = 16
        IMG = 64
        CH = 3
        EMBED = 64
        GP = 16
        PRE = [1, 2, 4]
        N_LEVELS = 3
        FUSED = EMBED * N_LEVELS

        def hilbert_flat_indices(n):
            t = np.arange(n * n, dtype=np.int64)
            x = np.zeros(n * n, dtype=np.int64)
            y = np.zeros(n * n, dtype=np.int64)
            s = 1
            while s < n:
                rx = 1 & t // 2
                ry = 1 & (t ^ rx)
                swap = ry == 0
                flip = swap & (rx == 1)
                x = np.where(flip, s - 1 - x, x)
                y = np.where(flip, s - 1 - y, y)
                x2 = np.where(swap, y, x)
                y2 = np.where(swap, x, y)
                x, y = (x2, y2)
                x = x + s * rx
                y = y + s * ry
                t = t // 4
                s *= 2
            return y * n + x

        def _level(x, idx, W, b, p, gp):
            Bsz, C, H, _ = x.shape
            h = H // p
            t = x.reshape(Bsz, C, h, p, h, p).transpose(0, 2, 4, 3, 5, 1).reshape(Bsz, h * h, p * p * C)
            t = t[:, idx]
            t = t.reshape(Bsz, h * h // gp, gp * p * p * C)
            return t @ W.T + b

        def _interp_linear(x, n_out):
            L = x.shape[1]
            pos = (jnp.arange(n_out, dtype=jnp.float32) + 0.5) * (L / n_out) - 0.5
            pos = jnp.clip(pos, 0.0, L - 1)
            i0 = jnp.floor(pos).astype(jnp.int32)
            i1 = jnp.minimum(i0 + 1, L - 1)
            w = (pos - i0).astype(x.dtype)
            return x[:, i0] * (1.0 - w)[None, :, None] + x[:, i1] * w[None, :, None]
        key = jax.random.key(seed)
        ks = jax.random.split(key, 9)
        inp = {'x': jax.random.normal(ks[0], (B, CH, IMG, IMG), jnp.float32)}
        for i, p in enumerate(PRE):
            din = CH * p * p * GP
            inp[f'W{i}'] = jax.random.normal(ks[1 + 2 * i], (EMBED, din), jnp.float32) * din ** (-0.5)
            inp[f'b{i}'] = jax.random.normal(ks[2 + 2 * i], (EMBED,), jnp.float32) * 0.02
        inp['Wf'] = jax.random.normal(ks[7], (FUSED, FUSED), jnp.float32) * FUSED ** (-0.5)
        inp['bf'] = jax.random.normal(ks[8], (FUSED,), jnp.float32) * 0.02
        for i, p in enumerate(PRE):
            inp[f'idx{i}'] = jnp.asarray(hilbert_flat_indices(IMG // p), jnp.int32)
        return inp
    _L0_tok_all = _L0_tok_setup()
    _L0_tok_in = {k: v for k, v in _L0_tok_all.items() if k in ('W0', 'b0', 'W1', 'b1', 'W2', 'b2', 'Wf', 'bf', 'idx0', 'idx1', 'idx2')}
    del _L0_tok_all

    def _L0_attn_setup():
        import jax, jax.numpy as jnp
        import numpy as np
        EPS = 1e-06
        BASE_LR = 1.0

        def gelu_tanh(x):
            return 0.5 * x * (1.0 + jnp.tanh(0.79788456 * x * (1.0 + 0.044715 * x * x)))

        def gelu_bwd(x):
            t = jnp.tanh(0.79788456 * x * (1.0 + 0.044715 * x * x))
            return 0.5 * x * ((1.0 - t * t) * (0.79788456 + 0.1070322243 * x * x)) + 0.5 * (1.0 + t)

        def layer_norm(x, gamma, beta):
            mu = jnp.mean(x, axis=-1, keepdims=True)
            var = jnp.var(x, axis=-1, keepdims=True)
            return gamma * (x - mu) / jnp.sqrt(var + EPS) + beta

        def ln_l2_bwd(x, target, gamma, beta):
            D = x.shape[-1]
            mu = jnp.mean(x, axis=-1, keepdims=True)
            std = jnp.sqrt(jnp.var(x, axis=-1, keepdims=True) + EPS)
            xh = (x - mu) / std
            gxh = (gamma * xh + beta - target) * gamma
            return (D * gxh - jnp.sum(gxh, -1, keepdims=True) - xh * jnp.sum(gxh * xh, -1, keepdims=True)) / (D * std)

        def _forward(hidden_states, Wq, Wk, Wv, Wo, Wg, lr_weight, lr_bias, learnable_token_idx, norm_weight, norm_bias, post_norm_weight, post_norm_bias, W1, b1, W2, b2):
            B, L, width = hidden_states.shape
            nh, hd = norm_weight.shape
            mb = learnable_token_idx.shape[0]
            nmb = L // mb

            def heads(x):
                return x.reshape(B, L, nh, hd).transpose(0, 2, 1, 3).reshape(B, nh, nmb, mb, hd)
            XQ = heads(hidden_states @ Wq)
            XK = heads(hidden_states @ Wk)
            XV = heads(hidden_states @ Wv)
            X = hidden_states.reshape(B, nmb, mb, width)
            lr = jax.nn.sigmoid(jnp.einsum('bnkc,hdc->bhnkd', X, lr_weight) + lr_bias.reshape(1, nh, 1, 1, 1))
            lr_eta = BASE_LR * jnp.transpose(lr, (0, 1, 2, 4, 3)) / hd
            token_idx = jnp.maximum(1.0 / jnp.arange(1, mb + 1, dtype=jnp.float32) + learnable_token_idx, 0.0)
            eta = token_idx.reshape(1, 1, 1, mb, 1) * lr_eta
            tril = jnp.tril(jnp.ones((mb, mb), hidden_states.dtype))
            lnw = norm_weight.reshape(nh, 1, hd)
            lnb = norm_bias.reshape(nh, 1, hd)

            def step(carry, xs):
                W1s, b1s, W2s, b2s = carry
                XQm, XKm, XVm, etam = xs
                X1 = XKm
                Z1 = X1 @ W1s + b1s
                X2 = gelu_tanh(Z1)
                Z2 = X2 @ W2s + b2s
                gZ2 = ln_l2_bwd(Z2, XVm - XKm, lnw, lnb)
                gZ1 = gZ2 @ jnp.swapaxes(W2s, -1, -2) * gelu_bwd(Z1)
                Attn1 = tril * (XQm @ jnp.swapaxes(X1, -1, -2))
                eta_tril = tril * etam
                b1_bar = b1s - eta_tril @ gZ1
                Z1_bar = XQm @ W1s - etam * Attn1 @ gZ1 + b1_bar
                X2_bar = gelu_tanh(Z1_bar)
                Attn2 = tril * (X2_bar @ jnp.swapaxes(X2, -1, -2))
                b2_bar = b2s - eta_tril @ gZ2
                Z2_bar = X2_bar @ W2s - etam * Attn2 @ gZ2 + b2_bar
                last_eta = etam[:, :, -1, :, None]
                W1_last = W1s - jnp.swapaxes(last_eta * X1, -1, -2) @ gZ1
                b1_last = b1s - jnp.sum(last_eta * gZ1, -2, keepdims=True)
                W2_last = W2s - jnp.swapaxes(last_eta * X2, -1, -2) @ gZ2
                b2_last = b2s - jnp.sum(last_eta * gZ2, -2, keepdims=True)
                out = XQm + layer_norm(Z2_bar, lnw, lnb)
                return ((W1_last, b1_last, W2_last, b2_last), out)
            carry = tuple((jnp.broadcast_to(p, (B,) + p.shape) for p in (W1, b1, W2, b2)))
            xs = tuple((jnp.moveaxis(t, 2, 0) for t in (XQ, XK, XV, eta)))
            _, outs = jax.lax.scan(step, carry, xs)
            out = outs.transpose(1, 0, 3, 2, 4).reshape(B, L, width)
            out = layer_norm(out, post_norm_weight, post_norm_bias)
            out = gelu_tanh(hidden_states @ Wg) * out
            return out @ Wo
        key = jax.random.key(seed)
        B, L, width, nh, mb = (8, 1024, 192, 12, 16)
        hd = width // nh
        ks = jax.random.split(key, 9)
        s = 0.02
        return dict(hidden_states=jax.random.normal(ks[0], (B, L, width), jnp.float32), Wq=jax.random.normal(ks[1], (width, width), jnp.float32) * s, Wk=jax.random.normal(ks[2], (width, width), jnp.float32) * s, Wv=jax.random.normal(ks[3], (width, width), jnp.float32) * s, Wo=jax.random.normal(ks[4], (width, width), jnp.float32) * s, Wg=jax.random.normal(ks[5], (width, width), jnp.float32) * s, lr_weight=jax.random.normal(ks[6], (nh, 1, width), jnp.float32) * s, lr_bias=jnp.zeros((nh, 1), jnp.float32), learnable_token_idx=jnp.zeros((mb,), jnp.float32), norm_weight=jnp.ones((nh, hd), jnp.float32), norm_bias=jnp.zeros((nh, hd), jnp.float32), post_norm_weight=jnp.ones((width,), jnp.float32), post_norm_bias=jnp.zeros((width,), jnp.float32), W1=jax.random.normal(ks[7], (nh, hd, 4 * hd), jnp.float32) * s, b1=jnp.zeros((nh, 1, 4 * hd), jnp.float32), W2=jax.random.normal(ks[8], (nh, 4 * hd, hd), jnp.float32) * s, b2=jnp.zeros((nh, 1, hd), jnp.float32))
    _L0_attn_all = _L0_attn_setup()
    _L0_attn_in = {k: v for k, v in _L0_attn_all.items() if k in ('Wq', 'Wk', 'Wv', 'Wo', 'Wg', 'lr_weight', 'lr_bias', 'learnable_token_idx', 'norm_weight', 'norm_bias', 'post_norm_weight', 'post_norm_bias', 'W1', 'b1', 'W2', 'b2')}
    del _L0_attn_all

    def _L0_ffn_setup():
        import jax, jax.numpy as jnp
        import numpy as np
        B, S, H, D, E = (4, 512, 192, 256, 8)
        TOP_K = 2
        EPS = 1e-08
        LN_EPS = 1e-05

        def _gelu(t):
            return jax.nn.gelu(t, approximate=False)

        def _layer_norm(t, gamma, beta):
            mu = jnp.mean(t, axis=-1, keepdims=True)
            var = jnp.mean(jnp.square(t - mu), axis=-1, keepdims=True)
            return (t - mu) * jax.lax.rsqrt(var + LN_EPS) * gamma + beta
        key = jax.random.key(seed)
        ks = jax.random.split(key, 8)
        x = jax.random.normal(ks[0], (B, S, H), dtype=jnp.float32)
        w1 = jax.random.normal(ks[1], (H, H // 2), dtype=jnp.float32) * 0.02
        b1 = jnp.zeros((H // 2,), dtype=jnp.float32)
        w2 = jax.random.normal(ks[2], (H // 2, E), dtype=jnp.float32) * 0.02
        b2 = jnp.zeros((E,), dtype=jnp.float32)
        a_dn = float(np.sqrt(6.0 / (H + D)))
        a_up = float(np.sqrt(6.0 / (D + H)))
        down_w = jax.random.uniform(ks[3], (E, H, D), dtype=jnp.float32, minval=-a_dn, maxval=a_dn)
        down_b = jnp.zeros((E, D), dtype=jnp.float32)
        up_w = jax.random.uniform(ks[4], (E, D, H), dtype=jnp.float32, minval=-a_up, maxval=a_up)
        gamma = jnp.ones((H,), dtype=jnp.float32)
        beta = jnp.zeros((H,), dtype=jnp.float32)
        return {'x': x, 'w1': w1, 'b1': b1, 'w2': w2, 'b2': b2, 'down_w': down_w, 'down_b': down_b, 'up_w': up_w, 'gamma': gamma, 'beta': beta}
    _L0_ffn_all = _L0_ffn_setup()
    _L0_ffn_in = {k: v for k, v in _L0_ffn_all.items() if k in ('w1', 'b1', 'w2', 'b2', 'down_w', 'down_b', 'up_w', 'gamma', 'beta')}
    del _L0_ffn_all
    return {'x': x, 'L0_tok_W0': _L0_tok_in['W0'], 'L0_tok_b0': _L0_tok_in['b0'], 'L0_tok_W1': _L0_tok_in['W1'], 'L0_tok_b1': _L0_tok_in['b1'], 'L0_tok_W2': _L0_tok_in['W2'], 'L0_tok_b2': _L0_tok_in['b2'], 'L0_tok_Wf': _L0_tok_in['Wf'], 'L0_tok_bf': _L0_tok_in['bf'], 'L0_tok_idx0': _L0_tok_in['idx0'], 'L0_tok_idx1': _L0_tok_in['idx1'], 'L0_tok_idx2': _L0_tok_in['idx2'], 'L0_attn_Wq': _L0_attn_in['Wq'], 'L0_attn_Wk': _L0_attn_in['Wk'], 'L0_attn_Wv': _L0_attn_in['Wv'], 'L0_attn_Wo': _L0_attn_in['Wo'], 'L0_attn_Wg': _L0_attn_in['Wg'], 'L0_attn_lr_weight': _L0_attn_in['lr_weight'], 'L0_attn_lr_bias': _L0_attn_in['lr_bias'], 'L0_attn_learnable_token_idx': _L0_attn_in['learnable_token_idx'], 'L0_attn_norm_weight': _L0_attn_in['norm_weight'], 'L0_attn_norm_bias': _L0_attn_in['norm_bias'], 'L0_attn_post_norm_weight': _L0_attn_in['post_norm_weight'], 'L0_attn_post_norm_bias': _L0_attn_in['post_norm_bias'], 'L0_attn_W1': _L0_attn_in['W1'], 'L0_attn_b1': _L0_attn_in['b1'], 'L0_attn_W2': _L0_attn_in['W2'], 'L0_attn_b2': _L0_attn_in['b2'], 'L0_ffn_w1': _L0_ffn_in['w1'], 'L0_ffn_b1': _L0_ffn_in['b1'], 'L0_ffn_w2': _L0_ffn_in['w2'], 'L0_ffn_b2': _L0_ffn_in['b2'], 'L0_ffn_down_w': _L0_ffn_in['down_w'], 'L0_ffn_down_b': _L0_ffn_in['down_b'], 'L0_ffn_up_w': _L0_ffn_in['up_w'], 'L0_ffn_gamma': _L0_ffn_in['gamma'], 'L0_ffn_beta': _L0_ffn_in['beta']}

def reference(x, L0_tok_W0, L0_tok_b0, L0_tok_W1, L0_tok_b1, L0_tok_W2, L0_tok_b2, L0_tok_Wf, L0_tok_bf, L0_tok_idx0, L0_tok_idx1, L0_tok_idx2, L0_attn_Wq, L0_attn_Wk, L0_attn_Wv, L0_attn_Wo, L0_attn_Wg, L0_attn_lr_weight, L0_attn_lr_bias, L0_attn_learnable_token_idx, L0_attn_norm_weight, L0_attn_norm_bias, L0_attn_post_norm_weight, L0_attn_post_norm_bias, L0_attn_W1, L0_attn_b1, L0_attn_W2, L0_attn_b2, L0_ffn_w1, L0_ffn_b1, L0_ffn_w2, L0_ffn_b2, L0_ffn_down_w, L0_ffn_down_b, L0_ffn_up_w, L0_ffn_gamma, L0_ffn_beta):
    import jax
    import jax.numpy as jnp

    def _L0_tok_ref(x, W0, b0, W1, b1, W2, b2, Wf, bf, idx0, idx1, idx2):
        import jax, jax.numpy as jnp
        import numpy as np
        B = 16
        IMG = 64
        CH = 3
        EMBED = 64
        GP = 16
        PRE = [1, 2, 4]
        N_LEVELS = 3
        FUSED = EMBED * N_LEVELS

        def hilbert_flat_indices(n):
            t = np.arange(n * n, dtype=np.int64)
            x = np.zeros(n * n, dtype=np.int64)
            y = np.zeros(n * n, dtype=np.int64)
            s = 1
            while s < n:
                rx = 1 & t // 2
                ry = 1 & (t ^ rx)
                swap = ry == 0
                flip = swap & (rx == 1)
                x = np.where(flip, s - 1 - x, x)
                y = np.where(flip, s - 1 - y, y)
                x2 = np.where(swap, y, x)
                y2 = np.where(swap, x, y)
                x, y = (x2, y2)
                x = x + s * rx
                y = y + s * ry
                t = t // 4
                s *= 2
            return y * n + x

        def _level(x, idx, W, b, p, gp):
            Bsz, C, H, _ = x.shape
            h = H // p
            t = x.reshape(Bsz, C, h, p, h, p).transpose(0, 2, 4, 3, 5, 1).reshape(Bsz, h * h, p * p * C)
            t = t[:, idx]
            t = t.reshape(Bsz, h * h // gp, gp * p * p * C)
            return t @ W.T + b

        def _interp_linear(x, n_out):
            L = x.shape[1]
            pos = (jnp.arange(n_out, dtype=jnp.float32) + 0.5) * (L / n_out) - 0.5
            pos = jnp.clip(pos, 0.0, L - 1)
            i0 = jnp.floor(pos).astype(jnp.int32)
            i1 = jnp.minimum(i0 + 1, L - 1)
            w = (pos - i0).astype(x.dtype)
            return x[:, i0] * (1.0 - w)[None, :, None] + x[:, i1] * w[None, :, None]
        Ws = [(idx0, W0, b0, PRE[0]), (idx1, W1, b1, PRE[1]), (idx2, W2, b2, PRE[2])]
        outs = [_level(x, idx, W, b, p, GP) for idx, W, b, p in Ws]
        n_tokens = outs[0].shape[1]
        outs = [outs[0]] + [_interp_linear(o, n_tokens) for o in outs[1:]]
        y = jnp.concatenate(outs, axis=-1)
        return y @ Wf.T + bf

    def _L0_attn_ref(hidden_states, Wq, Wk, Wv, Wo, Wg, lr_weight, lr_bias, learnable_token_idx, norm_weight, norm_bias, post_norm_weight, post_norm_bias, W1, b1, W2, b2):
        import jax, jax.numpy as jnp
        import numpy as np
        EPS = 1e-06
        BASE_LR = 1.0

        def gelu_tanh(x):
            return 0.5 * x * (1.0 + jnp.tanh(0.79788456 * x * (1.0 + 0.044715 * x * x)))

        def gelu_bwd(x):
            t = jnp.tanh(0.79788456 * x * (1.0 + 0.044715 * x * x))
            return 0.5 * x * ((1.0 - t * t) * (0.79788456 + 0.1070322243 * x * x)) + 0.5 * (1.0 + t)

        def layer_norm(x, gamma, beta):
            mu = jnp.mean(x, axis=-1, keepdims=True)
            var = jnp.var(x, axis=-1, keepdims=True)
            return gamma * (x - mu) / jnp.sqrt(var + EPS) + beta

        def ln_l2_bwd(x, target, gamma, beta):
            D = x.shape[-1]
            mu = jnp.mean(x, axis=-1, keepdims=True)
            std = jnp.sqrt(jnp.var(x, axis=-1, keepdims=True) + EPS)
            xh = (x - mu) / std
            gxh = (gamma * xh + beta - target) * gamma
            return (D * gxh - jnp.sum(gxh, -1, keepdims=True) - xh * jnp.sum(gxh * xh, -1, keepdims=True)) / (D * std)

        def _forward(hidden_states, Wq, Wk, Wv, Wo, Wg, lr_weight, lr_bias, learnable_token_idx, norm_weight, norm_bias, post_norm_weight, post_norm_bias, W1, b1, W2, b2):
            B, L, width = hidden_states.shape
            nh, hd = norm_weight.shape
            mb = learnable_token_idx.shape[0]
            nmb = L // mb

            def heads(x):
                return x.reshape(B, L, nh, hd).transpose(0, 2, 1, 3).reshape(B, nh, nmb, mb, hd)
            XQ = heads(hidden_states @ Wq)
            XK = heads(hidden_states @ Wk)
            XV = heads(hidden_states @ Wv)
            X = hidden_states.reshape(B, nmb, mb, width)
            lr = jax.nn.sigmoid(jnp.einsum('bnkc,hdc->bhnkd', X, lr_weight) + lr_bias.reshape(1, nh, 1, 1, 1))
            lr_eta = BASE_LR * jnp.transpose(lr, (0, 1, 2, 4, 3)) / hd
            token_idx = jnp.maximum(1.0 / jnp.arange(1, mb + 1, dtype=jnp.float32) + learnable_token_idx, 0.0)
            eta = token_idx.reshape(1, 1, 1, mb, 1) * lr_eta
            tril = jnp.tril(jnp.ones((mb, mb), hidden_states.dtype))
            lnw = norm_weight.reshape(nh, 1, hd)
            lnb = norm_bias.reshape(nh, 1, hd)

            def step(carry, xs):
                W1s, b1s, W2s, b2s = carry
                XQm, XKm, XVm, etam = xs
                X1 = XKm
                Z1 = X1 @ W1s + b1s
                X2 = gelu_tanh(Z1)
                Z2 = X2 @ W2s + b2s
                gZ2 = ln_l2_bwd(Z2, XVm - XKm, lnw, lnb)
                gZ1 = gZ2 @ jnp.swapaxes(W2s, -1, -2) * gelu_bwd(Z1)
                Attn1 = tril * (XQm @ jnp.swapaxes(X1, -1, -2))
                eta_tril = tril * etam
                b1_bar = b1s - eta_tril @ gZ1
                Z1_bar = XQm @ W1s - etam * Attn1 @ gZ1 + b1_bar
                X2_bar = gelu_tanh(Z1_bar)
                Attn2 = tril * (X2_bar @ jnp.swapaxes(X2, -1, -2))
                b2_bar = b2s - eta_tril @ gZ2
                Z2_bar = X2_bar @ W2s - etam * Attn2 @ gZ2 + b2_bar
                last_eta = etam[:, :, -1, :, None]
                W1_last = W1s - jnp.swapaxes(last_eta * X1, -1, -2) @ gZ1
                b1_last = b1s - jnp.sum(last_eta * gZ1, -2, keepdims=True)
                W2_last = W2s - jnp.swapaxes(last_eta * X2, -1, -2) @ gZ2
                b2_last = b2s - jnp.sum(last_eta * gZ2, -2, keepdims=True)
                out = XQm + layer_norm(Z2_bar, lnw, lnb)
                return ((W1_last, b1_last, W2_last, b2_last), out)
            carry = tuple((jnp.broadcast_to(p, (B,) + p.shape) for p in (W1, b1, W2, b2)))
            xs = tuple((jnp.moveaxis(t, 2, 0) for t in (XQ, XK, XV, eta)))
            _, outs = jax.lax.scan(step, carry, xs)
            out = outs.transpose(1, 0, 3, 2, 4).reshape(B, L, width)
            out = layer_norm(out, post_norm_weight, post_norm_bias)
            out = gelu_tanh(hidden_states @ Wg) * out
            return out @ Wo
        return _forward(hidden_states, Wq, Wk, Wv, Wo, Wg, lr_weight, lr_bias, learnable_token_idx, norm_weight, norm_bias, post_norm_weight, post_norm_bias, W1, b1, W2, b2)

    def _L0_ffn_ref(x, w1, b1, w2, b2, down_w, down_b, up_w, gamma, beta):
        import jax, jax.numpy as jnp
        import numpy as np
        B, S, H, D, E = (4, 512, 192, 256, 8)
        TOP_K = 2
        EPS = 1e-08
        LN_EPS = 1e-05

        def _gelu(t):
            return jax.nn.gelu(t, approximate=False)

        def _layer_norm(t, gamma, beta):
            mu = jnp.mean(t, axis=-1, keepdims=True)
            var = jnp.mean(jnp.square(t - mu), axis=-1, keepdims=True)
            return (t - mu) * jax.lax.rsqrt(var + LN_EPS) * gamma + beta
        logits = _gelu(x @ w1 + b1) @ w2 + b2
        routing = jax.nn.softmax(logits, axis=-1)
        topv, topi = jax.lax.top_k(routing, TOP_K)
        sparse = jnp.sum(jax.nn.one_hot(topi, E, dtype=routing.dtype) * topv[..., None], axis=-2)
        sparse = sparse / (jnp.sum(sparse, axis=-1, keepdims=True) + EPS)
        z = _gelu(jnp.einsum('bsh,ehd->bsed', x, down_w) + down_b)
        expert_out = jnp.einsum('bsed,edh->bseh', z, up_w)
        moe_out = jnp.einsum('bseh,bse->bsh', expert_out, sparse)
        return _layer_norm(x + moe_out, gamma, beta)
    h = _L0_tok_ref(x, L0_tok_W0, L0_tok_b0, L0_tok_W1, L0_tok_b1, L0_tok_W2, L0_tok_b2, L0_tok_Wf, L0_tok_bf, L0_tok_idx0, L0_tok_idx1, L0_tok_idx2)
    h = _layernorm(h + _L0_attn_ref(h, L0_attn_Wq, L0_attn_Wk, L0_attn_Wv, L0_attn_Wo, L0_attn_Wg, L0_attn_lr_weight, L0_attn_lr_bias, L0_attn_learnable_token_idx, L0_attn_norm_weight, L0_attn_norm_bias, L0_attn_post_norm_weight, L0_attn_post_norm_bias, L0_attn_W1, L0_attn_b1, L0_attn_W2, L0_attn_b2), axis=-1)
    h = _layernorm(h + _L0_ffn_ref(h, L0_ffn_w1, L0_ffn_b1, L0_ffn_w2, L0_ffn_b2, L0_ffn_down_w, L0_ffn_down_b, L0_ffn_up_w, L0_ffn_gamma, L0_ffn_beta), axis=-1)
    return h

_drawn_inputs = setup_inputs


def setup_inputs(seed=0):
    import zlib

    import numpy as np

    out = dict(_drawn_inputs(seed))
    spreads = {'L0_attn_lr_bias': (0.0, 2.0),
     'L0_attn_learnable_token_idx': (0.0, 0.382),
     'L0_attn_norm_weight': (1.0, 0.582),
     'L0_attn_norm_bias': (0.0, 0.472),
     'L0_attn_post_norm_weight': (1.0, 0.6),
     'L0_attn_post_norm_bias': (0.0, 0.633),
     'L0_attn_b1': (0.0, 0.784),
     'L0_attn_b2': (0.0, 0.569),
     'L0_ffn_b1': (0.0, 0.1),
     'L0_ffn_b2': (0.0, 0.1),
     'L0_ffn_down_b': (0.0, 0.349),
     'L0_ffn_gamma': (1.0, 0.2),
     'L0_ffn_beta': (0.0, 0.1)}
    factors = {'L0_tok_b0': 2.758,
     'L0_tok_b1': 3.333,
     'L0_tok_b2': 2.803,
     'L0_attn_Wq': 2.994,
     'L0_attn_lr_weight': 33.294,
     'L0_attn_W1': 8.0,
     'L0_attn_W2': 6.6,
     'L0_attn_Wk': 4.33,
     'L0_attn_Wv': 4.172}
    for name, (base, spread) in spreads.items():
        noise = np.random.default_rng([zlib.crc32(name.encode()), seed]).standard_normal(out[name].shape)
        drawn = base * np.exp(spread * noise) if base else spread * noise
        out[name] = jnp.asarray(drawn.astype(out[name].dtype))
    for name, factor in factors.items():
        out[name] = (out[name] * factor).astype(out[name].dtype)
    return out
```

```python
import numpy as np
import concourse.bass as bass
from concourse import mybir
from contextlib import ExitStack

F32 = mybir.dt.float32
U32 = mybir.dt.uint32
ALU = mybir.AluOpType
ACT = mybir.ActivationFunctionType
AX = mybir.AxisListType.X

P = 128
B, T, W = 16, 256, 192
NH, D, F = 12, 16, 64
MB = 16
NS = T // MB
BH = P // MB
NU = NS * B // BH
WB = W - P
GP, CH, EMB = 16, 3, 64
SIDES = (64, 32, 16)
DIN = tuple(CH * (64 // s) ** 2 for s in SIDES)
GROUPS = tuple(s * s // GP for s in SIDES)
E, DE = 8, 256
EC = E * DE // P
BANK = 512
NBANK = 8
EPS_INNER, EPS_LN, EPS_GATE = 1e-6, 1e-5, 1e-8
GELU_C, GELU_A, GELU_D = 0.79788456, 0.044715, 0.1070322243


def bcast(ap, axis, n):
    ap = ap.unsqueeze(axis)
    shape = list(ap.shape)
    shape[axis] = n
    return ap.broadcast_to(shape)


def rsqrt_steps(tag):
    return [f"{tag}eps", f"{tag}half", f"{tag}seed"] + [f"{tag}newton{k}" for k in range(9)]


def rsqrt(nc, step, own, y, a, x, var, eps, tag):
    V = nc.vector
    I32 = mybir.dt.int32
    names = rsqrt_steps(tag)
    step(V.tensor_scalar(x, var, eps, None, ALU.add))
    own(names[0])
    step(V.tensor_scalar(y.bitcast(I32), x.bitcast(I32), 1, None, ALU.logical_shift_right))
    own(names[1])
    step(V.tensor_scalar(y.bitcast(I32), y.bitcast(I32), -1.0, float(0x5F3759DF), ALU.mult, ALU.add))
    own(names[2])
    for k in range(3):
        step(V.tensor_tensor(a, y, y, ALU.mult))
        own(names[3 + 3 * k])
        step(V.scalar_tensor_tensor(a, a, -0.5, x, ALU.mult, ALU.mult))
        own(names[4 + 3 * k])
        step(V.scalar_tensor_tensor(y, a, 1.5, y, ALU.add, ALU.mult))
        own(names[5 + 3 * k])


def previous_jobs(readers):
    n = len(readers)
    out = []
    for k, r in enumerate(readers):
        j = k - NBANK
        while readers[j % n] is None:
            j -= NBANK
        out.append((j // n, j % n))
    return out


def tokenizer(nc, A, hT, LR, ident):
    NCOL = B * T
    T1, T2 = GROUPS[1], GROUPS[2]
    jobs = ["act"] * 4 + ["act"] * 4 + ["dve"] * 2 + ["dve"] + ["act"] * 8 + ["act"] * 8
    J_T1, J_T2, J_Y1, J_Y2, J_T0, J_Y0 = 0, 4, 8, 10, 11, 19
    J_H = len(jobs)
    for _ in range(NS // 2):
        jobs += ["act", "dve", "act"]
    J_LR = len(jobs)
    jobs += ["dve"]
    emptied_by = []
    n = {"act": 0, "dve": 0}
    for r in jobs:
        n[r] += 1
        emptied_by.append(n[r])

    with ExitStack() as ctx:
        sb = lambda name, shape, dt=F32: ctx.enter_context(nc.sbuf_tensor(name, shape, dt))
        sem = lambda name: ctx.enter_context(nc.semaphore(name))
        idx0 = sb("idx0_sb", [P, 2 * GP], U32)
        idx1 = sb("idx1_sb", [T1, GP], U32)
        idx2 = sb("idx2_sb", [T2, GP], U32)
        G0 = sb("G0", [P, 2 * GP * B * DIN[0]])
        G1 = sb("G1", [T1, GP * B * DIN[1]])
        G2 = sb("G2", [T2, GP * B * DIN[2]])
        K0, K1, K2 = GP * DIN[0], GP * DIN[1] // 2, 2 * DIN[2]
        X0T = sb("X0T", [K0, NCOL])
        X1T = sb("X1T", [K1, 2, B * T1])
        X2T = sb("X2T", [K2, GP // 2, B * T2])
        W0 = sb("W0_sb", [K0, EMB])
        W1 = sb("W1_sb", [K1, 2, EMB])
        W2 = sb("W2_sb", [K2, GP // 2, EMB])
        bias01 = sb("bias01", [P, 1])
        bias2 = sb("bias2", [EMB, 1])
        WfA = sb("WfA", [P, W])
        WfB = sb("WfB", [WB + 1, W])
        lrA = sb("lrA", [P, NH])
        lrB = sb("lrB", [WB + 1, NH])
        Y1 = sb("Y1", [P, B, T1 + 2])
        D1 = sb("D1", [P, B, T1 + 1])
        Y2 = sb("Y2", [EMB, B, T2 + 2])
        D2 = sb("D2", [EMB, B, T2 + 1])
        YA = sb("YA", [P, NCOL])
        YB = sb("YB", [WB + 1, NCOL])
        HA = sb("HA", [P, 2, BANK])
        HB = sb("HB", [WB + 1, 2, BANK])
        LE = sb("LE", [NH, NCOL])
        bank = [ctx.enter_context(nc.psum_tensor(f"tok_bank{i}", [P, BANK], F32)) for i in range(NBANK)]

        idx_loaded, weights_loaded = sem("tok_idx_loaded"), sem("tok_weights_loaded")
        gathered = [sem(f"gathered{i}") for i in range(3)]
        filled, act_emptied, dve_emptied = sem("tok_filled"), sem("tok_act_emptied"), sem("tok_dve_emptied")
        padded, levels_done, ones_set = sem("tok_padded"), sem("tok_levels_done"), sem("tok_ones_set")
        h_stored, lr_steps = [sem("h_stored0"), sem("h_stored1")], sem("lr_steps")
        emptied = {"act": act_emptied, "dve": dve_emptied}
        NLOAD = 16

        with nc.Block() as block:
            @block.sync
            def _(sp):
                sp.dma_start(idx1[:], A["idx1"].bitcast(U32)).then_inc(idx_loaded, 16)
                sp.dma_start(idx2[:], A["idx2"].bitcast(U32)).then_inc(idx_loaded, 16)
                sp.dma_start(idx0[:].rearrange("p (t g) -> p t g", t=2),
                             A["idx0"].bitcast(U32).rearrange("(t p) g -> p t g", t=2)).then_inc(idx_loaded, 16)
                loads = [
                    (ident[:], A["ident"]),
                    (W1[:], A["W1T"].rearrange("(j k) e -> k j e", j=2)),
                    (W2[:], A["W2T"].rearrange("(j k) e -> k j e", k=K2)),
                    (W0[:], A["W0T"]),
                    (bias01[0:EMB, :], A["b0"]), (bias01[EMB:P, :], A["b1"]), (bias2[:], A["b2"]),
                    (WfA[:], A["WfT"][0:P, :]), (WfB[0:WB, :], A["WfT"][P:W, :]), (WfB[WB:WB + 1, :], A["bf"]),
                    (lrA[:], A["lrT"][0:P, :]), (lrB[0:WB, :], A["lrT"][P:W, :]), (lrB[WB:WB + 1, :], A["lrb"]),
                ]
                for dst, src in loads:
                    sp.dma_start(dst, src).then_inc(weights_loaded, 16)
                for i in range(NS // 2):
                    sp.wait_ge(act_emptied, emptied_by[J_H + 3 * i])
                    sp.dma_start(hT[4 * i:4 * i + 4, 0:P, :].rearrange("u f k -> f u k"),
                                 HA[:, i % 2, :].rearrange("p (u k) -> p u k", u=4)).then_inc(h_stored[i % 2], 16)
                    sp.wait_ge(dve_emptied, emptied_by[J_H + 3 * i + 1])
                    sp.dma_start(hT[4 * i:4 * i + 4, P:W, :].rearrange("u f k -> f u k"),
                                 HB[0:WB, i % 2, :].rearrange("p (u k) -> p u k", u=4)).then_inc(h_stored[i % 2], 16)
                for u in range(SPARE):
                    sp.dma_start(hT[NU + u, 0:P, :], HA[:, 1, u * P:(u + 1) * P]).then_inc(h_stored[u % 2], 16)
                    sp.dma_start(hT[NU + u, P:W, :], HB[0:WB, 1, u * P:(u + 1) * P]).then_inc(h_stored[u % 2], 16)
                for k in range(2):
                    sp.wait_ge(h_stored[k], 16 * (NS // 2) + 32 * len(range(k, SPARE, 2)))

            @block.gpsimd
            def _(pool):
                nc.gpsimd.memset(YB[WB:WB + 1, :], 1.0).then_inc(ones_set, 1)
                nc.gpsimd.memset(HB[WB:WB + 1, :, :], 1.0).then_inc(ones_set, 1)
                pool.wait_ge(idx_loaded, 48)
                for g in range(GP):
                    n1, n2 = B * DIN[1], B * DIN[2]
                    nc.gpsimd.indirect_dma_start(
                        G1[:, g * n1:(g + 1) * n1], None, A["x1"],
                        bass.IndirectOffsetOnAxis(idx1[:, g:g + 1], 0)).then_inc(gathered[1], 16)
                    nc.gpsimd.indirect_dma_start(
                        G2[:, g * n2:(g + 1) * n2], None, A["x2"],
                        bass.IndirectOffsetOnAxis(idx2[:, g:g + 1], 0)).then_inc(gathered[2], 16)
                for j in range(2 * GP):
                    n0 = B * DIN[0]
                    nc.gpsimd.indirect_dma_start(
                        G0[:, j * n0:(j + 1) * n0], None, A["x0"],
                        bass.IndirectOffsetOnAxis(idx0[:, j:j + 1], 0)).then_inc(gathered[0], 16)

            @block.tensor
            def _(pe):
                def bank_free(k):
                    if k >= NBANK:
                        pe.wait_ge(emptied[jobs[k - NBANK]], emptied_by[k - NBANK])
                    return bank[k % NBANK]

                pe.wait_ge(weights_loaded, 16 * 13)
                pe.wait_ge(gathered[1], 16 * GP)
                v1 = G1[:].rearrange("t (j n b) -> t j b n", j=2, b=B)
                for k in range(4):
                    pb = bank_free(J_T1 + k)
                    for m in range(8):
                        q = nc.tensor.transpose(pb[0:K1, m * T1:(m + 1) * T1], v1[:, k // 2, 8 * (k % 2) + m],
                                                ident[0:T1, 0:T1])
                    q.then_inc(filled, 1)
                pe.wait_ge(gathered[2], 16 * GP)
                v2 = G2[:].rearrange("t (j n b) -> t j b n", j=GP // 2, b=B)
                for k in range(4):
                    pb = bank_free(J_T2 + k)
                    for m in range(2 * B):
                        q = nc.tensor.transpose(pb[0:K2, m * T2:(m + 1) * T2], v2[:, 2 * k + m // B, m % B],
                                                ident[0:T2, 0:T2])
                    q.then_inc(filled, 1)
                pe.wait_ge(act_emptied, emptied_by[J_T1 + 3])
                for k in range(2):
                    pb = bank_free(J_Y1 + k)
                    for j in range(2):
                        q = nc.tensor.matmul(pb[EMB:P, :], W1[:, j, :], X1T[:, j, k * BANK:(k + 1) * BANK],
                                             start=(j == 0), stop=(j == 1))
                    q.then_inc(filled, 1)
                pe.wait_ge(act_emptied, emptied_by[J_T2 + 3])
                pb = bank_free(J_Y2)
                for j in range(GP // 2):
                    q = nc.tensor.matmul(pb[0:EMB, 0:B * T2], W2[:, j, :], X2T[:, j, :],
                                         start=(j == 0), stop=(j == GP // 2 - 1))
                q.then_inc(filled, 1)
                pe.wait_ge(gathered[0], 16 * 2 * GP)
                v0 = G0[:].rearrange("t (j n b) -> t j b n", j=2, b=B)
                for k in range(8):
                    pb = bank_free(J_T0 + k)
                    for m in range(4):
                        q = nc.tensor.transpose(pb[0:K0, m * P:(m + 1) * P], v0[:, k % 2, 4 * (k // 2) + m], ident[:])
                    q.then_inc(filled, 1)
                for k in range(8):
                    pb = bank_free(J_Y0 + k)
                    pe.wait_ge(act_emptied, emptied_by[J_T0 + (k // 2) * 2 + 1])
                    nc.tensor.matmul(pb[0:EMB, :], W0[:], X0T[:, k * BANK:(k + 1) * BANK],
                                     start=True, stop=True).then_inc(filled, 1)
                pe.wait_ge(act_emptied, emptied_by[J_Y0 + 7])
                pe.wait_ge(levels_done, 2)
                pe.wait_ge(ones_set, 2)
                yA = YA[:].rearrange("p (b s k) -> p s b k", b=B, s=NS)
                yB = YB[:].rearrange("p (b s k) -> p s b k", b=B, s=NS)

                def rates(i):
                    pb = bank_free(J_H + 3 * i + 2)
                    pe.wait_ge(act_emptied, emptied_by[J_H + 3 * i])
                    pe.wait_ge(dve_emptied, emptied_by[J_H + 3 * i + 1])
                    nc.tensor.matmul(pb[0:NH, :], lrA[:], HA[:, i % 2, :], start=True, stop=False)
                    nc.tensor.matmul(pb[0:NH, :], lrB[:], HB[:, i % 2, :], start=False, stop=True).then_inc(filled, 1)

                for i in range(NS // 2):
                    for half, (m0, m1) in enumerate(((0, P), (P, W))):
                        pb = bank_free(J_H + 3 * i + half)
                        nc.tensor.matmul(pb[0:m1 - m0, :], WfA[:, m0:m1], yA[:, 2 * i:2 * i + 2], start=True, stop=False)
                        nc.tensor.matmul(pb[0:m1 - m0, :], WfB[:, m0:m1], yB[:, 2 * i:2 * i + 2],
                                         start=False, stop=True).then_inc(filled, 1)
                    rates(i)
                pb = bank_free(J_LR)
                pe.wait_ge(act_emptied, emptied_by[J_LR - 1])
                for u in range(NU):
                    q = nc.tensor.transpose(pb[:, u * NH:(u + 1) * NH], LE[:, u * P:(u + 1) * P], ident[0:NH, 0:NH])
                q.then_inc(filled, 1)

            @block.scalar
            def _(act):
                def job(k, out, in_, func=ACT.Copy, **kw):
                    act.wait_ge(filled, k + 1)
                    nc.scalar.activation(out, in_, func, **kw).then_inc(act_emptied, 1)

                for k in range(4):
                    job(J_T1 + k, X1T[:, k // 2, (k % 2) * BANK:(k % 2 + 1) * BANK], bank[(J_T1 + k) % NBANK][0:K1, :])
                for k in range(4):
                    job(J_T2 + k, X2T[:, 2 * k:2 * k + 2, :].rearrange("p j n -> p (j n)"),
                        bank[(J_T2 + k) % NBANK][0:K2, :])
                x0 = X0T[:].rearrange("p (b t n) -> p b t n", b=B, t=2)
                for k in range(8):
                    job(J_T0 + k, x0[:, 4 * (k // 2):4 * (k // 2) + 4, k % 2, :],
                        bank[(J_T0 + k) % NBANK][0:K0, :].rearrange("p (b n) -> p b n", b=4))
                act.wait_ge(weights_loaded, 16 * 13)
                for k in range(8):
                    job(J_Y0 + k, YA[0:EMB, k * BANK:(k + 1) * BANK], bank[(J_Y0 + k) % NBANK][0:EMB, :],
                        ACT.Identity, bias=bias01[0:EMB, 0:1])
                for i in range(NS // 2):
                    if i >= 2:
                        act.wait_ge(h_stored[i % 2], 32 * (i // 2))
                    k = J_H + 3 * i
                    job(k, HA[:, i % 2, :], bank[k % NBANK][:, :])
                    job(k + 2, LE[:, i * BANK:(i + 1) * BANK], bank[(k + 2) % NBANK][0:NH, :], ACT.Exp, scale=-1.0)

            @block.vector
            def _(dve):
                dve.wait_ge(weights_loaded, 16 * 13)
                for k in range(2):
                    dve.wait_ge(filled, J_Y1 + k + 1)
                    nc.vector.tensor_scalar(Y1[EMB:P, 8 * k:8 * k + 8, 1:T1 + 1],
                                            bank[(J_Y1 + k) % NBANK][EMB:P, :].rearrange("p (b t) -> p b t", b=8),
                                            bias01[EMB:P, 0:1], None, ALU.add).then_inc(dve_emptied, 1)
                dve.wait_ge(filled, J_Y2 + 1)
                nc.vector.tensor_scalar(Y2[:, :, 1:T2 + 1],
                                        bank[J_Y2 % NBANK][0:EMB, 0:B * T2].rearrange("p (b t) -> p b t", b=B),
                                        bias2[:, 0:1], None, ALU.add).then_inc(dve_emptied, 1)
                for Y, rows, t in ((Y1, slice(EMB, P), T1), (Y2, slice(0, EMB), T2)):
                    if t == T1:
                        dve.wait_ge(dve_emptied, 3)
                    nc.vector.tensor_copy(Y[rows, :, 0:1], Y[rows, :, 1:2]).then_inc(padded, 1)
                    nc.vector.tensor_copy(Y[rows, :, t + 1:t + 2], Y[rows, :, t:t + 1]).then_inc(padded, 1)
                dve.wait_ge(padded, 4)
                nc.vector.tensor_tensor(D1[EMB:P], Y1[EMB:P, :, 1:T1 + 2], Y1[EMB:P, :, 0:T1 + 1],
                                        ALU.subtract).then_inc(padded, 1)
                nc.vector.tensor_tensor(D2[:], Y2[:, :, 1:T2 + 2], Y2[:, :, 0:T2 + 1], ALU.subtract).then_inc(padded, 1)
                dve.wait_ge(padded, 6)
                for Y, Df, rows, t, out in ((Y1, D1, slice(EMB, P), T1, YA), (Y2, D2, slice(0, EMB), T2, YB)):
                    R = T // t
                    o = out[rows, :].rearrange("p (b k r) -> p b k r", b=B, r=R)
                    for r in range(R):
                        w = (r + 0.5) / R - 0.5
                        first = 0 if w < 0 else 1
                        w = w + 1.0 if w < 0 else w
                        q = nc.vector.scalar_tensor_tensor(o[:, :, :, r], Df[rows, :, first:first + t], w,
                                                           Y[rows, :, first:first + t], ALU.mult, ALU.add)
                    q.then_inc(levels_done, 1)
                for i in range(NS // 2):
                    k = J_H + 3 * i + 1
                    if i >= 2:
                        dve.wait_ge(h_stored[i % 2], 32 * (i // 2))
                    dve.wait_ge(filled, k + 1)
                    nc.vector.tensor_copy(HB[0:WB, i % 2, :], bank[k % NBANK][0:WB, :]).then_inc(dve_emptied, 1)
                dve.wait_ge(filled, J_LR + 1)
                nc.vector.tensor_scalar(LR[:], bank[J_LR % NBANK][:, 0:NU * NH], float(D), float(D),
                                        ALU.mult, ALU.add).then_inc(lr_steps, 1)
                dve.wait_ge(lr_steps, 1)
                nc.vector.reciprocal(LR[:], LR[:]).then_inc(lr_steps, 1)
                dve.wait_ge(lr_steps, 2)


SPARE = 3
JOBS = [("xT", 2, "act"), ("xbT", 2, "act"), ("attn", 4, "dve"), ("z2", 4, "dve"), ("z2b", 4, "act"), ("w2", 2, "dve"),
        ("kqT", 6, "act"), ("w2T", 2, "act"), ("m1", 3, "dve"), ("gT", 3, "act"), ("gx", 2, "dve"), ("z1", 2, "dve"),
        ("proj", 2, "act"), ("z1b", 2, "dve"), ("w1", 2, "dve"), ("b1", 2, "dve")]
SLOTS = [f"{n}{i}" for n, k, _ in JOBS for i in range(k)]
READER = {f"{n}{i}": r for n, k, r in JOBS for i in range(k)}
NJ = len(SLOTS)
PADDED = SLOTS + [None] * (-NJ % 4)
NP = len(PADDED)
SLOT_OF = {s: i for i, s in enumerate(PADDED) if s}
PREV = previous_jobs([READER[s] if s else None for s in PADDED])
ACT_STEPS = (["xT0", "xT1", "xbT0", "xbT1", "z2b0", "z2b1", "z2b2", "z2b3"] + [f"kqT{i}" for i in range(6)]
             + ["w2T0", "w2T1", "gT0", "gT1", "gT2", "sq", "proj0", "proj1", "tanh", "gelu_b"])
DVE_STEPS = (["da", "db", "dc", "attn0", "attn1", "dgelu", "attn2", "attn3"]
             + ["z20", "z21", "z22", "z23", "z2_fold", "z2_bias", "mean", "center", "square", "var"] + rsqrt_steps("r_")
             + ["xhat", "gxh0", "gxh", "s1", "gx_xh", "s2", "lr_rstd", "w20", "w21", "b2", "s2_xh", "sub1", "sub2", "g2"]
             + ["m10", "m11", "m12", "gx0", "gx1", "z10", "z11", "cube", "arg"]
             + ["z1b0", "z1b1", "x2", "w10", "w11", "b10", "b11"])
POOL_STEPS = ["k_bd", "q_bd", "t0", "t1", "t2", "b2_copy", "g2_bd", "zb_mask", "zb_half", "zb_quarter", "zb_fold", "out"]
DVE_OF = {"w21": "b2"}


def count_of(engine, job):
    if engine == "act":
        return ACT_STEPS.index(job) + 1
    return DVE_STEPS.index(DVE_OF.get(job, job)) + 1


def scan(nc, A, hT, attn, q_dram, LR, ident):
    with ExitStack() as ctx:
        sb = lambda name, shape: ctx.enter_context(nc.sbuf_tensor(name, shape, F32))
        two = lambda name, shape: [sb(f"{name}_{i}", shape) for i in range(2)]
        sem = lambda name: ctx.enter_context(nc.semaphore(name))
        HD, HF, HP = NH * D, NH * F, NH * P
        block_mask = sb("block_mask", [P, P])
        neg_tril = sb("neg_tril", [P, P])
        neg_last = sb("neg_last", [P, P])
        tok = sb("tok", [P, MB])
        half_last = sb("half_last", [P, 2])
        recip = sb("recip", [P, MB])
        lnw, lnb, lnw2 = sb("lnw", [P, HD]), sb("lnb", [P, HD]), sb("lnw2", [P, HD])
        WqkvA, WqkvB = sb("WqkvA", [P, 3 * W]), sb("WqkvB", [WB, 3 * W])
        w2_small = sb("w2_small", [P, NH // 2, D])
        W1s = two("W1s", [P, HF])
        b1s = two("b1s", [P, HF])
        W2s = two("W2s", [P, HP // 2])
        W2T = two("W2T", [P, HF])
        b2s = two("b2s", [P, HD])
        hA, hB = two("hA", [P, P]), two("hB", [WB, P])
        QKV = sb("QKV", [P, 3 * W])
        K_bd, Q_bd = two("K_bd", [P, HP]), sb("Q_bd", [P, HP])
        KT, QT = sb("KT", [P, HP]), two("QT", [P, HP])
        M1T, M2T = two("M1T", [P, HP]), sb("M2T", [P, HP])
        target, tt = two("target", [P, HD]), sb("tt", [P, HD])
        x, x_sq, arg, th = sb("x", [P, HF]), sb("x_sq", [P, HF]), sb("arg", [P, HF]), sb("th", [P, HF])
        tmp, dg = sb("tmp", [P, HF]), sb("dg", [P, HF])
        X2 = two("X2", [P, HF])
        X2T, XbT = two("X2Tr", [P, HF]), sb("XbT", [P, HF])
        xb, X2b = sb("xb", [P, HF]), sb("X2b", [P, HF])
        Zm, Zb, b2_copy = sb("Zm", [P, HP]), sb("Zb", [P, HP]), sb("b2_copy", [P, HD])
        z, zc, zs, xh, g = sb("z", [P, HD]), sb("zc", [P, HD]), sb("zs", [P, HD]), sb("xh", [P, HD]), sb("g", [P, HD])
        st = sb("st", [P, 8, NH])
        G2, G2bd, GT = two("G2v", [P, HD]), two("G2bd", [P, HP]), sb("GT", [P, HP])
        G1 = sb("G1v", [P, HF])
        out = two("scan_out", [P, HD])
        bank = [ctx.enter_context(nc.psum_tensor(f"scan_bank{i}", [P, BANK], F32)) for i in range(NBANK)]

        consts_loaded, consts_made, state_made = sem("consts_loaded"), sem("consts_made"), sem("state_made")
        pe_filled, act_done, dve_done, pool_done = sem("pe_filled"), sem("act_done"), sem("dve_done"), sem("pool_done")
        h_loaded = [sem("h_loaded0"), sem("h_loaded1")]
        out_stored = [sem("out_stored0"), sem("out_stored1")]
        q_stored, first_projected, first_copied = sem("q_stored"), sem("first_projected"), sem("first_copied")
        done = {"act": act_done, "dve": dve_done}
        per = {"act": len(ACT_STEPS), "dve": len(DVE_STEPS), "pool": len(POOL_STEPS), "pe": NJ}

        class Step:
            def __init__(self, i, c):
                self.i, self.c = i, c
                self.n, self.u, self.p = c % 2, (c - 1) % 2, c % 2

            def at(self, each, k, back=0):
                const = each * (self.c - back) + k
                return const if isinstance(self.i, int) else self.i * (2 * each) + const

        def bank_of(s, job):
            return bank[(s.c * NP + SLOT_OF[job]) % NBANK]

        def act_at(s, name, back=0):
            return s.at(per["act"], ACT_STEPS.index(name) + 1, back)

        def dve_at(s, name, back=0):
            return s.at(per["dve"], DVE_STEPS.index(name) + 1, back)

        def pool_at(s, name, back=0):
            return s.at(per["pool"], POOL_STEPS.index(name) + 1, back)

        def pe_at(s, job, back=0):
            return s.at(NJ, SLOTS.index(job) + 1, back)

        def steps(eng, first, body, last, sign_off=None):
            first(Step(0, 0))
            with eng.Fori(0, NU // 2) as i:
                body(Step(i, 1))
                body(Step(i, 2))
            last(Step(0, NU + 1))

        head = lambda ap, h, n: ap[:, h * n:(h + 1) * n]
        SPLIT = [(0, 2, 4, 6), (1, 3, 5, 7), (8, 10), (9, 11)]
        PLACE = {h: n for n, h in enumerate(h for hs in SPLIT for h in hs)}
        rows_of = lambda h: slice(F * (h % 2), F * (h % 2) + F)
        heads4 = lambda ap: ap.rearrange("p (h n) -> p h n", n=P)

        def split_view(ap, k):
            part = ap[:, 0:8 * P] if k < 2 else ap[:, 8 * P:]
            return part.rearrange("p (h two n) -> p two h n", two=2, n=P)[:, k % 2]

        def split_bank(pb, k):
            return pb[:, 0:len(SPLIT[k]) * P].rearrange("p (h n) -> p h n", n=P)

        def split_mask(m, k):
            return bcast(m[:, :], 1, len(SPLIT[k]))

        with nc.Block() as block:
            @block.sync
            def _(sp):
                w2v = A["W2"].rearrange("(q two) f d -> two f q d", two=2)
                loads = [(block_mask[:], A["block_mask"]), (neg_tril[:], A["triu_mask"]), (recip[:], A["recip"]),
                         (tok[:], A["learn"].broadcast_to([P, MB])),
                         (lnw[:], A["lnw"].broadcast_to([P, HD])), (lnb[:], A["lnb"].broadcast_to([P, HD])),
                         (b1s[0][:], A["ab1"].broadcast_to([P, HF])), (b1s[1][:], A["ab1"].broadcast_to([P, HF])),
                         (b2s[0][:], A["ab2"].broadcast_to([P, HD])), (b2s[1][:], A["ab2"].broadcast_to([P, HD])),
                         (WqkvA[:], A["Wqkv"][0:P, :]), (WqkvB[:], A["Wqkv"][P:W, :]),
                         (w2_small[0:F], w2v[0]), (w2_small[F:P], w2v[1])]
                for k in range(2):
                    for b in range(BH):
                        loads.append((W1s[k][b * D:(b + 1) * D, :].rearrange("p (h f) -> p h f", f=F),
                                      A["W1"].rearrange("h d f -> d h f")))
                assert len(loads) == 14 + 2 * BH
                for dst, src in loads:
                    sp.dma_start(dst, src).then_inc(consts_loaded, 16)

                def load_h(row, par):
                    sp.dma_start(hA[par][:], hT[row, 0:P, :].rearrange("u f k -> (u f) k")).then_inc(h_loaded[par], 16)
                    sp.dma_start(hB[par][:], hT[row, P:W, :].rearrange("u f k -> (u f) k")).then_inc(h_loaded[par], 16)

                def store_q(row):
                    sp.dma_start(q_dram[row, :, :].rearrange("u p k -> (u p) k"), QKV[:, 0:W]).then_inc(q_stored, 16)

                def first(s):
                    for par in range(2):
                        sp.sem_inc(out_stored[par], 16)
                    load_h(slice(0, 1), 0)
                    load_h(slice(1, 2), 1)
                    sp.wait_ge(first_projected, 2)
                    load_h(slice(2, 3), 0)
                    sp.wait_ge(first_copied, 2)
                    store_q(slice(0, 1))
                    sp.wait_ge(act_done, act_at(s, "proj1"))
                    store_q(slice(1, 2))

                def body(s):
                    sp.wait_ge(pe_filled, pe_at(s, "proj1", 1))
                    load_h(bass.ds(s.i * 2 + (s.c + 2), 1), s.n)
                    sp.wait_ge(act_done, act_at(s, "proj1"))
                    store_q(bass.ds(s.i * 2 + (s.c + 1), 1))
                    sp.wait_ge(pool_done, pool_at(s, "out"))
                    sp.dma_start(attn[bass.ds(s.i * 2 + (s.c - 1), 1), :, :].rearrange("u p k -> (u p) k"),
                                 out[s.p][:]).then_inc(out_stored[s.p], 16)

                def last(s):
                    sp.wait_ge(pool_done, pool_at(s, "out"))
                    sp.dma_start(attn[NU, :, :], out[s.p][:]).then_inc(out_stored[s.p], 16)
                    sp.wait_ge(q_stored, 16 * (NU + 2))
                    sp.wait_ge(out_stored[0], 16 * (NU // 2 + 1))
                    sp.wait_ge(out_stored[1], 16 * (NU // 2 + 2))
                    for par in range(2):
                        sp.wait_ge(h_loaded[par], 32 * len(range(par, NU + SPARE, 2)))

                steps(sp, first, body, last)

            @block.tensor
            def _(pe):
                def free(s, job):
                    step, slot = PREV[SLOT_OF[job]]
                    prev = PADDED[slot]
                    r = READER[prev]
                    if not (isinstance(s.i, int) and s.c + step < 0):
                        pe.wait_ge(done[r], s.at(per[r], count_of(r, prev), -step))
                    return bank_of(s, job)

                def projection(pb, k, par):
                    c = slice(k * 288, (k + 1) * 288)
                    nc.tensor.matmul(pb[:, 0:288], hA[par][:], WqkvA[:, c], start=True, stop=False)
                    return nc.tensor.matmul(pb[:, 0:288], hB[par][:], WqkvB[:, c], start=False, stop=True)

                def proj(s):
                    pe.wait_ge(h_loaded[1 - s.n], s.i * 32 + 32 * ((s.c + 1) // 2 + 1))
                    for k in range(2):
                        projection(free(s, f"proj{k}"), k, 1 - s.n).then_inc(pe_filled, 1)

                def transposes(s, job, k, src, blocks):
                    pb = free(s, f"{job}{k}")
                    for m, h in enumerate(blocks):
                        q = nc.tensor.transpose(head(pb, m, P), head(src, h, P), ident[:])
                    q.then_inc(pe_filled, 1)

                def kq(s):
                    pe.wait_ge(pool_done, pool_at(s, "k_bd"))
                    for k in range(3):
                        transposes(s, "kqT", k, K_bd[s.n], range(4 * k, 4 * k + 4))
                    pe.wait_ge(pool_done, pool_at(s, "q_bd"))
                    for k in range(3):
                        transposes(s, "kqT", 3 + k, Q_bd, range(4 * k, 4 * k + 4))

                def w2T(s):
                    transposes(s, "w2T", 0, W2s[s.p], range(4))
                    transposes(s, "w2T", 1, W2s[s.p], range(4, 6))

                def m1(s):
                    pe.wait_ge(act_done, act_at(s, "kqT5"))
                    for k in range(3):
                        pb = free(s, f"m1{k}")
                        for m in range(4):
                            h = 4 * k + m
                            q = nc.tensor.matmul(head(pb, m, P), head(KT, h, P), head(QT[s.n], h, P), start=True, stop=True)
                        q.then_inc(pe_filled, 1)

                def z1(s):
                    if not (isinstance(s.i, int) and s.c == 0):
                        pe.wait_ge(dve_done, dve_at(s, "w11", 1))
                    by64(s, "z1", lambda o, h: nc.tensor.matmul(o, head(KT, h, P), head(W1s[s.n], h, F), start=True, stop=True))

                def by64(s, job, product):
                    for k, hs in enumerate((range(8), range(8, 12))):
                        pb = free(s, f"{job}{k}")
                        for m, h in enumerate(hs):
                            q = product(head(pb, m, F), h)
                        q.then_inc(pe_filled, 1)

                def xbT(s):
                    pe.wait_ge(act_done, act_at(s, "gelu_b", 1))
                    transposes(s, "xbT", 0, X2b, range(4))
                    transposes(s, "xbT", 1, X2b, range(4, 6))

                def split_jobs(s, job, product):
                    for k in range(4):
                        pb = free(s, f"{job}{k}")
                        for m, h in enumerate(SPLIT[k]):
                            q = product(head(pb, m, P), h)
                        q.then_inc(pe_filled, 1)

                def attn2(s):
                    pe.wait_ge(act_done, act_at(s, "xbT1"))
                    split_jobs(s, "attn", lambda o, h: nc.tensor.matmul(
                        o, head(X2T[s.p][rows_of(h)], h // 2, P), head(XbT[rows_of(h)], h // 2, P), start=True, stop=True))

                def z2b(s):
                    pe.wait_ge(dve_done, dve_at(s, "attn3"))

                    def product(o, h):
                        nc.tensor.matmul(o, head(XbT[rows_of(h)], h // 2, P), head(W2s[s.p][rows_of(h)], h // 2, P),
                                         start=True, stop=False)
                        return nc.tensor.matmul(o, head(M2T, PLACE[h], P), head(G2bd[s.p], h, P), start=False, stop=True)
                    split_jobs(s, "z2b", product)

                def w2(s):
                    for k, qs in enumerate((range(4), range(4, 6))):
                        pb = free(s, f"w2{k}")
                        for m, q2 in enumerate(qs):
                            for par in range(2):
                                h = 2 * q2 + par
                                q = nc.tensor.matmul(pb[rows_of(par), m * P:(m + 1) * P], head(X2[s.p], h, F),
                                                     head(G2bd[s.p], h, P), start=True, stop=True)
                        if k == 1:
                            q = nc.tensor.matmul(pb[:, 2 * P:2 * P + HD], neg_last[:], G2[s.p][:], start=True, stop=True)
                        q.then_inc(pe_filled, 1)

                def skip(s, a, b=None):
                    pe.wait_ge(pe_filled, s.at(NJ, SLOTS.index(a)))
                    pe.sem_inc(pe_filled, (SLOTS.index(b) if b else NJ) - SLOTS.index(a))

                def first(s):
                    skip(s, "xT0", "kqT0")
                    kq(s)
                    w2T(s)
                    m1(s)
                    skip(s, "gT0", "z10")
                    z1(s)
                    proj(s)
                    skip(s, "z1b0")

                def body(s):
                    pe.wait_ge(dve_done, dve_at(s, "x2", 1))
                    transposes(s, "xT", 0, X2[s.u], range(4))
                    transposes(s, "xT", 1, X2[s.u], range(4, 6))
                    xbT(s)
                    attn2(s)
                    split_jobs(s, "z2", lambda o, h: nc.tensor.matmul(
                        o, head(X2T[s.u][rows_of(h)], h // 2, P), head(W2s[s.u][rows_of(h)], h // 2, P), start=True, stop=True))
                    z2b(s)
                    w2(s)
                    kq(s)
                    pe.wait_ge(dve_done, dve_at(s, "w21"))
                    w2T(s)
                    m1(s)
                    pe.wait_ge(pool_done, pool_at(s, "g2_bd"))
                    for k in range(3):
                        transposes(s, "gT", k, G2bd[s.u], range(4 * k, 4 * k + 4))
                    pe.wait_ge(act_done, act_at(s, "gT2"))
                    by64(s, "gx", lambda o, h: nc.tensor.matmul(o, head(GT, h, P), head(W2T[s.u], h, F), start=True, stop=True))
                    z1(s)
                    proj(s)
                    pe.wait_ge(dve_done, dve_at(s, "gx1"))

                    def product(o, h):
                        nc.tensor.matmul(o, head(QT[s.u], h, P), head(W1s[s.u], h, F), start=True, stop=False)
                        return nc.tensor.matmul(o, head(M1T[s.u], h, P), head(G1, h, F), start=False, stop=True)
                    by64(s, "z1b", product)
                    by64(s, "w1", lambda o, h: nc.tensor.matmul(o, head(K_bd[s.u], h, P), head(G1, h, F), start=True, stop=True))
                    for k, c in enumerate((slice(0, BANK), slice(BANK, HF))):
                        pb = free(s, f"b1{k}")
                        nc.tensor.matmul(pb[:, 0:c.stop - c.start], neg_last[:], G1[:, c],
                                         start=True, stop=True).then_inc(pe_filled, 1)

                def last(s):
                    skip(s, "xT0", "xbT0")
                    xbT(s)
                    attn2(s)
                    skip(s, "z20", "z2b0")
                    z2b(s)

                pe.wait_ge(consts_loaded, 16 * (14 + 2 * BH))
                pe.wait_ge(consts_made, 5)
                pe.wait_ge(state_made, 9)
                pe.wait_ge(h_loaded[0], 32)
                for k in range(2):
                    projection(bank[k], k, 0).then_inc(first_projected, 1)
                pe.wait_ge(first_copied, 2)
                steps(pe, first, body, last)

            @block.scalar
            def _(act):
                def skip(s, a, b=None):
                    act.wait_ge(act_done, s.at(per["act"], ACT_STEPS.index(a)))
                    act.sem_inc(act_done, (ACT_STEPS.index(b) if b else len(ACT_STEPS)) - ACT_STEPS.index(a))

                def evac(s, job, dst, width=BANK, **kw):
                    act.wait_ge(pe_filled, pe_at(s, job))
                    nc.scalar.activation(dst, bank_of(s, job)[:, 0:width], ACT.Copy, **kw).then_inc(act_done, 1)

                def proj(s):
                    act.wait_ge(pool_done, pool_at(s, "t2"))
                    act.wait_ge(q_stored, s.at(16, 16))
                    for k in range(2):
                        evac(s, f"proj{k}", QKV[:, k * 288:(k + 1) * 288], 288)

                def kq(s):
                    for k in range(3):
                        evac(s, f"kqT{k}", KT[:, k * BANK:(k + 1) * BANK])
                    for k in range(3):
                        evac(s, f"kqT{3 + k}", QT[s.n][:, k * BANK:(k + 1) * BANK])

                def wide(s, job, dst, **kw):
                    evac(s, f"{job}0", dst[:, 0:BANK], **kw)
                    evac(s, f"{job}1", dst[:, BANK:HF], HF - BANK, **kw)

                def first_layer(s):
                    act.wait_ge(dve_done, dve_at(s, "z11"))
                    nc.scalar.activation(x_sq[:], x[:], ACT.Square).then_inc(act_done, 1)
                    proj(s)
                    act.wait_ge(dve_done, dve_at(s, "arg"))
                    nc.scalar.activation(th[:], arg[:], ACT.Tanh, scale=GELU_C).then_inc(act_done, 1)

                def z2b(s):
                    if not (isinstance(s.i, int) and s.c == 1):
                        act.wait_ge(pool_done, pool_at(s, "zb_fold", 1))
                    for k in range(4):
                        act.wait_ge(pe_filled, pe_at(s, f"z2b{k}"))
                        nc.scalar.activation(split_view(Zb[:], k), split_bank(bank_of(s, f"z2b{k}"), k),
                                             ACT.Copy).then_inc(act_done, 1)

                def first(s):
                    skip(s, "xT0", "kqT0")
                    kq(s)
                    wide(s, "w2T", W2T[s.p])
                    skip(s, "gT0", "sq")
                    first_layer(s)
                    skip(s, "gelu_b")

                def body(s):
                    wide(s, "xT", X2T[s.u], scale=0.5)
                    wide(s, "xbT", XbT)
                    z2b(s)
                    kq(s)
                    wide(s, "w2T", W2T[s.p])
                    for k in range(3):
                        evac(s, f"gT{k}", GT[:, k * BANK:(k + 1) * BANK])
                    first_layer(s)
                    act.wait_ge(dve_done, dve_at(s, "z1b1"))
                    nc.scalar.activation(X2b[:], xb[:], ACT.Gelu_apprx_tanh).then_inc(act_done, 1)

                def last(s):
                    skip(s, "xT0", "xbT0")
                    wide(s, "xbT", XbT)
                    z2b(s)

                for k in range(2):
                    act.wait_ge(first_projected, k + 1)
                    nc.scalar.activation(QKV[:, k * 288:(k + 1) * 288], bank[k][:, 0:288], ACT.Copy).then_inc(first_copied, 1)
                steps(act, first, body, last)

            @block.gpsimd
            def _(pool):
                TT = nc.gpsimd.tensor_tensor

                def skip(s, a, b=None):
                    pool.wait_ge(pool_done, s.at(per["pool"], POOL_STEPS.index(a)))
                    pool.sem_inc(pool_done, (POOL_STEPS.index(b) if b else len(POOL_STEPS)) - POOL_STEPS.index(a))

                def step(ins):
                    ins.then_inc(pool_done, 1)

                def masked(dst, src):
                    step(TT(dst[:].rearrange("p (h b d) -> p h b d", h=NH, b=BH),
                            bcast(src.rearrange("p (h d) -> p h d", h=NH), 2, BH),
                            bcast(block_mask[:].rearrange("p (b d) -> p b d", b=BH), 1, NH), ALU.mult))

                def inputs(s):
                    Q, K, V = (QKV[:, k * W:(k + 1) * W] for k in range(3))
                    masked(K_bd[s.n], K)
                    masked(Q_bd, Q)
                    step(TT(tt[:], K, V, ALU.subtract))
                    pool.wait_ge(pool_done, pool_at(s, "t0"))
                    step(TT(tt[:], tt[:], lnb[:], ALU.add))
                    pool.wait_ge(pool_done, pool_at(s, "t1"))
                    step(TT(target[s.n][:], tt[:], lnw[:], ALU.mult))

                def output(s):
                    pool.wait_ge(act_done, act_at(s, "z2b3"))
                    step(TT(Zb[:].rearrange("p (h n) -> p h n", n=P), Zb[:].rearrange("p (h n) -> p h n", n=P),
                            bcast(block_mask[:, :], 1, NH), ALU.mult))
                    by_image = Zb[:].rearrange("p (h b d) -> p h b d", h=NH, b=BH)
                    n = BH
                    for name in ("zb_mask", "zb_half", "zb_quarter"):
                        pool.wait_ge(pool_done, pool_at(s, name))
                        n //= 2
                        if n > 1:
                            step(TT(by_image[:, :, 0:n], by_image[:, :, 0:n], by_image[:, :, n:2 * n], ALU.add))
                        else:
                            step(TT(out[s.p][:].rearrange("p (h d) -> p h d", h=NH), by_image[:, :, 0], by_image[:, :, 1],
                                    ALU.add))
                    pool.wait_ge(pool_done, pool_at(s, "zb_fold"))
                    step(TT(out[s.p][:], out[s.p][:], b2_copy[:], ALU.add))

                def first(s):
                    pool.wait_ge(first_copied, 2)
                    inputs(s)
                    skip(s, "b2_copy")

                def body(s):
                    pool.wait_ge(act_done, act_at(s, "proj1", 1))
                    pool.wait_ge(pe_filled, pe_at(s, "w11", 1))
                    inputs(s)
                    step(nc.gpsimd.tensor_copy(b2_copy[:], b2s[s.p][:]))
                    pool.wait_ge(dve_done, dve_at(s, "g2"))
                    masked(G2bd[s.u], G2[s.u][:])
                    pool.wait_ge(out_stored[s.p], s.i * 16 + 16)
                    output(s)

                def last(s):
                    skip(s, "k_bd", "b2_copy")
                    step(nc.gpsimd.tensor_copy(b2_copy[:], b2s[s.p][:]))
                    skip(s, "g2_bd", "zb_mask")
                    pool.wait_ge(out_stored[s.p], 16 * (NU // 2 + 1))
                    output(s)

                pool.wait_ge(consts_loaded, 16 * (14 + 2 * BH))
                steps(pool, first, body, last)

            @block.vector
            def _(dve):
                def skip(s, a, b=None):
                    dve.wait_ge(dve_done, s.at(per["dve"], DVE_STEPS.index(a)))
                    dve.sem_inc(dve_done, (DVE_STEPS.index(b) if b else len(DVE_STEPS)) - DVE_STEPS.index(a))

                def own(s, name):
                    dve.wait_ge(dve_done, dve_at(s, name))

                def step(ins):
                    ins.then_inc(dve_done, 1)

                V = nc.vector
                by_head = lambda ap: ap.rearrange("p (h d) -> p h d", h=NH)
                stat = lambda k: bcast(st[:, k, :], 2, D)

                def halves(s, job, emit):
                    for k, c in enumerate((slice(0, BANK), slice(BANK, HF))):
                        dve.wait_ge(pe_filled, pe_at(s, f"{job}{k}"))
                        step(emit(c, bank_of(s, f"{job}{k}")[:, 0:c.stop - c.start]))

                def attention(s, banks):
                    for k in banks:
                        dve.wait_ge(pe_filled, pe_at(s, f"attn{k}"))
                        n0 = PLACE[SPLIT[k][0]] * P
                        step(V.scalar_tensor_tensor(heads4(M2T[:, n0:n0 + len(SPLIT[k]) * P]),
                                                    split_bank(bank_of(s, f"attn{k}"), k), 1.0,
                                                    split_mask(neg_tril, k), ALU.add, ALU.mult))

                def diagonal(s, job, fold, dst, b2):
                    for k in range(4):
                        dve.wait_ge(pe_filled, pe_at(s, f"{job}{k}"))
                        step(V.tensor_tensor(split_view(Zm[:], k), split_bank(bank_of(s, f"{job}{k}"), k),
                                             split_mask(block_mask, k), ALU.mult))
                    own(s, f"{job}3")
                    step(V.tensor_reduce(z[:], Zm[:].rearrange("p (h b d) -> p h d b", h=NH, b=BH), AX, ALU.add))
                    own(s, fold)
                    step(V.tensor_tensor(dst, z[:], b2[:], ALU.add))

                def first(s):
                    skip(s, "da", "m10")
                    m1(s)
                    skip(s, "gx0", "z10")
                    first_layer(s)
                    skip(s, "z1b0", "x2")
                    x2(s)
                    skip(s, "w10")

                def m1(s):
                    for k in range(3):
                        dve.wait_ge(pe_filled, pe_at(s, f"m1{k}"))
                        step(V.scalar_tensor_tensor(heads4(M1T[s.n][:, k * BANK:(k + 1) * BANK]),
                                                    heads4(bank_of(s, f"m1{k}")[:, :]), 1.0,
                                                    bcast(neg_tril[:, :], 1, 4), ALU.add, ALU.mult))

                def first_layer(s):
                    halves(s, "z1", lambda c, pb: V.tensor_tensor(x[:, c], pb, b1s[s.n][:, c], ALU.add))
                    dve.wait_ge(act_done, act_at(s, "sq"))
                    step(V.tensor_scalar(tmp[:], x_sq[:], GELU_A, 1.0, ALU.mult, ALU.add))
                    own(s, "cube")
                    step(V.tensor_tensor(arg[:], tmp[:], x[:], ALU.mult))

                def x2(s):
                    dve.wait_ge(act_done, act_at(s, "tanh"))
                    step(V.scalar_tensor_tensor(X2[s.n][:], th[:], 1.0, x[:], ALU.add, ALU.mult))

                def body(s):
                    step(V.tensor_scalar(tmp[:], x_sq[:], GELU_D, GELU_C, ALU.mult, ALU.add))
                    own(s, "da")
                    step(V.scalar_tensor_tensor(tmp[:], th[:], 1.0, tmp[:], ALU.subtract, ALU.mult))
                    own(s, "db")
                    step(V.tensor_tensor(tmp[:], tmp[:], X2[s.u][:], ALU.mult))
                    attention(s, (0, 1))
                    own(s, "dc")
                    step(V.scalar_tensor_tensor(dg[:], th[:], 1.0, tmp[:], ALU.add, ALU.subtract))
                    attention(s, (2, 3))
                    diagonal(s, "z2", "z2_fold", z[:], b2s[s.u])
                    own(s, "z2_bias")
                    step(V.tensor_reduce(st[:, 0, :], by_head(z[:]), AX, ALU.add))
                    own(s, "mean")
                    step(V.scalar_tensor_tensor(by_head(zc[:]), stat(0), -1.0 / D, by_head(z[:]), ALU.mult, ALU.add))
                    own(s, "center")
                    step(V.tensor_tensor(zs[:], zc[:], zc[:], ALU.mult))
                    own(s, "square")
                    step(V.tensor_reduce(st[:, 1, :], by_head(zs[:]), AX, ALU.add))
                    own(s, "var")
                    rsqrt(nc, step, lambda name: own(s, name), st[:, 2, :], st[:, 6, :], st[:, 7, :], st[:, 1, :],
                          D * EPS_INNER, "r_")
                    step(V.scalar_tensor_tensor(by_head(xh[:]), by_head(zc[:]), float(D) ** 0.5, stat(2), ALU.mult, ALU.mult))
                    own(s, "xhat")
                    step(V.tensor_tensor(zs[:], xh[:], lnw2[:], ALU.mult))
                    own(s, "gxh0")
                    dve.wait_ge(pool_done, pool_at(s, "t2", 1))
                    step(V.tensor_tensor(g[:], zs[:], target[s.u][:], ALU.add))
                    own(s, "gxh")
                    step(V.tensor_reduce(st[:, 3, :], by_head(g[:]), AX, ALU.add))
                    step(V.tensor_tensor(zs[:], g[:], xh[:], ALU.mult))
                    own(s, "gx_xh")
                    step(V.tensor_reduce(st[:, 4, :], by_head(zs[:]), AX, ALU.add))
                    unit = s.i * (2 * NH) + (s.c - 1) * NH
                    step(V.scalar_tensor_tensor(st[:, 5, :], st[:, 2, :], float(D) ** 0.5, LR[:, bass.ds(unit, NH)],
                                                ALU.mult, ALU.mult))
                    halves(s, "w2", lambda c, pb: V.scalar_tensor_tensor(
                        W2s[s.p][:, c], pb, half_last[:, 0:1], W2s[s.p][:, c], ALU.mult, ALU.add))
                    dve.wait_ge(pool_done, pool_at(s, "b2_copy"))
                    step(V.tensor_tensor(b2s[s.p][:], bank_of(s, "w21")[:, 2 * P:2 * P + HD], b2s[s.p][:], ALU.add))
                    own(s, "lr_rstd")
                    step(V.tensor_tensor(by_head(zc[:]), by_head(xh[:]), stat(4), ALU.mult))
                    step(V.scalar_tensor_tensor(by_head(g[:]), stat(3), -1.0 / D, by_head(g[:]), ALU.mult, ALU.add))
                    own(s, "sub1")
                    step(V.scalar_tensor_tensor(g[:], zc[:], -1.0 / D, g[:], ALU.mult, ALU.add))
                    own(s, "sub2")
                    step(V.tensor_tensor(by_head(G2[s.u][:]), by_head(g[:]), stat(5), ALU.mult))
                    m1(s)
                    halves(s, "gx", lambda c, pb: V.scalar_tensor_tensor(G1[:, c], pb, 0.5, dg[:, c], ALU.mult, ALU.mult))
                    first_layer(s)
                    dve.wait_ge(act_done, act_at(s, "gelu_b", 1))
                    halves(s, "z1b", lambda c, pb: V.tensor_tensor(xb[:, c], pb, b1s[s.u][:, c], ALU.add))
                    x2(s)
                    halves(s, "w1", lambda c, pb: V.scalar_tensor_tensor(
                        W1s[s.u][:, c], pb, half_last[:, 1:2], W1s[s.u][:, c], ALU.mult, ALU.add))
                    halves(s, "b1", lambda c, pb: V.tensor_tensor(b1s[s.u][:, c], pb, b1s[s.u][:, c], ALU.add))

                def last(s):
                    skip(s, "da", "attn0")
                    attention(s, (0, 1))
                    skip(s, "dgelu", "attn2")
                    attention(s, (2, 3))

                dve.wait_ge(consts_loaded, 16 * (14 + 2 * BH))
                made = [0]

                def make(ins, wait=True):
                    ins.then_inc(consts_made, 1)
                    made[0] += 1
                    if wait:
                        dve.wait_ge(consts_made, made[0])
                make(V.tensor_tensor(tok[:], tok[:], recip[:], ALU.add))
                make(V.tensor_scalar(tok[:], tok[:], 0.0, None, ALU.max))
                make(V.scalar_tensor_tensor(neg_tril[:].rearrange("p (b k) -> p b k", b=BH),
                                            neg_tril[:].rearrange("p (b k) -> p b k", b=BH), -1.0,
                                            bcast(tok[:, :], 1, BH), ALU.mult, ALU.mult))
                make(V.tensor_scalar(half_last[:, 0:1], tok[:, MB - 1:MB], -0.5, None, ALU.mult))
                make(V.tensor_scalar(half_last[:, 1:2], tok[:, MB - 1:MB], -1.0, None, ALU.mult))
                V.tensor_scalar(neg_last[:], block_mask[:], half_last[:, 1:2], None, ALU.mult).then_inc(state_made, 1)
                for k in range(2):
                    V.tensor_copy(W2s[k][:].rearrange("p (q b d) -> p q b d", q=NH // 2, b=BH),
                                  bcast(w2_small[:], 2, BH)).then_inc(state_made, 1)
                V.tensor_tensor(lnw2[:], lnw[:], lnw[:], ALU.mult).then_inc(state_made, 1)
                for t in (X2T[1], X2b, X2[1], G2bd[1], G2[1]):
                    V.memset(t[:], 0.0).then_inc(state_made, 1)
                dve.wait_ge(state_made, 9)
                steps(dve, first, body, last)


GU = 4
NG = NU // GU
GPE = ["gate0", "gate1", "oT0", "oT1", "h0", "h1", "hT0", "hT1"]
GACT = ["gate0", "gate1", "oT0", "oT1", "hT0", "hT1"]


def ln_steps(tag):
    return ([f"{tag}bn{j}" for j in range(GU)] + [f"{tag}{x}" for x in ("sum", "diff", "m2", "between", "var")] + rsqrt_steps(tag) + [f"{tag}shift"]
            + [f"{tag}norm{j}" for j in range(GU)])


GDVE = ["i_mean", "i_center", "i_square", "i_var"] + rsqrt_steps("i_") + ["i_xhat", "i_scale", "i_query", "i_beta"] + ln_steps("o_") + ["weight", "bias", "gated"] + ln_steps("h_")
MDVE = ([f"y{e}_{j}" for e in range(E) for j in range(GU)] + ln_steps("m_")
        + ["gamma", "beta", "residual"] + ln_steps("f_"))
MPE = []
for _e in range(E + 1):
    if _e < E:
        MPE += [f"z{2 * _e}", f"z{2 * _e + 1}"]
    if _e > 0:
        MPE += [f"y{_e - 1}_0", f"y{_e - 1}_1"]
MACT = [f"z{c}" for c in range(EC)]


class Group:
    def __init__(self, i, c):
        self.i, self.c = i, c

    def at(self, names, name, back=0):
        each = len(names)
        return self.i * (2 * each) + each * (self.c + 1 - back) + names.index(name) + 1

    def row(self, n, first=0):
        return bass.ds(self.i * (2 * GU * n) + (self.c * GU * n + first), GU * n)


def groups(eng, body):
    with eng.Fori(0, NG // 2) as i:
        body(Group(i, 0))
        body(Group(i, 1))


def layer_norm(nc, step, own, src, dst, stats, mv, rs, eps, tag):
    V = nc.vector
    for j in range(GU):
        step(V.bn_stats(stats[:, j, :], src(j)))
    own(f"{tag}bn{GU - 1}")
    mean2, diff, m2, var = (mv[:, k, :] for k in range(4))
    step(V.tensor_tensor(mean2, stats[:, :, 1], stats[:, :, 4], ALU.add))
    step(V.tensor_tensor(diff, stats[:, :, 1], stats[:, :, 4], ALU.subtract))
    step(V.tensor_tensor(m2, stats[:, :, 2], stats[:, :, 5], ALU.add))
    own(f"{tag}m2")
    step(V.scalar_tensor_tensor(diff, diff, 0.25, diff, ALU.mult, ALU.mult))
    own(f"{tag}between")
    step(V.scalar_tensor_tensor(var, m2, 1.0 / W, diff, ALU.mult, ALU.add))
    own(f"{tag}var")
    rsqrt(nc, step, own, rs[:, 0, :], rs[:, 1, :], rs[:, 2, :], var, eps, tag)
    step(V.scalar_tensor_tensor(rs[:, 3, :], mean2, -0.5, rs[:, 0, :], ALU.mult, ALU.mult))
    own(f"{tag}shift")
    for j in range(GU):
        step(V.tensor_scalar(dst(j), src(j), rs[:, 0, j:j + 1], rs[:, 3, j:j + 1], ALU.mult, ALU.add))
    own(f"{tag}norm{GU - 1}")


def attention_out(nc, A, hT, attn, q_dram, h2_dram, H2TA, H2TB, ident):
    with ExitStack() as ctx:
        sb = lambda name, shape: ctx.enter_context(nc.sbuf_tensor(name, shape, F32))
        two = lambda name, shape: [sb(f"{name}_{i}", shape) for i in range(2)]
        sem = lambda name: ctx.enter_context(nc.semaphore(name))
        WgA, WgB = sb("WgA", [P, W]), sb("WgB", [WB, W])
        WoA, WoB = sb("WoA", [P, W]), sb("WoB", [WB, W])
        pw, pb_ = sb("pw", [P, W]), sb("pb", [P, W])
        lnw, lnb = sb("lnw3", [P, W]), sb("lnb3", [P, W])
        O, Qr, hA, hB = two("O", [P, GU, W]), two("Qr", [P, GU, W]), two("ghA", [P, GU, P]), two("ghB", [WB, GU, P])
        sq, ist = sb("sq3", [P, GU, W]), sb("ist", [P, 5, GU * NH])
        gate, normed = sb("gate", [P, GU, W]), sb("normed", [P, GU, W])
        oTA, oTB = sb("oTA", [P, GU * P]), sb("oTB", [WB, GU * P])
        h2 = two("h2", [P, GU, W])
        stats, mv, rs = sb("stats", [P, GU, 6]), sb("mv", [P, 4, GU]), sb("rs", [P, 4, GU])
        bank = [ctx.enter_context(nc.psum_tensor(f"out_bank{i}", [P, BANK], F32)) for i in range(NBANK)]
        weights_loaded = sem("out_weights_loaded")
        in_loaded = [sem("in_loaded0"), sem("in_loaded1")]
        h2_stored = [sem("h2_stored0"), sem("h2_stored1")]
        pe_filled, act_done, dve_done = sem("o_pe_filled"), sem("o_act_done"), sem("o_dve_done")
        bank_of = {name: bank[k] for k, name in enumerate(GPE)}
        unit_pair = lambda pb: pb[:, 0:2 * W].rearrange("p (j n) -> p j n", j=2)

        with nc.Block() as block:
            @block.sync
            def _(sp):
                def load(s, ahead):
                    r = s.i * (2 * GU) + (s.c + ahead) * GU
                    for dst, src in ((O[s.c], attn[bass.ds(r + 1, GU), :, :].rearrange("u p k -> p u k")),
                                     (Qr[s.c], q_dram[bass.ds(r, GU), :, :].rearrange("u p k -> p u k")),
                                     (hA[s.c], hT[bass.ds(r, GU), 0:P, :].rearrange("u f k -> f u k")),
                                     (hB[s.c], hT[bass.ds(r, GU), P:W, :].rearrange("u f k -> f u k"))):
                        sp.dma_start(dst[:], src).then_inc(in_loaded[s.c], 16)

                def store(s):
                    sp.wait_ge(dve_done, s.at(GDVE, f"h_norm{GU - 1}"))
                    sp.dma_start(h2_dram[s.row(1), :, :].rearrange("u p k -> p u k"), h2[s.c][:]).then_inc(h2_stored[s.c], 16)

                def body(s):
                    store(s)
                    sp.wait_ge(pe_filled, s.at(GPE, "h1"))
                    load(s, 2)

                for c in range(2):
                    sp.sem_inc(h2_stored[c], 16)
                load(Group(0, 0), 0)
                load(Group(0, 1), 0)
                for dst, src in ((WgA, A["Wg"][0:P, :]), (WgB, A["Wg"][P:W, :]), (WoA, A["Wo"][0:P, :]),
                                 (WoB, A["Wo"][P:W, :]), (pw, A["pw"].broadcast_to([P, W])),
                                 (pb_, A["pb"].broadcast_to([P, W])),
                                 (lnw, A["lnw"].broadcast_to([P, W])), (lnb, A["lnb"].broadcast_to([P, W]))):
                    sp.dma_start(dst[:], src).then_inc(weights_loaded, 16)
                with sp.Fori(0, NG // 2 - 1) as i:
                    body(Group(i, 0))
                    body(Group(i, 1))
                for c in range(2):
                    store(Group(NG // 2 - 1, c))
                for c in range(2):
                    sp.wait_ge(h2_stored[c], 16 * (NG // 2 + 1))

            @block.tensor
            def _(pe):
                pe.sem_inc(pe_filled, len(GPE))
                pe.wait_ge(weights_loaded, 16 * 8)

                def body(s):
                    pe.wait_ge(in_loaded[s.c], s.i * 64 + 64)
                    for k in range(2):
                        pe.wait_ge(act_done, s.at(GACT, f"gate{k}", 1))
                        for m in range(2):
                            j = 2 * k + m
                            o = bank_of[f"gate{k}"][:, m * W:(m + 1) * W]
                            nc.tensor.matmul(o, hA[s.c][:, j, :], WgA[:], start=True, stop=False)
                            q = nc.tensor.matmul(o, hB[s.c][:, j, :], WgB[:], start=False, stop=True)
                        q.then_inc(pe_filled, 1)
                    pe.wait_ge(dve_done, s.at(GDVE, "gated"))
                    pe.wait_ge(act_done, s.at(GACT, "oT1", 1))
                    for k, (f0, f1) in enumerate(((0, P), (P, W))):
                        for j in range(GU):
                            q = nc.tensor.transpose(bank_of[f"oT{k}"][0:f1 - f0, j * P:(j + 1) * P],
                                                    normed[:, j, f0:f1], ident[:])
                        q.then_inc(pe_filled, 1)
                    pe.wait_ge(act_done, s.at(GACT, "oT1"))
                    for k in range(2):
                        pe.wait_ge(dve_done, s.at(GDVE, f"h_norm{GU - 1}", 1))
                        for m in range(2):
                            j = 2 * k + m
                            c = slice(j * P, (j + 1) * P)
                            o = bank_of[f"h{k}"][:, m * W:(m + 1) * W]
                            nc.tensor.matmul(o, oTA[:, c], WoA[:], start=True, stop=False)
                            nc.tensor.matmul(o, oTB[:, c], WoB[:], start=False, stop=False)
                            nc.tensor.matmul(o[:, 0:P], hA[s.c][:, j, :], ident[:], start=False, stop=False)
                            q = nc.tensor.matmul(o[:, P:W], hB[s.c][:, j, :], ident[0:WB, 0:WB], start=False, stop=True)
                        q.then_inc(pe_filled, 1)
                    pe.wait_ge(dve_done, s.at(GDVE, f"h_norm{GU - 1}"))
                    pe.wait_ge(act_done, s.at(GACT, "hT1", 1))
                    for k, (f0, f1) in enumerate(((0, P), (P, W))):
                        for j in range(GU):
                            q = nc.tensor.transpose(bank_of[f"hT{k}"][0:f1 - f0, j * P:(j + 1) * P],
                                                    h2[s.c][:, j, f0:f1], ident[:])
                        q.then_inc(pe_filled, 1)
                groups(pe, body)

            @block.scalar
            def _(act):
                act.sem_inc(act_done, len(GACT))

                def body(s):
                    def evac(name, dst, src, func=ACT.Copy):
                        act.wait_ge(pe_filled, s.at(GPE, name))
                        nc.scalar.activation(dst, src, func).then_inc(act_done, 1)
                    act.wait_ge(dve_done, s.at(GDVE, "gated", 1))
                    for k in range(2):
                        evac(f"gate{k}", gate[:, 2 * k:2 * k + 2, :], unit_pair(bank_of[f"gate{k}"]), ACT.Gelu_apprx_tanh)
                    evac("oT0", oTA[:], bank_of["oT0"][:, :])
                    evac("oT1", oTB[:], bank_of["oT1"][0:WB, :])
                    evac("hT0", H2TA[:, s.row(P)], bank_of["hT0"][:, :])
                    evac("hT1", H2TB[0:WB, s.row(P)], bank_of["hT1"][0:WB, :])
                groups(act, body)

            @block.vector
            def _(dve):
                V = nc.vector
                dve.sem_inc(dve_done, len(GDVE))
                dve.wait_ge(weights_loaded, 16 * 8)

                def body(s):
                    step = lambda ins: ins.then_inc(dve_done, 1)
                    own = lambda name: dve.wait_ge(dve_done, s.at(GDVE, name))
                    dve.wait_ge(in_loaded[s.c], s.i * 64 + 64)
                    o, by = O[s.c][:].rearrange("p u k -> p (u k)"), lambda t: t.rearrange("p (g d) -> p g d", d=D)
                    sf = sq[:].rearrange("p u k -> p (u k)")
                    stat = lambda k: bcast(ist[:, k, :], 2, D)
                    step(V.tensor_reduce(ist[:, 0, :], by(o), AX, ALU.add))
                    own("i_mean")
                    step(V.scalar_tensor_tensor(by(o), stat(0), -1.0 / D, by(o), ALU.mult, ALU.add))
                    own("i_center")
                    step(V.tensor_tensor(sf, o, o, ALU.mult))
                    own("i_square")
                    step(V.tensor_reduce(ist[:, 1, :], by(sf), AX, ALU.add))
                    own("i_var")
                    rsqrt(nc, step, own, ist[:, 2, :], ist[:, 3, :], ist[:, 4, :], ist[:, 1, :], D * EPS_INNER, "i_")
                    step(V.scalar_tensor_tensor(by(o), by(o), float(D) ** 0.5, stat(2), ALU.mult, ALU.mult))
                    own("i_xhat")
                    step(V.tensor_tensor(O[s.c][:], O[s.c][:], bcast(lnw[:, :], 1, GU), ALU.mult))
                    own("i_scale")
                    step(V.tensor_tensor(O[s.c][:], O[s.c][:], Qr[s.c][:], ALU.add))
                    own("i_query")
                    step(V.tensor_tensor(O[s.c][:], O[s.c][:], bcast(lnb[:, :], 1, GU), ALU.add))
                    own("i_beta")
                    layer_norm(nc, step, own, lambda j: O[s.c][:, j, :], lambda j: normed[:, j, :], stats, mv, rs,
                               EPS_INNER, "o_")
                    step(V.tensor_tensor(normed[:], normed[:], bcast(pw[:, :], 1, GU), ALU.mult))
                    own("weight")
                    step(V.tensor_tensor(normed[:], normed[:], bcast(pb_[:, :], 1, GU), ALU.add))
                    own("bias")
                    dve.wait_ge(act_done, s.at(GACT, "gate1"))
                    step(V.tensor_tensor(normed[:], normed[:], gate[:], ALU.mult))
                    dve.wait_ge(pe_filled, s.at(GPE, "h1"))
                    dve.wait_ge(h2_stored[s.c], s.i * 16 + 16)
                    layer_norm(nc, step, own, lambda j: unit_pair(bank_of[f"h{j // 2}"])[:, j % 2, :],
                               lambda j: h2[s.c][:, j, :], stats, mv, rs, EPS_LN, "h_")
                groups(dve, body)


def experts(nc, A, out_dram, h2_dram, H2TA, H2TB):
    with ExitStack() as ctx:
        sb = lambda name, shape: ctx.enter_context(nc.sbuf_tensor(name, shape, F32))
        two = lambda name, shape: [sb(f"{name}_{i}", shape) for i in range(2)]
        sem = lambda name: ctx.enter_context(nc.semaphore(name))
        HR = W // 2
        gamma, beta = sb("gamma", [P, W]), sb("beta", [P, W])
        w1A, w1B, w2r = sb("w1A", [P, HR]), sb("w1B", [WB + 1, HR]), sb("w2r", [HR + 1, E])
        downA, downB = sb("downA", [P, E * DE]), sb("downB", [WB + 1, E * DE])
        up = sb("up", [P, EC, W])
        rank = sb("rank", [P, E])
        router = two("router", [HR + 1, GU * P])
        gates, logit, picked = sb("gates", [P, NU * E]), sb("logit", [P, NU * E]), sb("picked", [P, NU * E])
        eq, score = sb("eq", [P, NU * E]), sb("score", [P, NU * E])
        col = sb("col", [P, 8, NU])
        Z = sb("Z", [P, 4, GU * P])
        h2, acc = two("mh2", [P, GU, W]), two("acc", [P, GU, W])
        stats, mv, rs = sb("mstats", [P, GU, 6]), sb("mmv", [P, 4, GU]), sb("mrs", [P, 4, GU])
        bank = [ctx.enter_context(nc.psum_tensor(f"moe_bank{i}", [P, BANK], F32)) for i in range(NBANK)]
        router_loaded, weights_loaded, ones_set = sem("router_loaded"), sem("moe_weights_loaded"), sem("moe_ones_set")
        in_loaded = [sem("h2_loaded0"), sem("h2_loaded1")]
        out_stored = [sem("y_stored0"), sem("y_stored1")]
        r_filled, r_act, r_dve = sem("router_filled"), sem("router_act"), sem("router_dve")
        pe_filled, act_done, dve_done = sem("m_pe_filled"), sem("m_act_done"), sem("m_dve_done")
        z_bank = lambda c: bank[c % 4]
        y_bank = lambda e, k: bank[4 + 2 * (e % 2) + k]

        with nc.Block() as block:
            @block.sync
            def _(sp):
                for dst, src in ((w1A[:], A["fw1"][0:P, :]), (w1B[0:WB, :], A["fw1"][P:W, :]), (w1B[WB:WB + 1, :], A["fb1"]),
                                 (w2r[0:HR, :], A["fw2"]), (w2r[HR:HR + 1, :], A["fb2"]),
                                 (rank[:], A["rank"].broadcast_to([P, E]))):
                    sp.dma_start(dst, src).then_inc(router_loaded, 16)
                dn = A["down"].rearrange("e h d -> h e d")
                for dst, src in ((downA[:].rearrange("p (e d) -> p e d", e=E), dn[0:P]),
                                 (downB[0:WB, :].rearrange("p (e d) -> p e d", e=E), dn[P:W]),
                                 (downB[WB:WB + 1, :], A["downb"]),
                                 (up[:], A["up"].rearrange("(c p) h -> p c h", p=P)),
                                 (gamma[:], A["gamma"].broadcast_to([P, W])), (beta[:], A["beta"].broadcast_to([P, W]))):
                    sp.dma_start(dst, src).then_inc(weights_loaded, 16)

                def load(s, ahead):
                    sp.dma_start(h2[s.c][:], h2_dram[bass.ds(s.i * (2 * GU) + (s.c + ahead) * GU, GU), :, :].rearrange(
                        "u p k -> p u k")).then_inc(in_loaded[s.c], 16)

                def store(s):
                    sp.wait_ge(dve_done, s.at(MDVE, f"f_norm{GU - 1}"))
                    sp.dma_start(out_dram[s.row(1), :, :].rearrange("u p k -> p u k"), acc[s.c][:]).then_inc(out_stored[s.c], 16)

                for c in range(2):
                    sp.sem_inc(out_stored[c], 16)
                load(Group(0, 0), 0)
                load(Group(0, 1), 0)
                with sp.Fori(0, NG // 2 - 1) as i:
                    for c in range(2):
                        store(Group(i, c))
                        load(Group(i, c), 2)
                for c in range(2):
                    store(Group(NG // 2 - 1, c))
                for c in range(2):
                    sp.wait_ge(out_stored[c], 16 * (NG // 2 + 1))

            @block.gpsimd
            def _(pool):
                nc.gpsimd.memset(H2TB[WB:WB + 1, :], 1.0).then_inc(ones_set, 1)
                for k in range(2):
                    nc.gpsimd.memset(router[k][HR:HR + 1, :], 1.0).then_inc(ones_set, 1)

            @block.tensor
            def _(pe):
                pe.wait_ge(router_loaded, 16 * 6)
                pe.wait_ge(ones_set, 3)

                def hidden(g):
                    c = slice(g * GU * P, (g + 1) * GU * P)
                    if g >= 2:
                        pe.wait_ge(r_act, g - 1)
                    nc.tensor.matmul(bank[g % 2][0:HR, :], w1A[:], H2TA[:, c], start=True, stop=False)
                    nc.tensor.matmul(bank[g % 2][0:HR, :], w1B[:], H2TB[:, c], start=False, stop=True).then_inc(r_filled, 1)

                def logits(g):
                    pe.wait_ge(r_act, g + 1)
                    for j in range(GU):
                        u = g * GU + j
                        q = nc.tensor.matmul(bank[2][:, u * E:(u + 1) * E], router[g % 2][:, j * P:(j + 1) * P], w2r[:],
                                             start=True, stop=True)
                    q.then_inc(r_filled, 1)
                hidden(0)
                for g in range(NG):
                    if g + 1 < NG:
                        hidden(g + 1)
                    logits(g)

                pe.wait_ge(weights_loaded, 16 * 6)
                pe.wait_ge(r_dve, 1)
                pe.sem_inc(pe_filled, len(MPE))

                def body(s):
                    def z(c):
                        prev = c - 4 if c >= 4 else c - 4 + EC
                        pe.wait_ge(act_done, s.at(MACT, f"z{prev}", 0 if c >= 4 else 1))
                        o, w = z_bank(c)[:, :], slice(c * P, (c + 1) * P)
                        nc.tensor.matmul(o, downA[:, w], H2TA[:, s.row(P)], start=True, stop=False)
                        nc.tensor.matmul(o, downB[:, w], H2TB[:, s.row(P)], start=False, stop=True).then_inc(pe_filled, 1)

                    def y(e):
                        pe.wait_ge(act_done, s.at(MACT, f"z{2 * e + 1}"))
                        for k in range(2):
                            prev = e - 2 if e >= 2 else e - 2 + E
                            pe.wait_ge(dve_done, s.at(MDVE, f"y{prev}_{2 * k + 1}", 0 if e >= 2 else 1))
                            for m in range(2):
                                j = 2 * k + m
                                o = y_bank(e, k)[:, m * W:(m + 1) * W]
                                for d in range(2):
                                    c = 2 * e + d
                                    q = nc.tensor.matmul(o, Z[:, c % 4, j * P:(j + 1) * P], up[:, c, :],
                                                         start=(d == 0), stop=(d == 1))
                            q.then_inc(pe_filled, 1)
                    for e in range(E + 1):
                        if e < E:
                            z(2 * e)
                            z(2 * e + 1)
                        if e > 0:
                            y(e - 1)
                groups(pe, body)

            @block.scalar
            def _(act):
                for g in range(NG):
                    act.wait_ge(r_filled, max(2 * g, 1))
                    nc.scalar.activation(router[g % 2][0:HR, :], bank[g % 2][0:HR, :], ACT.Gelu).then_inc(r_act, 1)
                act.wait_ge(r_dve, 3)
                nc.scalar.activation(picked[:], logit[:], ACT.Exp).then_inc(r_act, 1)
                act.sem_inc(act_done, len(MACT))

                def body(s):
                    for c in range(EC):
                        act.wait_ge(pe_filled, s.at(MPE, f"z{c}"))
                        prev = c // 2 - 2
                        act.wait_ge(pe_filled, s.at(MPE, f"y{prev}_1") if prev >= 0 else s.at(MPE, f"y{prev + E}_1", 1))
                        nc.scalar.activation(Z[:, c % 4, :], z_bank(c)[:, :], ACT.Gelu).then_inc(act_done, 1)
                groups(act, body)

            @block.vector
            def _(dve):
                V = nc.vector
                n = [0]

                def link(ins):
                    n[0] += 1
                    ins.then_inc(r_dve, 1)
                    dve.wait_ge(r_dve, n[0])
                ue = lambda t: t[:].rearrange("p (u e) -> p u e", e=E)
                c_ = lambda k: bcast(col[:, k, :], 2, E)
                dve.wait_ge(r_filled, 2 * NG)
                dve.wait_ge(router_loaded, 16 * 6)
                link(V.tensor_copy(logit[:], bank[2][:, 0:NU * E]))
                link(V.tensor_reduce(col[:, 0, :], ue(logit), AX, ALU.max))
                link(V.tensor_tensor(ue(logit), ue(logit), c_(0), ALU.subtract))
                dve.wait_ge(r_act, NG + 1)
                link(V.tensor_reduce(col[:, 1, :], ue(picked), AX, ALU.add))
                link(V.reciprocal(col[:, 1, :], col[:, 1, :]))
                link(V.tensor_tensor(ue(gates), ue(picked), c_(1), ALU.mult))
                link(V.tensor_copy(picked[:], gates[:]))
                for k in range(2):
                    link(V.tensor_reduce(col[:, 2, :], ue(picked), AX, ALU.max))
                    link(V.tensor_tensor(ue(eq), ue(picked), c_(2), ALU.is_equal))
                    link(V.tensor_tensor(ue(score), ue(eq), bcast(rank[:, :], 1, NU), ALU.mult))
                    link(V.tensor_reduce(col[:, 3, :], ue(score), AX, ALU.max))
                    link(V.tensor_tensor(ue(eq), ue(score), c_(3), ALU.is_equal))
                    link(V.scalar_tensor_tensor(picked[:], eq[:], -2.0, picked[:], ALU.mult, ALU.add))
                link(V.tensor_scalar(eq[:], picked[:], 0.0, None, ALU.is_lt))
                link(V.tensor_tensor(gates[:], gates[:], eq[:], ALU.mult))
                link(V.tensor_reduce(col[:, 4, :], ue(gates), AX, ALU.add))
                link(V.tensor_scalar(col[:, 4, :], col[:, 4, :], EPS_GATE, None, ALU.add))
                link(V.reciprocal(col[:, 4, :], col[:, 4, :]))
                link(V.tensor_tensor(ue(gates), ue(gates), c_(4), ALU.mult))
                dve.wait_ge(weights_loaded, 16 * 6)
                dve.sem_inc(dve_done, len(MDVE))

                def body(s):
                    step = lambda ins: ins.then_inc(dve_done, 1)
                    own = lambda name: dve.wait_ge(dve_done, s.at(MDVE, name))
                    a, h = acc[s.c], h2[s.c]
                    dve.wait_ge(in_loaded[s.c], s.i * 16 + 16)
                    dve.wait_ge(out_stored[s.c], s.i * 16 + 16)
                    for e in range(E):
                        for j in range(GU):
                            if j % 2 == 0:
                                dve.wait_ge(pe_filled, s.at(MPE, f"y{e}_{j // 2}"))
                            if e > 0:
                                own(f"y{e - 1}_{j}")
                            gate = gates[:, bass.ds(s.i * (2 * GU * E) + ((s.c * GU + j) * E + e), 1)]
                            step(V.scalar_tensor_tensor(a[:, j, :], y_bank(e, j // 2)[:, (j % 2) * W:(j % 2 + 1) * W], gate,
                                                        (h if e == 0 else a)[:, j, :], ALU.mult, ALU.add))
                    own(f"y{E - 1}_{GU - 1}")
                    one = lambda j: a[:, j, :]
                    layer_norm(nc, step, own, one, one, stats, mv, rs, EPS_LN, "m_")
                    step(V.tensor_tensor(a[:], a[:], bcast(gamma[:, :], 1, GU), ALU.mult))
                    own("gamma")
                    step(V.tensor_tensor(a[:], a[:], bcast(beta[:, :], 1, GU), ALU.add))
                    own("beta")
                    step(V.tensor_tensor(a[:], a[:], h[:], ALU.add))
                    own("residual")
                    layer_norm(nc, step, own, one, one, stats, mv, rs, EPS_LN, "f_")
                groups(dve, body)


def build(nc, A, out):
    dram = lambda name, shape: nc.dram_tensor(name, shape, F32, kind="Internal").ap()
    hT = dram("hT", (NU + SPARE, W, P))
    attn = dram("attn", (NU + 1, P, W))
    q_dram = dram("q", (NU + 2, P, W))
    h2_dram = dram("h2", (NU, P, W))
    with ExitStack() as ctx:
        ident = ctx.enter_context(nc.sbuf_tensor("ident_sb", [P, P], F32))
        with nc.sbuf_tensor("LR", [P, NU * NH], F32) as LR:
            tokenizer(nc, A, hT, LR, ident)
            scan(nc, A, hT, attn, q_dram, LR, ident)
        H2TA = ctx.enter_context(nc.sbuf_tensor("H2TA", [P, NU * P], F32))
        H2TB = ctx.enter_context(nc.sbuf_tensor("H2TB", [WB + 1, NU * P], F32))
        attention_out(nc, A, hT, attn, q_dram, h2_dram, H2TA, H2TB, ident)
        experts(nc, A, out, h2_dram, H2TA, H2TB)


def layouts(v):
    def patches(x, side):
        p = 64 // side
        t = x.reshape(B, CH, side, p, side, p).transpose(2, 4, 3, 5, 1, 0)
        return t.reshape(side * side, B * p * p * CH)
    a = {"x0": patches(v["x"], 64), "x1": patches(v["x"], 32), "x2": patches(v["x"], 16)}
    for k in range(3):
        a[f"idx{k}"] = v[f"L0_tok_idx{k}"].reshape(GROUPS[k], GP)
        a[f"W{k}T"] = v[f"L0_tok_W{k}"].T
        a[f"b{k}"] = v[f"L0_tok_b{k}"].reshape(EMB, 1)
    a["WfT"], a["bf"] = v["L0_tok_Wf"].T, v["L0_tok_bf"].reshape(1, W)
    t = lambda n: v["L0_attn_" + n]
    a["lrT"], a["lrb"] = t("lr_weight").reshape(NH, W).T, t("lr_bias").reshape(1, NH)
    a["Wqkv"] = np.concatenate([t("Wq"), t("Wk"), t("Wv")], axis=1)
    a["learn"] = t("learnable_token_idx").reshape(1, MB)
    a["lnw"], a["lnb"] = t("norm_weight").reshape(1, W), t("norm_bias").reshape(1, W)
    a["ab1"], a["ab2"] = t("b1").reshape(1, NH * F), t("b2").reshape(1, NH * D)
    a["W1"], a["W2"], a["Wg"], a["Wo"] = t("W1"), t("W2"), t("Wg"), t("Wo")
    a["pw"], a["pb"] = t("post_norm_weight").reshape(1, W), t("post_norm_bias").reshape(1, W)
    f = lambda n: v["L0_ffn_" + n]
    a["fw1"], a["fb1"], a["fw2"], a["fb2"] = f("w1"), f("b1").reshape(1, W // 2), f("w2"), f("b2").reshape(1, E)
    a["down"], a["downb"], a["up"] = f("down_w"), f("down_b").reshape(1, E * DE), f("up_w").reshape(E * DE, W)
    a["gamma"], a["beta"] = f("gamma").reshape(1, W), f("beta").reshape(1, W)
    i = np.arange(P)
    same = (i[:, None] // MB) == (i[None, :] // MB)
    a["ident"] = np.eye(P, dtype=np.float32)
    a["block_mask"] = same.astype(np.float32)
    a["triu_mask"] = (same & (i[:, None] <= i[None, :])).astype(np.float32)
    a["recip"] = np.tile(np.float32(1) / np.arange(1, MB + 1, dtype=np.float32), (P, 1))
    a["rank"] = np.arange(E, 0, -1, dtype=np.float32).reshape(1, E)
    return {k: np.ascontiguousarray(x) for k, x in a.items()}


def kernel(**inputs):
    import concourse.bacc as bacc
    from concourse.bass_utils import run_bass_kernel_spmd
    nc = bacc.Bacc("TRN2", target_bir_lowering=False, num_devices=1)
    arrays = layouts({k: np.asarray(x) for k, x in inputs.items()})
    aps = {k: nc.dram_tensor(f"in_{k}", x.shape, mybir.dt.from_np(x.dtype), kind="ExternalInput").ap()
           for k, x in arrays.items()}
    out = nc.dram_tensor("out", (NU, P, W), F32, kind="ExternalOutput").ap()
    build(nc, aps, out)
    r = run_bass_kernel_spmd(nc, [{f"in_{k}": x for k, x in arrays.items()}], core_ids=[0])
    y = r.results[0]["out"].reshape(NS, B // BH, BH, MB, W)
    return y.transpose(1, 2, 0, 3, 4).reshape(B, T, W)
```

```python
import numpy as np
import concourse.bass as bass
from concourse import mybir
from contextlib import ExitStack

F32 = mybir.dt.float32
U32 = mybir.dt.uint32
ALU = mybir.AluOpType
ACT = mybir.ActivationFunctionType
AX = mybir.AxisListType.X

P = 128
B, T, W = 16, 256, 192
NH, D, F = 12, 16, 64
MB = 16
NS = T // MB
BH = P // MB
NU = NS * B // BH
WB = W - P
GP, CH, EMB = 16, 3, 64
SIDES = (64, 32, 16)
DIN = tuple(CH * (64 // s) ** 2 for s in SIDES)
GROUPS = tuple(s * s // GP for s in SIDES)
E, DE = 8, 256
EC = E * DE // P
BANK = 512
NBANK = 8
EPS_INNER, EPS_LN, EPS_GATE = 1e-6, 1e-5, 1e-8
GELU_C, GELU_A, GELU_D = 0.79788456, 0.044715, 0.1070322243


def bcast(ap, axis, n):
    ap = ap.unsqueeze(axis)
    shape = list(ap.shape)
    shape[axis] = n
    return ap.broadcast_to(shape)


def rsqrt_steps(tag, scaled=False):
    return [f"{tag}eps", f"{tag}half", f"{tag}seed"] + [f"{tag}newton{k}" for k in range(10 if scaled else 9)]


def rsqrt(nc, step, own, y, a, x, var, eps, tag, scale=1.0):
    V = nc.vector
    I32 = mybir.dt.int32
    names = rsqrt_steps(tag, scale != 1.0)
    step(V.tensor_scalar(x, var, eps, None, ALU.add))
    own(names[0])
    step(V.tensor_scalar(y.bitcast(I32), x.bitcast(I32), 1, None, ALU.logical_shift_right))
    own(names[1])
    step(V.tensor_scalar(y.bitcast(I32), y.bitcast(I32), -1.0, float(0x5F3759DF), ALU.mult, ALU.add))
    own(names[2])
    for k in range(3):
        step(V.tensor_tensor(a, y, y, ALU.mult))
        own(names[3 + 3 * k])
        step(V.scalar_tensor_tensor(a, a, -0.5, x, ALU.mult, ALU.mult))
        own(names[4 + 3 * k])
        if k == 2 and scale != 1.0:
            step(V.tensor_scalar(a, a, 1.5, scale, ALU.add, ALU.mult))
            own(names[5 + 3 * k])
            step(V.tensor_tensor(y, a, y, ALU.mult))
            own(names[6 + 3 * k])
        else:
            step(V.scalar_tensor_tensor(y, a, 1.5, y, ALU.add, ALU.mult))
            own(names[5 + 3 * k])


def previous_jobs(readers):
    n = len(readers)
    out = []
    for k, r in enumerate(readers):
        j = k - NBANK
        while readers[j % n] is None:
            j -= NBANK
        out.append((j // n, j % n))
    return out


def tokenizer(nc, A, hT, LR, ident):
    NCOL = B * T
    T1, T2 = GROUPS[1], GROUPS[2]
    jobs = ["act"] * 4 + ["act"] * 4 + ["dve"] * 2 + ["dve"] + ["act"] * 8 + ["act"] * 8
    J_T1, J_T2, J_Y1, J_Y2, J_T0, J_Y0 = 0, 4, 8, 10, 11, 19
    J_H = len(jobs)
    for _ in range(NS // 2):
        jobs += ["act", "dve", "act"]
    J_LR = len(jobs)
    jobs += ["dve"]
    emptied_by = []
    n = {"act": 0, "dve": 0}
    for r in jobs:
        n[r] += 1
        emptied_by.append(n[r])

    with ExitStack() as ctx:
        sb = lambda name, shape, dt=F32: ctx.enter_context(nc.sbuf_tensor(name, shape, dt))
        sem = lambda name: ctx.enter_context(nc.semaphore(name))
        idx0 = sb("idx0_sb", [P, 2 * GP], U32)
        idx1 = sb("idx1_sb", [T1, GP], U32)
        idx2 = sb("idx2_sb", [T2, GP], U32)
        G0 = sb("G0", [P, 2 * GP * B * DIN[0]])
        G1 = sb("G1", [T1, GP * B * DIN[1]])
        G2 = sb("G2", [T2, GP * B * DIN[2]])
        K0, K1, K2 = GP * DIN[0], GP * DIN[1] // 2, 2 * DIN[2]
        X0T = sb("X0T", [K0, NCOL])
        X1T = sb("X1T", [K1, 2, B * T1])
        X2T = sb("X2T", [K2, GP // 2, B * T2])
        W0 = sb("W0_sb", [K0, EMB])
        W1 = sb("W1_sb", [K1, 2, EMB])
        W2 = sb("W2_sb", [K2, GP // 2, EMB])
        bias01 = sb("bias01", [P, 1])
        bias2 = sb("bias2", [EMB, 1])
        WfA = sb("WfA", [P, W])
        WfB = sb("WfB", [WB + 1, W])
        lrA = sb("lrA", [P, NH])
        lrB = sb("lrB", [WB + 1, NH])
        Y1 = sb("Y1", [P, B, T1 + 2])
        D1 = sb("D1", [P, B, T1 + 1])
        Y2 = sb("Y2", [EMB, B, T2 + 2])
        D2 = sb("D2", [EMB, B, T2 + 1])
        YA = sb("YA", [P, NCOL])
        YB = sb("YB", [WB + 1, NCOL])
        HA = sb("HA", [P, 2, BANK])
        HB = sb("HB", [WB + 1, 2, BANK])
        LE = sb("LE", [NH, NCOL])
        bank = [ctx.enter_context(nc.psum_tensor(f"tok_bank{i}", [P, BANK], F32)) for i in range(NBANK)]

        idx_loaded, weights_loaded = sem("tok_idx_loaded"), sem("tok_weights_loaded")
        gathered = [sem(f"gathered{i}") for i in range(3)]
        filled, act_emptied, dve_emptied = sem("tok_filled"), sem("tok_act_emptied"), sem("tok_dve_emptied")
        padded, levels_done, ones_set = sem("tok_padded"), sem("tok_levels_done"), sem("tok_ones_set")
        h_stored, lr_steps = [sem("h_stored0"), sem("h_stored1")], sem("lr_steps")
        emptied = {"act": act_emptied, "dve": dve_emptied}
        NLOAD = 16

        with nc.Block() as block:
            @block.sync
            def _(sp):
                sp.dma_start(idx1[:], A["idx1"].bitcast(U32)).then_inc(idx_loaded, 16)
                sp.dma_start(idx2[:], A["idx2"].bitcast(U32)).then_inc(idx_loaded, 16)
                sp.dma_start(idx0[:].rearrange("p (t g) -> p t g", t=2),
                             A["idx0"].bitcast(U32).rearrange("(t p) g -> p t g", t=2)).then_inc(idx_loaded, 16)
                loads = [
                    (ident[:], A["ident"]),
                    (W1[:], A["W1T"].rearrange("(j k) e -> k j e", j=2)),
                    (W2[:], A["W2T"].rearrange("(j k) e -> k j e", k=K2)),
                    (W0[:], A["W0T"]),
                    (bias01[0:EMB, :], A["b0"]), (bias01[EMB:P, :], A["b1"]), (bias2[:], A["b2"]),
                    (WfA[:], A["WfT"][0:P, :]), (WfB[0:WB, :], A["WfT"][P:W, :]), (WfB[WB:WB + 1, :], A["bf"]),
                    (lrA[:], A["lrT"][0:P, :]), (lrB[0:WB, :], A["lrT"][P:W, :]), (lrB[WB:WB + 1, :], A["lrb"]),
                ]
                for dst, src in loads:
                    sp.dma_start(dst, src).then_inc(weights_loaded, 16)
                for i in range(NS // 2):
                    sp.wait_ge(act_emptied, emptied_by[J_H + 3 * i])
                    sp.dma_start(hT[4 * i:4 * i + 4, 0:P, :].rearrange("u f k -> f u k"),
                                 HA[:, i % 2, :].rearrange("p (u k) -> p u k", u=4)).then_inc(h_stored[i % 2], 16)
                    sp.wait_ge(dve_emptied, emptied_by[J_H + 3 * i + 1])
                    sp.dma_start(hT[4 * i:4 * i + 4, P:W, :].rearrange("u f k -> f u k"),
                                 HB[0:WB, i % 2, :].rearrange("p (u k) -> p u k", u=4)).then_inc(h_stored[i % 2], 16)
                for u in range(SPARE):
                    sp.dma_start(hT[NU + u, 0:P, :], HA[:, 1, u * P:(u + 1) * P]).then_inc(h_stored[u % 2], 16)
                    sp.dma_start(hT[NU + u, P:W, :], HB[0:WB, 1, u * P:(u + 1) * P]).then_inc(h_stored[u % 2], 16)
                for k in range(2):
                    sp.wait_ge(h_stored[k], 16 * (NS // 2) + 32 * len(range(k, SPARE, 2)))

            @block.gpsimd
            def _(pool):
                nc.gpsimd.memset(YB[WB:WB + 1, :], 1.0).then_inc(ones_set, 1)
                nc.gpsimd.memset(HB[WB:WB + 1, :, :], 1.0).then_inc(ones_set, 1)
                pool.wait_ge(idx_loaded, 48)
                for g in range(GP):
                    n1, n2 = B * DIN[1], B * DIN[2]
                    nc.gpsimd.indirect_dma_start(
                        G1[:, g * n1:(g + 1) * n1], None, A["x1"],
                        bass.IndirectOffsetOnAxis(idx1[:, g:g + 1], 0)).then_inc(gathered[1], 16)
                    nc.gpsimd.indirect_dma_start(
                        G2[:, g * n2:(g + 1) * n2], None, A["x2"],
                        bass.IndirectOffsetOnAxis(idx2[:, g:g + 1], 0)).then_inc(gathered[2], 16)
                for j in range(2 * GP):
                    n0 = B * DIN[0]
                    nc.gpsimd.indirect_dma_start(
                        G0[:, j * n0:(j + 1) * n0], None, A["x0"],
                        bass.IndirectOffsetOnAxis(idx0[:, j:j + 1], 0)).then_inc(gathered[0], 16)

            @block.tensor
            def _(pe):
                def bank_free(k):
                    if k >= NBANK:
                        pe.wait_ge(emptied[jobs[k - NBANK]], emptied_by[k - NBANK])
                    return bank[k % NBANK]

                pe.wait_ge(weights_loaded, 16 * 13)
                pe.wait_ge(gathered[1], 16 * GP)
                v1 = G1[:].rearrange("t (j n b) -> t j b n", j=2, b=B)
                for k in range(4):
                    pb = bank_free(J_T1 + k)
                    for m in range(8):
                        q = nc.tensor.transpose(pb[0:K1, m * T1:(m + 1) * T1], v1[:, k // 2, 8 * (k % 2) + m],
                                                ident[0:T1, 0:T1])
                    q.then_inc(filled, 1)
                pe.wait_ge(gathered[2], 16 * GP)
                v2 = G2[:].rearrange("t (j n b) -> t j b n", j=GP // 2, b=B)
                for k in range(4):
                    pb = bank_free(J_T2 + k)
                    for m in range(2 * B):
                        q = nc.tensor.transpose(pb[0:K2, m * T2:(m + 1) * T2], v2[:, 2 * k + m // B, m % B],
                                                ident[0:T2, 0:T2])
                    q.then_inc(filled, 1)
                pe.wait_ge(act_emptied, emptied_by[J_T1 + 3])
                for k in range(2):
                    pb = bank_free(J_Y1 + k)
                    for j in range(2):
                        q = nc.tensor.matmul(pb[EMB:P, :], W1[:, j, :], X1T[:, j, k * BANK:(k + 1) * BANK],
                                             start=(j == 0), stop=(j == 1))
                    q.then_inc(filled, 1)
                pe.wait_ge(act_emptied, emptied_by[J_T2 + 3])
                pb = bank_free(J_Y2)
                for j in range(GP // 2):
                    q = nc.tensor.matmul(pb[0:EMB, 0:B * T2], W2[:, j, :], X2T[:, j, :],
                                         start=(j == 0), stop=(j == GP // 2 - 1))
                q.then_inc(filled, 1)
                pe.wait_ge(gathered[0], 16 * 2 * GP)
                v0 = G0[:].rearrange("t (j n b) -> t j b n", j=2, b=B)
                for k in range(8):
                    pb = bank_free(J_T0 + k)
                    for m in range(4):
                        q = nc.tensor.transpose(pb[0:K0, m * P:(m + 1) * P], v0[:, k % 2, 4 * (k // 2) + m], ident[:])
                    q.then_inc(filled, 1)
                for k in range(8):
                    pb = bank_free(J_Y0 + k)
                    pe.wait_ge(act_emptied, emptied_by[J_T0 + (k // 2) * 2 + 1])
                    nc.tensor.matmul(pb[0:EMB, :], W0[:], X0T[:, k * BANK:(k + 1) * BANK],
                                     start=True, stop=True).then_inc(filled, 1)
                pe.wait_ge(act_emptied, emptied_by[J_Y0 + 7])
                pe.wait_ge(levels_done, 2)
                pe.wait_ge(ones_set, 2)
                yA = YA[:].rearrange("p (b s k) -> p s b k", b=B, s=NS)
                yB = YB[:].rearrange("p (b s k) -> p s b k", b=B, s=NS)

                def rates(i):
                    pb = bank_free(J_H + 3 * i + 2)
                    pe.wait_ge(act_emptied, emptied_by[J_H + 3 * i])
                    pe.wait_ge(dve_emptied, emptied_by[J_H + 3 * i + 1])
                    nc.tensor.matmul(pb[0:NH, :], lrA[:], HA[:, i % 2, :], start=True, stop=False)
                    nc.tensor.matmul(pb[0:NH, :], lrB[:], HB[:, i % 2, :], start=False, stop=True).then_inc(filled, 1)

                for i in range(NS // 2):
                    for half, (m0, m1) in enumerate(((0, P), (P, W))):
                        pb = bank_free(J_H + 3 * i + half)
                        nc.tensor.matmul(pb[0:m1 - m0, :], WfA[:, m0:m1], yA[:, 2 * i:2 * i + 2], start=True, stop=False)
                        nc.tensor.matmul(pb[0:m1 - m0, :], WfB[:, m0:m1], yB[:, 2 * i:2 * i + 2],
                                         start=False, stop=True).then_inc(filled, 1)
                    rates(i)
                pb = bank_free(J_LR)
                pe.wait_ge(act_emptied, emptied_by[J_LR - 1])
                for u in range(NU):
                    q = nc.tensor.transpose(pb[:, u * NH:(u + 1) * NH], LE[:, u * P:(u + 1) * P], ident[0:NH, 0:NH])
                q.then_inc(filled, 1)

            @block.scalar
            def _(act):
                def job(k, out, in_, func=ACT.Copy, **kw):
                    act.wait_ge(filled, k + 1)
                    nc.scalar.activation(out, in_, func, **kw).then_inc(act_emptied, 1)

                for k in range(4):
                    job(J_T1 + k, X1T[:, k // 2, (k % 2) * BANK:(k % 2 + 1) * BANK], bank[(J_T1 + k) % NBANK][0:K1, :])
                for k in range(4):
                    job(J_T2 + k, X2T[:, 2 * k:2 * k + 2, :].rearrange("p j n -> p (j n)"),
                        bank[(J_T2 + k) % NBANK][0:K2, :])
                x0 = X0T[:].rearrange("p (b t n) -> p b t n", b=B, t=2)
                for k in range(8):
                    job(J_T0 + k, x0[:, 4 * (k // 2):4 * (k // 2) + 4, k % 2, :],
                        bank[(J_T0 + k) % NBANK][0:K0, :].rearrange("p (b n) -> p b n", b=4))
                act.wait_ge(weights_loaded, 16 * 13)
                for k in range(8):
                    job(J_Y0 + k, YA[0:EMB, k * BANK:(k + 1) * BANK], bank[(J_Y0 + k) % NBANK][0:EMB, :],
                        ACT.Identity, bias=bias01[0:EMB, 0:1])
                for i in range(NS // 2):
                    if i >= 2:
                        act.wait_ge(h_stored[i % 2], 32 * (i // 2))
                    k = J_H + 3 * i
                    job(k, HA[:, i % 2, :], bank[k % NBANK][:, :])
                    job(k + 2, LE[:, i * BANK:(i + 1) * BANK], bank[(k + 2) % NBANK][0:NH, :], ACT.Exp, scale=-1.0)

            @block.vector
            def _(dve):
                dve.wait_ge(weights_loaded, 16 * 13)
                for k in range(2):
                    dve.wait_ge(filled, J_Y1 + k + 1)
                    nc.vector.tensor_scalar(Y1[EMB:P, 8 * k:8 * k + 8, 1:T1 + 1],
                                            bank[(J_Y1 + k) % NBANK][EMB:P, :].rearrange("p (b t) -> p b t", b=8),
                                            bias01[EMB:P, 0:1], None, ALU.add).then_inc(dve_emptied, 1)
                dve.wait_ge(filled, J_Y2 + 1)
                nc.vector.tensor_scalar(Y2[:, :, 1:T2 + 1],
                                        bank[J_Y2 % NBANK][0:EMB, 0:B * T2].rearrange("p (b t) -> p b t", b=B),
                                        bias2[:, 0:1], None, ALU.add).then_inc(dve_emptied, 1)
                for Y, rows, t in ((Y1, slice(EMB, P), T1), (Y2, slice(0, EMB), T2)):
                    if t == T1:
                        dve.wait_ge(dve_emptied, 3)
                    nc.vector.tensor_copy(Y[rows, :, 0:1], Y[rows, :, 1:2]).then_inc(padded, 1)
                    nc.vector.tensor_copy(Y[rows, :, t + 1:t + 2], Y[rows, :, t:t + 1]).then_inc(padded, 1)
                dve.wait_ge(padded, 4)
                nc.vector.tensor_tensor(D1[EMB:P], Y1[EMB:P, :, 1:T1 + 2], Y1[EMB:P, :, 0:T1 + 1],
                                        ALU.subtract).then_inc(padded, 1)
                nc.vector.tensor_tensor(D2[:], Y2[:, :, 1:T2 + 2], Y2[:, :, 0:T2 + 1], ALU.subtract).then_inc(padded, 1)
                dve.wait_ge(padded, 6)
                for Y, Df, rows, t, out in ((Y1, D1, slice(EMB, P), T1, YA), (Y2, D2, slice(0, EMB), T2, YB)):
                    R = T // t
                    o = out[rows, :].rearrange("p (b k r) -> p b k r", b=B, r=R)
                    for r in range(R):
                        w = (r + 0.5) / R - 0.5
                        first = 0 if w < 0 else 1
                        w = w + 1.0 if w < 0 else w
                        q = nc.vector.scalar_tensor_tensor(o[:, :, :, r], Df[rows, :, first:first + t], w,
                                                           Y[rows, :, first:first + t], ALU.mult, ALU.add)
                    q.then_inc(levels_done, 1)
                for i in range(NS // 2):
                    k = J_H + 3 * i + 1
                    if i >= 2:
                        dve.wait_ge(h_stored[i % 2], 32 * (i // 2))
                    dve.wait_ge(filled, k + 1)
                    nc.vector.tensor_copy(HB[0:WB, i % 2, :], bank[k % NBANK][0:WB, :]).then_inc(dve_emptied, 1)
                dve.wait_ge(filled, J_LR + 1)
                nc.vector.tensor_scalar(LR[:], bank[J_LR % NBANK][:, 0:NU * NH], float(D), float(D),
                                        ALU.mult, ALU.add).then_inc(lr_steps, 1)
                dve.wait_ge(lr_steps, 1)
                nc.vector.reciprocal(LR[:], LR[:]).then_inc(lr_steps, 1)
                dve.wait_ge(lr_steps, 2)


SPARE = 3
JOBS = [("attn", 4, "dve"), ("z2", 4, "dve"), ("kqT", 6, "act"), ("z2b", 4, "act"), ("w2", 2, "dve"), ("m1", 3, "dve"),
        ("w2T", 2, "act"), ("gT", 3, "act"), ("proj", 2, "act"), ("gx", 2, "dve"), ("z1", 2, "dve"),
        ("z1b", 2, "dve"), ("w1", 2, "dve"), ("xT", 2, "act"), ("xbT", 2, "act"), ("b1", 2, "dve")]
SLOTS = [f"{n}{i}" for n, k, _ in JOBS for i in range(k)]
READER = {f"{n}{i}": r for n, k, r in JOBS for i in range(k)}
NJ = len(SLOTS)
PADDED = SLOTS + [None] * (-NJ % 4)
NP = len(PADDED)
SLOT_OF = {s: i for i, s in enumerate(PADDED) if s}
PREV = previous_jobs([READER[s] if s else None for s in PADDED])
ACT_STEPS = ([f"kqT{i}" for i in range(6)] + ["z2b0", "z2b1", "z2b2", "z2b3"]
             + ["w2T0", "w2T1", "gT0", "gT1", "gT2", "proj0", "proj1", "sq", "tanh", "gelu_b", "xT0", "xT1", "xbT0", "xbT1"])
DVE_STEPS = (["attn0", "attn1", "da", "attn2", "attn3"]
             + ["z20", "z21", "z22", "z23", "z2_fold", "z2_bias", "mean", "center", "square", "var"] + rsqrt_steps("r_")
             + ["xhat", "gxh0", "gxh", "s1", "gx_xh", "s2", "lr_rstd", "w20", "w21", "b2", "s2_xh", "sub1", "sub2", "g2", "g2_bd"]
             + ["m10", "m11", "m12", "db", "dc", "dgelu", "gx0", "gx1", "z10", "z11", "cube", "arg"]
             + ["z1b0", "z1b1", "x2", "w10", "w11", "b10", "b11"])
POOL_STEPS = ["k_bd", "q_bd", "t0", "t1", "t2", "b2_copy", "zb_mask", "zb_half", "zb_quarter", "zb_fold", "out"]
DVE_OF = {"w21": "b2"}


def count_of(engine, job):
    if engine == "act":
        return ACT_STEPS.index(job) + 1
    return DVE_STEPS.index(DVE_OF.get(job, job)) + 1


def scan(nc, A, hT, attn, q_dram, LR, ident):
    with ExitStack() as ctx:
        sb = lambda name, shape: ctx.enter_context(nc.sbuf_tensor(name, shape, F32))
        two = lambda name, shape: [sb(f"{name}_{i}", shape) for i in range(2)]
        sem = lambda name: ctx.enter_context(nc.semaphore(name))
        HD, HF, HP = NH * D, NH * F, NH * P
        block_mask = sb("block_mask", [P, P])
        neg_tril = sb("neg_tril", [P, P])
        neg_last = sb("neg_last", [P, P])
        tok = sb("tok", [P, MB])
        half_last = sb("half_last", [P, 2])
        recip = sb("recip", [P, MB])
        lnw, lnb, lnw2 = sb("lnw", [P, HD]), sb("lnb", [P, HD]), sb("lnw2", [P, HD])
        WqkvA, WqkvB = sb("WqkvA", [P, 3 * W]), sb("WqkvB", [WB, 3 * W])
        w2_small = sb("w2_small", [P, NH // 2, D])
        W1s = two("W1s", [P, HF])
        b1s = two("b1s", [P, HF])
        W2s = two("W2s", [P, HP // 2])
        W2T = two("W2T", [P, HF])
        b2s = two("b2s", [P, HD])
        hA, hB = two("hA", [P, P]), two("hB", [WB, P])
        QKV = sb("QKV", [P, 3 * W])
        K_bd, Q_bd = two("K_bd", [P, HP]), sb("Q_bd", [P, HP])
        KT, QT = sb("KT", [P, HP]), two("QT", [P, HP])
        M1T, M2T = two("M1T", [P, HP]), sb("M2T", [P, HP])
        target, tt = two("target", [P, HD]), sb("tt", [P, HD])
        x, x_sq, arg, th = sb("x", [P, HF]), sb("x_sq", [P, HF]), sb("arg", [P, HF]), sb("th", [P, HF])
        tmp, dg = sb("tmp", [P, HF]), sb("dg", [P, HF])
        X2 = two("X2", [P, HF])
        X2T, XbT = two("X2Tr", [P, HF]), sb("XbT", [P, HF])
        xb, X2b = sb("xb", [P, HF]), sb("X2b", [P, HF])
        Zm, Zb, b2_copy = sb("Zm", [P, HP]), sb("Zb", [P, HP]), sb("b2_copy", [P, HD])
        z, zc, zs, xh, g = sb("z", [P, HD]), sb("zc", [P, HD]), sb("zs", [P, HD]), sb("xh", [P, HD]), sb("g", [P, HD])
        st = sb("st", [P, 8, NH])
        G2, G2bd, GT = two("G2v", [P, HD]), two("G2bd", [P, HP]), sb("GT", [P, HP])
        G1 = sb("G1v", [P, HF])
        out = two("scan_out", [P, HD])
        bank = [ctx.enter_context(nc.psum_tensor(f"scan_bank{i}", [P, BANK], F32)) for i in range(NBANK)]

        consts_loaded, consts_made, state_made = sem("consts_loaded"), sem("consts_made"), sem("state_made")
        pe_filled, act_done, dve_done, pool_done = sem("pe_filled"), sem("act_done"), sem("dve_done"), sem("pool_done")
        h_loaded = [sem("h_loaded0"), sem("h_loaded1")]
        out_stored = [sem("out_stored0"), sem("out_stored1")]
        q_stored, first_projected, first_copied = sem("q_stored"), sem("first_projected"), sem("first_copied")
        done = {"act": act_done, "dve": dve_done}
        per = {"act": len(ACT_STEPS), "dve": len(DVE_STEPS), "pool": len(POOL_STEPS), "pe": NJ}

        class Step:
            def __init__(self, i, c):
                self.i, self.c = i, c
                self.n, self.u, self.p = c % 2, (c - 1) % 2, c % 2

            def at(self, each, k, back=0):
                const = each * (self.c - back) + k
                return const if isinstance(self.i, int) else self.i * (2 * each) + const

        def bank_of(s, job):
            return bank[(s.c * NP + SLOT_OF[job]) % NBANK]

        def act_at(s, name, back=0):
            return s.at(per["act"], ACT_STEPS.index(name) + 1, back)

        def dve_at(s, name, back=0):
            return s.at(per["dve"], DVE_STEPS.index(name) + 1, back)

        def pool_at(s, name, back=0):
            return s.at(per["pool"], POOL_STEPS.index(name) + 1, back)

        def pe_at(s, job, back=0):
            return s.at(NJ, SLOTS.index(job) + 1, back)

        def steps(eng, first, body, last, sign_off=None):
            first(Step(0, 0))
            with eng.Fori(0, NU // 2) as i:
                body(Step(i, 1))
                body(Step(i, 2))
            last(Step(0, NU + 1))

        head = lambda ap, h, n: ap[:, h * n:(h + 1) * n]
        SPLIT = [(0, 2, 4, 6), (1, 3, 5, 7), (8, 10), (9, 11)]
        PLACE = {h: n for n, h in enumerate(h for hs in SPLIT for h in hs)}
        rows_of = lambda h: slice(F * (h % 2), F * (h % 2) + F)
        heads4 = lambda ap: ap.rearrange("p (h n) -> p h n", n=P)

        def split_view(ap, k):
            part = ap[:, 0:8 * P] if k < 2 else ap[:, 8 * P:]
            return part.rearrange("p (h two n) -> p two h n", two=2, n=P)[:, k % 2]

        def split_bank(pb, k):
            return pb[:, 0:len(SPLIT[k]) * P].rearrange("p (h n) -> p h n", n=P)

        def split_mask(m, k):
            return bcast(m[:, :], 1, len(SPLIT[k]))

        with nc.Block() as block:
            @block.sync
            def _(sp):
                w2v = A["W2"].rearrange("(q two) f d -> two f q d", two=2)
                loads = [(block_mask[:], A["block_mask"]), (neg_tril[:], A["triu_mask"]), (recip[:], A["recip"]),
                         (tok[:], A["learn"].broadcast_to([P, MB])),
                         (lnw[:], A["lnw"].broadcast_to([P, HD])), (lnb[:], A["lnb"].broadcast_to([P, HD])),
                         (b1s[0][:], A["ab1"].broadcast_to([P, HF])), (b1s[1][:], A["ab1"].broadcast_to([P, HF])),
                         (b2s[0][:], A["ab2"].broadcast_to([P, HD])), (b2s[1][:], A["ab2"].broadcast_to([P, HD])),
                         (WqkvA[:], A["Wqkv"][0:P, :]), (WqkvB[:], A["Wqkv"][P:W, :]),
                         (w2_small[0:F], w2v[0]), (w2_small[F:P], w2v[1])]
                for k in range(2):
                    for b in range(BH):
                        loads.append((W1s[k][b * D:(b + 1) * D, :].rearrange("p (h f) -> p h f", f=F),
                                      A["W1"].rearrange("h d f -> d h f")))
                assert len(loads) == 14 + 2 * BH
                for dst, src in loads:
                    sp.dma_start(dst, src).then_inc(consts_loaded, 16)

                def load_h(row, par):
                    sp.dma_start(hA[par][:], hT[row, 0:P, :].rearrange("u f k -> (u f) k")).then_inc(h_loaded[par], 16)
                    sp.dma_start(hB[par][:], hT[row, P:W, :].rearrange("u f k -> (u f) k")).then_inc(h_loaded[par], 16)

                def store_q(row):
                    sp.dma_start(q_dram[row, :, :].rearrange("u p k -> (u p) k"), QKV[:, 0:W]).then_inc(q_stored, 16)

                def first(s):
                    for par in range(2):
                        sp.sem_inc(out_stored[par], 16)
                    load_h(slice(0, 1), 0)
                    load_h(slice(1, 2), 1)
                    sp.wait_ge(first_projected, 2)
                    load_h(slice(2, 3), 0)
                    sp.wait_ge(first_copied, 3)
                    store_q(slice(0, 1))
                    sp.wait_ge(act_done, act_at(s, "proj1"))
                    store_q(slice(1, 2))

                def body(s):
                    sp.wait_ge(pe_filled, pe_at(s, "proj1", 1))
                    load_h(bass.ds(s.i * 2 + (s.c + 2), 1), s.n)
                    sp.wait_ge(act_done, act_at(s, "proj1"))
                    store_q(bass.ds(s.i * 2 + (s.c + 1), 1))
                    sp.wait_ge(pool_done, pool_at(s, "out"))
                    sp.dma_start(attn[bass.ds(s.i * 2 + (s.c - 1), 1), :, :].rearrange("u p k -> (u p) k"),
                                 out[s.p][:]).then_inc(out_stored[s.p], 16)

                def last(s):
                    sp.wait_ge(pool_done, pool_at(s, "out"))
                    sp.dma_start(attn[NU, :, :], out[s.p][:]).then_inc(out_stored[s.p], 16)
                    sp.wait_ge(q_stored, 16 * (NU + 2))
                    sp.wait_ge(out_stored[0], 16 * (NU // 2 + 1))
                    sp.wait_ge(out_stored[1], 16 * (NU // 2 + 2))
                    for par in range(2):
                        sp.wait_ge(h_loaded[par], 32 * len(range(par, NU + SPARE, 2)))

                steps(sp, first, body, last)

            @block.tensor
            def _(pe):
                def free(s, job):
                    step, slot = PREV[SLOT_OF[job]]
                    prev = PADDED[slot]
                    r = READER[prev]
                    if not (isinstance(s.i, int) and s.c + step < 0):
                        pe.wait_ge(done[r], s.at(per[r], count_of(r, prev), -step))
                    return bank_of(s, job)

                def projection(pb, k, par):
                    c = slice(k * 288, (k + 1) * 288)
                    nc.tensor.matmul(pb[:, 0:288], hA[par][:], WqkvA[:, c], start=True, stop=False)
                    return nc.tensor.matmul(pb[:, 0:288], hB[par][:], WqkvB[:, c], start=False, stop=True)

                def proj(s):
                    pe.wait_ge(h_loaded[1 - s.n], s.i * 32 + 32 * ((s.c + 1) // 2 + 1))
                    for k in range(2):
                        projection(free(s, f"proj{k}"), k, 1 - s.n).then_inc(pe_filled, 1)

                def transposes(s, job, k, src, blocks):
                    pb = free(s, f"{job}{k}")
                    for m, h in enumerate(blocks):
                        q = nc.tensor.transpose(head(pb, m, P), head(src, h, P), ident[:])
                    q.then_inc(pe_filled, 1)

                def kq(s):
                    pe.wait_ge(pool_done, pool_at(s, "k_bd"))
                    for k in range(3):
                        transposes(s, "kqT", k, K_bd[s.n], range(4 * k, 4 * k + 4))
                    pe.wait_ge(pool_done, pool_at(s, "q_bd"))
                    for k in range(3):
                        transposes(s, "kqT", 3 + k, Q_bd, range(4 * k, 4 * k + 4))

                def w2T(s):
                    transposes(s, "w2T", 0, W2s[s.p], range(4))
                    transposes(s, "w2T", 1, W2s[s.p], range(4, 6))

                def m1(s):
                    pe.wait_ge(act_done, act_at(s, "kqT5"))
                    for k in range(3):
                        pb = free(s, f"m1{k}")
                        for m in range(4):
                            h = 4 * k + m
                            q = nc.tensor.matmul(head(pb, m, P), head(KT, h, P), head(QT[s.n], h, P), start=True, stop=True)
                        q.then_inc(pe_filled, 1)

                def z1(s):
                    if not (isinstance(s.i, int) and s.c == 0):
                        pe.wait_ge(dve_done, dve_at(s, "w11", 1))
                    by64(s, "z1", lambda o, h: nc.tensor.matmul(o, head(KT, h, P), head(W1s[s.n], h, F), start=True, stop=True))

                def by64(s, job, product):
                    for k, hs in enumerate((range(8), range(8, 12))):
                        pb = free(s, f"{job}{k}")
                        for m, h in enumerate(hs):
                            q = product(head(pb, m, F), h)
                        q.then_inc(pe_filled, 1)

                def xT(s):
                    pe.wait_ge(dve_done, dve_at(s, "x2"))
                    transposes(s, "xT", 0, X2[s.n], range(4))
                    transposes(s, "xT", 1, X2[s.n], range(4, 6))

                def xbT(s):
                    transposes(s, "xbT", 0, X2b, range(4))
                    transposes(s, "xbT", 1, X2b, range(4, 6))

                def split_jobs(s, job, product):
                    for k in range(4):
                        pb = free(s, f"{job}{k}")
                        for m, h in enumerate(SPLIT[k]):
                            q = product(head(pb, m, P), h)
                        q.then_inc(pe_filled, 1)

                def attn2(s):
                    pe.wait_ge(act_done, act_at(s, "xbT1", 1))
                    split_jobs(s, "attn", lambda o, h: nc.tensor.matmul(
                        o, head(X2T[s.p][rows_of(h)], h // 2, P), head(XbT[rows_of(h)], h // 2, P), start=True, stop=True))

                def z2b(s):
                    pe.wait_ge(dve_done, dve_at(s, "attn3"))

                    def product(o, h):
                        nc.tensor.matmul(o, head(XbT[rows_of(h)], h // 2, P), head(W2s[s.p][rows_of(h)], h // 2, P),
                                         start=True, stop=False)
                        return nc.tensor.matmul(o, head(M2T, PLACE[h], P), head(G2bd[s.p], h, P), start=False, stop=True)
                    split_jobs(s, "z2b", product)

                def w2(s):
                    for k, qs in enumerate((range(4), range(4, 6))):
                        pb = free(s, f"w2{k}")
                        for m, q2 in enumerate(qs):
                            for par in range(2):
                                h = 2 * q2 + par
                                q = nc.tensor.matmul(pb[rows_of(par), m * P:(m + 1) * P], head(X2[s.p], h, F),
                                                     head(G2bd[s.p], h, P), start=True, stop=True)
                        if k == 1:
                            q = nc.tensor.matmul(pb[:, 2 * P:2 * P + HD], neg_last[:], G2[s.p][:], start=True, stop=True)
                        q.then_inc(pe_filled, 1)

                def skip(s, a, b=None):
                    pe.wait_ge(pe_filled, s.at(NJ, SLOTS.index(a)))
                    pe.sem_inc(pe_filled, (SLOTS.index(b) if b else NJ) - SLOTS.index(a))

                def first(s):
                    skip(s, "attn0", "kqT0")
                    kq(s)
                    skip(s, "z2b0", "m10")
                    m1(s)
                    w2T(s)
                    skip(s, "gT0", "proj0")
                    proj(s)
                    skip(s, "gx0", "z10")
                    z1(s)
                    skip(s, "z1b0", "xT0")
                    xT(s)
                    xbT(s)
                    skip(s, "b10")

                def body(s):
                    attn2(s)
                    split_jobs(s, "z2", lambda o, h: nc.tensor.matmul(
                        o, head(X2T[s.u][rows_of(h)], h // 2, P), head(W2s[s.u][rows_of(h)], h // 2, P), start=True, stop=True))
                    kq(s)
                    z2b(s)
                    w2(s)
                    m1(s)
                    pe.wait_ge(dve_done, dve_at(s, "w21"))
                    w2T(s)
                    pe.wait_ge(dve_done, dve_at(s, "g2_bd"))
                    for k in range(3):
                        transposes(s, "gT", k, G2bd[s.u], range(4 * k, 4 * k + 4))
                    proj(s)
                    pe.wait_ge(act_done, act_at(s, "gT2"))
                    by64(s, "gx", lambda o, h: nc.tensor.matmul(o, head(GT, h, P), head(W2T[s.u], h, F), start=True, stop=True))
                    z1(s)
                    pe.wait_ge(dve_done, dve_at(s, "gx1"))

                    def product(o, h):
                        nc.tensor.matmul(o, head(QT[s.u], h, P), head(W1s[s.u], h, F), start=True, stop=False)
                        return nc.tensor.matmul(o, head(M1T[s.u], h, P), head(G1, h, F), start=False, stop=True)
                    by64(s, "z1b", product)
                    by64(s, "w1", lambda o, h: nc.tensor.matmul(o, head(K_bd[s.u], h, P), head(G1, h, F), start=True, stop=True))
                    xT(s)
                    pe.wait_ge(act_done, act_at(s, "gelu_b"))
                    xbT(s)
                    for k, c in enumerate((slice(0, BANK), slice(BANK, HF))):
                        pb = free(s, f"b1{k}")
                        nc.tensor.matmul(pb[:, 0:c.stop - c.start], neg_last[:], G1[:, c],
                                         start=True, stop=True).then_inc(pe_filled, 1)

                def last(s):
                    attn2(s)
                    skip(s, "z20", "z2b0")
                    z2b(s)

                pe.wait_ge(consts_loaded, 16 * (14 + 2 * BH))
                pe.wait_ge(consts_made, 5)
                pe.wait_ge(state_made, 9)
                pe.wait_ge(h_loaded[0], 32)
                for k in range(2):
                    projection(bank[k], k, 0).then_inc(first_projected, 1)
                pe.wait_ge(first_copied, 3)
                steps(pe, first, body, last)

            @block.scalar
            def _(act):
                def skip(s, a, b=None):
                    act.wait_ge(act_done, s.at(per["act"], ACT_STEPS.index(a)))
                    act.sem_inc(act_done, (ACT_STEPS.index(b) if b else len(ACT_STEPS)) - ACT_STEPS.index(a))

                def evac(s, job, dst, width=BANK, **kw):
                    act.wait_ge(pe_filled, pe_at(s, job))
                    nc.scalar.activation(dst, bank_of(s, job)[:, 0:width], ACT.Copy, **kw).then_inc(act_done, 1)

                def proj(s):
                    act.wait_ge(pool_done, pool_at(s, "t2"))
                    act.wait_ge(q_stored, s.at(16, 16))
                    for k in range(2):
                        evac(s, f"proj{k}", QKV[:, k * 288:(k + 1) * 288], 288)

                def kq(s):
                    for k in range(3):
                        evac(s, f"kqT{k}", KT[:, k * BANK:(k + 1) * BANK])
                    for k in range(3):
                        evac(s, f"kqT{3 + k}", QT[s.n][:, k * BANK:(k + 1) * BANK])

                def wide(s, job, dst, **kw):
                    evac(s, f"{job}0", dst[:, 0:BANK], **kw)
                    evac(s, f"{job}1", dst[:, BANK:HF], HF - BANK, **kw)

                def first_layer(s):
                    proj(s)
                    act.wait_ge(dve_done, dve_at(s, "z11"))
                    nc.scalar.activation(x_sq[:], x[:], ACT.Square).then_inc(act_done, 1)
                    act.wait_ge(dve_done, dve_at(s, "arg"))
                    nc.scalar.activation(th[:], arg[:], ACT.Tanh, scale=GELU_C).then_inc(act_done, 1)

                def z2b(s):
                    if not (isinstance(s.i, int) and s.c == 1):
                        act.wait_ge(pool_done, pool_at(s, "zb_fold", 1))
                    for k in range(4):
                        act.wait_ge(pe_filled, pe_at(s, f"z2b{k}"))
                        nc.scalar.activation(split_view(Zb[:], k), split_bank(bank_of(s, f"z2b{k}"), k),
                                             ACT.Copy).then_inc(act_done, 1)

                def first(s):
                    kq(s)
                    skip(s, "z2b0", "w2T0")
                    wide(s, "w2T", W2T[s.p])
                    skip(s, "gT0", "proj0")
                    first_layer(s)
                    skip(s, "gelu_b", "xT0")
                    wide(s, "xT", X2T[s.n], scale=0.5)
                    wide(s, "xbT", XbT)

                def body(s):
                    kq(s)
                    z2b(s)
                    wide(s, "w2T", W2T[s.p])
                    for k in range(3):
                        evac(s, f"gT{k}", GT[:, k * BANK:(k + 1) * BANK])
                    first_layer(s)
                    act.wait_ge(dve_done, dve_at(s, "z1b1"))
                    nc.scalar.activation(X2b[:], xb[:], ACT.Gelu_apprx_tanh).then_inc(act_done, 1)
                    wide(s, "xT", X2T[s.n], scale=0.5)
                    wide(s, "xbT", XbT)

                def last(s):
                    skip(s, "kqT0", "z2b0")
                    z2b(s)

                act.wait_ge(state_made, 9)
                nc.scalar.activation(X2b[:], xb[:], ACT.Gelu_apprx_tanh).then_inc(first_copied, 1)
                for k in range(2):
                    act.wait_ge(first_projected, k + 1)
                    nc.scalar.activation(QKV[:, k * 288:(k + 1) * 288], bank[k][:, 0:288], ACT.Copy).then_inc(first_copied, 1)
                steps(act, first, body, last)

            @block.gpsimd
            def _(pool):
                TT = nc.gpsimd.tensor_tensor

                def skip(s, a, b=None):
                    pool.wait_ge(pool_done, s.at(per["pool"], POOL_STEPS.index(a)))
                    pool.sem_inc(pool_done, (POOL_STEPS.index(b) if b else len(POOL_STEPS)) - POOL_STEPS.index(a))

                def step(ins):
                    ins.then_inc(pool_done, 1)

                def masked(dst, src):
                    step(TT(dst[:].rearrange("p (h b d) -> p h b d", h=NH, b=BH),
                            bcast(src.rearrange("p (h d) -> p h d", h=NH), 2, BH),
                            bcast(block_mask[:].rearrange("p (b d) -> p b d", b=BH), 1, NH), ALU.mult))

                def inputs(s):
                    Q, K, V = (QKV[:, k * W:(k + 1) * W] for k in range(3))
                    masked(K_bd[s.n], K)
                    masked(Q_bd, Q)
                    step(TT(tt[:], K, V, ALU.subtract))
                    pool.wait_ge(pool_done, pool_at(s, "t0"))
                    step(TT(tt[:], tt[:], lnb[:], ALU.add))
                    pool.wait_ge(pool_done, pool_at(s, "t1"))
                    step(TT(target[s.n][:], tt[:], lnw[:], ALU.mult))

                def output(s):
                    pool.wait_ge(act_done, act_at(s, "z2b3"))
                    step(TT(Zb[:].rearrange("p (h n) -> p h n", n=P), Zb[:].rearrange("p (h n) -> p h n", n=P),
                            bcast(block_mask[:, :], 1, NH), ALU.mult))
                    by_image = Zb[:].rearrange("p (h b d) -> p h b d", h=NH, b=BH)
                    n = BH
                    for name in ("zb_mask", "zb_half", "zb_quarter"):
                        pool.wait_ge(pool_done, pool_at(s, name))
                        n //= 2
                        if n > 1:
                            step(TT(by_image[:, :, 0:n], by_image[:, :, 0:n], by_image[:, :, n:2 * n], ALU.add))
                        else:
                            step(TT(out[s.p][:].rearrange("p (h d) -> p h d", h=NH), by_image[:, :, 0], by_image[:, :, 1],
                                    ALU.add))
                    pool.wait_ge(pool_done, pool_at(s, "zb_fold"))
                    step(TT(out[s.p][:], out[s.p][:], b2_copy[:], ALU.add))

                def first(s):
                    pool.wait_ge(first_copied, 3)
                    inputs(s)
                    skip(s, "b2_copy")

                def body(s):
                    pool.wait_ge(act_done, act_at(s, "proj1", 1))
                    pool.wait_ge(pe_filled, pe_at(s, "w11", 1))
                    inputs(s)
                    step(nc.gpsimd.tensor_copy(b2_copy[:], b2s[s.p][:]))
                    pool.wait_ge(out_stored[s.p], s.i * 16 + 16)
                    output(s)

                def last(s):
                    skip(s, "k_bd", "b2_copy")
                    step(nc.gpsimd.tensor_copy(b2_copy[:], b2s[s.p][:]))
                    pool.wait_ge(out_stored[s.p], 16 * (NU // 2 + 1))
                    output(s)

                pool.wait_ge(consts_loaded, 16 * (14 + 2 * BH))
                steps(pool, first, body, last)

            @block.vector
            def _(dve):
                def skip(s, a, b=None):
                    dve.wait_ge(dve_done, s.at(per["dve"], DVE_STEPS.index(a)))
                    dve.sem_inc(dve_done, (DVE_STEPS.index(b) if b else len(DVE_STEPS)) - DVE_STEPS.index(a))

                def own(s, name):
                    dve.wait_ge(dve_done, dve_at(s, name))

                def step(ins):
                    ins.then_inc(dve_done, 1)

                V = nc.vector
                by_head = lambda ap: ap.rearrange("p (h d) -> p h d", h=NH)
                stat = lambda k: bcast(st[:, k, :], 2, D)

                def halves(s, job, emit):
                    for k, c in enumerate((slice(0, BANK), slice(BANK, HF))):
                        dve.wait_ge(pe_filled, pe_at(s, f"{job}{k}"))
                        step(emit(c, bank_of(s, f"{job}{k}")[:, 0:c.stop - c.start]))

                def attention(s, banks):
                    for k in banks:
                        dve.wait_ge(pe_filled, pe_at(s, f"attn{k}"))
                        n0 = PLACE[SPLIT[k][0]] * P
                        step(V.scalar_tensor_tensor(heads4(M2T[:, n0:n0 + len(SPLIT[k]) * P]),
                                                    split_bank(bank_of(s, f"attn{k}"), k), 1.0,
                                                    split_mask(neg_tril, k), ALU.add, ALU.mult))

                def diagonal(s, job, fold, dst, b2):
                    for k in range(4):
                        dve.wait_ge(pe_filled, pe_at(s, f"{job}{k}"))
                        step(V.tensor_tensor(split_view(Zm[:], k), split_bank(bank_of(s, f"{job}{k}"), k),
                                             split_mask(block_mask, k), ALU.mult))
                    own(s, f"{job}3")
                    step(V.tensor_reduce(z[:], Zm[:].rearrange("p (h b d) -> p h d b", h=NH, b=BH), AX, ALU.add))
                    own(s, fold)
                    step(V.tensor_tensor(dst, z[:], b2[:], ALU.add))

                def first(s):
                    skip(s, "attn0", "m10")
                    m1(s)
                    skip(s, "db", "z10")
                    first_layer(s)
                    skip(s, "z1b0", "x2")
                    x2(s)
                    skip(s, "w10")

                def m1(s):
                    for k in range(3):
                        dve.wait_ge(pe_filled, pe_at(s, f"m1{k}"))
                        step(V.scalar_tensor_tensor(heads4(M1T[s.n][:, k * BANK:(k + 1) * BANK]),
                                                    heads4(bank_of(s, f"m1{k}")[:, :]), 1.0,
                                                    bcast(neg_tril[:, :], 1, 4), ALU.add, ALU.mult))

                def first_layer(s):
                    halves(s, "z1", lambda c, pb: V.tensor_tensor(x[:, c], pb, b1s[s.n][:, c], ALU.add))
                    dve.wait_ge(act_done, act_at(s, "sq"))
                    step(V.tensor_scalar(tmp[:], x_sq[:], GELU_A, 1.0, ALU.mult, ALU.add))
                    own(s, "cube")
                    step(V.tensor_tensor(arg[:], tmp[:], x[:], ALU.mult))

                def x2(s):
                    dve.wait_ge(act_done, act_at(s, "tanh"))
                    step(V.scalar_tensor_tensor(X2[s.n][:], th[:], 1.0, x[:], ALU.add, ALU.mult))

                def body(s):
                    attention(s, (0, 1))
                    step(V.tensor_scalar(tmp[:], x_sq[:], GELU_D, GELU_C, ALU.mult, ALU.add))
                    attention(s, (2, 3))
                    diagonal(s, "z2", "z2_fold", z[:], b2s[s.u])
                    own(s, "z2_bias")
                    step(V.tensor_reduce(st[:, 0, :], by_head(z[:]), AX, ALU.add))
                    own(s, "mean")
                    step(V.scalar_tensor_tensor(by_head(zc[:]), stat(0), -1.0 / D, by_head(z[:]), ALU.mult, ALU.add))
                    own(s, "center")
                    step(V.tensor_tensor(zs[:], zc[:], zc[:], ALU.mult))
                    own(s, "square")
                    step(V.tensor_reduce(st[:, 1, :], by_head(zs[:]), AX, ALU.add))
                    own(s, "var")
                    rsqrt(nc, step, lambda name: own(s, name), st[:, 2, :], st[:, 6, :], st[:, 7, :], st[:, 1, :],
                          D * EPS_INNER, "r_")
                    step(V.scalar_tensor_tensor(by_head(xh[:]), by_head(zc[:]), float(D) ** 0.5, stat(2), ALU.mult, ALU.mult))
                    own(s, "xhat")
                    step(V.tensor_tensor(zs[:], xh[:], lnw2[:], ALU.mult))
                    own(s, "gxh0")
                    dve.wait_ge(pool_done, pool_at(s, "t2", 1))
                    step(V.tensor_tensor(g[:], zs[:], target[s.u][:], ALU.add))
                    own(s, "gxh")
                    step(V.tensor_reduce(st[:, 3, :], by_head(g[:]), AX, ALU.add))
                    step(V.tensor_tensor(zs[:], g[:], xh[:], ALU.mult))
                    own(s, "gx_xh")
                    step(V.tensor_reduce(st[:, 4, :], by_head(zs[:]), AX, ALU.add))
                    unit = s.i * (2 * NH) + (s.c - 1) * NH
                    step(V.scalar_tensor_tensor(st[:, 5, :], st[:, 2, :], float(D) ** 0.5, LR[:, bass.ds(unit, NH)],
                                                ALU.mult, ALU.mult))
                    halves(s, "w2", lambda c, pb: V.scalar_tensor_tensor(
                        W2s[s.p][:, c], pb, half_last[:, 0:1], W2s[s.p][:, c], ALU.mult, ALU.add))
                    dve.wait_ge(pool_done, pool_at(s, "b2_copy"))
                    step(V.tensor_tensor(b2s[s.p][:], bank_of(s, "w21")[:, 2 * P:2 * P + HD], b2s[s.p][:], ALU.add))
                    own(s, "lr_rstd")
                    step(V.tensor_tensor(by_head(zc[:]), by_head(xh[:]), stat(4), ALU.mult))
                    step(V.scalar_tensor_tensor(by_head(g[:]), stat(3), -1.0 / D, by_head(g[:]), ALU.mult, ALU.add))
                    own(s, "sub1")
                    step(V.scalar_tensor_tensor(g[:], zc[:], -1.0 / D, g[:], ALU.mult, ALU.add))
                    own(s, "sub2")
                    step(V.tensor_tensor(by_head(G2[s.u][:]), by_head(g[:]), stat(5), ALU.mult))
                    own(s, "g2")
                    step(V.tensor_tensor(G2bd[s.u][:].rearrange("p (h b d) -> p h b d", h=NH, b=BH),
                                         bcast(by_head(G2[s.u][:]), 2, BH),
                                         bcast(block_mask[:].rearrange("p (b d) -> p b d", b=BH), 1, NH), ALU.mult))
                    m1(s)
                    step(V.scalar_tensor_tensor(tmp[:], th[:], 1.0, tmp[:], ALU.subtract, ALU.mult))
                    own(s, "db")
                    step(V.tensor_tensor(tmp[:], tmp[:], X2[s.u][:], ALU.mult))
                    own(s, "dc")
                    step(V.scalar_tensor_tensor(dg[:], th[:], 1.0, tmp[:], ALU.add, ALU.subtract))
                    own(s, "dgelu")
                    halves(s, "gx", lambda c, pb: V.scalar_tensor_tensor(G1[:, c], pb, 0.5, dg[:, c], ALU.mult, ALU.mult))
                    first_layer(s)
                    dve.wait_ge(act_done, act_at(s, "gelu_b", 1))
                    halves(s, "z1b", lambda c, pb: V.tensor_tensor(xb[:, c], pb, b1s[s.u][:, c], ALU.add))
                    x2(s)
                    halves(s, "w1", lambda c, pb: V.scalar_tensor_tensor(
                        W1s[s.u][:, c], pb, half_last[:, 1:2], W1s[s.u][:, c], ALU.mult, ALU.add))
                    halves(s, "b1", lambda c, pb: V.tensor_tensor(b1s[s.u][:, c], pb, b1s[s.u][:, c], ALU.add))

                def last(s):
                    attention(s, (0, 1))
                    skip(s, "da", "attn2")
                    attention(s, (2, 3))
                    skip(s, "z20")

                dve.wait_ge(consts_loaded, 16 * (14 + 2 * BH))
                made = [0]

                def make(ins, wait=True):
                    ins.then_inc(consts_made, 1)
                    made[0] += 1
                    if wait:
                        dve.wait_ge(consts_made, made[0])
                make(V.tensor_tensor(tok[:], tok[:], recip[:], ALU.add))
                make(V.tensor_scalar(tok[:], tok[:], 0.0, None, ALU.max))
                make(V.scalar_tensor_tensor(neg_tril[:].rearrange("p (b k) -> p b k", b=BH),
                                            neg_tril[:].rearrange("p (b k) -> p b k", b=BH), -1.0,
                                            bcast(tok[:, :], 1, BH), ALU.mult, ALU.mult))
                make(V.tensor_scalar(half_last[:, 0:1], tok[:, MB - 1:MB], -0.5, None, ALU.mult))
                make(V.tensor_scalar(half_last[:, 1:2], tok[:, MB - 1:MB], -1.0, None, ALU.mult))
                V.tensor_scalar(neg_last[:], block_mask[:], half_last[:, 1:2], None, ALU.mult).then_inc(state_made, 1)
                for k in range(2):
                    V.tensor_copy(W2s[k][:].rearrange("p (q b d) -> p q b d", q=NH // 2, b=BH),
                                  bcast(w2_small[:], 2, BH)).then_inc(state_made, 1)
                V.tensor_tensor(lnw2[:], lnw[:], lnw[:], ALU.mult).then_inc(state_made, 1)
                for t in (X2T[1], xb, X2[1], G2bd[1], G2[1]):
                    V.memset(t[:], 0.0).then_inc(state_made, 1)
                dve.wait_ge(state_made, 9)
                steps(dve, first, body, last)


GU = 4
NG = NU // GU


def ln_steps(tag):
    return ([f"{tag}bn{j}" for j in range(GU)] + [f"{tag}{x}" for x in ("sum", "diff", "m2", "between", "var")] + rsqrt_steps(tag) + [f"{tag}shift"]
            + [f"{tag}norm{j}" for j in range(GU)])


HEADS = ["i_mean", "i_center", "i_var"] + rsqrt_steps("i_", True)
NORMED = ln_steps("o_") + ["weight", "bias"]
FINAL = ln_steps("h_")
TWO = ["0", "1"]
GPOOL = ["query_beta", "gate_weight", "gate_bias", "xhat", "scale", "attention"]
MDVE = ([f"y{e}_{j}" for e in range(E) for j in range(GU)] + ln_steps("m_")
        + ["gamma", "beta", "residual"] + ln_steps("f_"))
MPE = []
for _e in range(E + 1):
    if _e < E:
        MPE += [f"z{2 * _e}", f"z{2 * _e + 1}"]
    if _e > 0:
        MPE += [f"y{_e - 1}_0", f"y{_e - 1}_1"]
MACT = [f"z{c}" for c in range(EC)]


class Group:
    def __init__(self, i, c):
        self.i, self.c, self.par = i, c, c % 2

    def loads(self, each):
        return self.i * (16 * each) + 16 * each * (self.c // 2 + 1)

    def at(self, names, name, back=0):
        each = len(names)
        return self.i * (2 * each) + each * (self.c + 1 - back) + names.index(name) + 1

    def row(self, n, first=0):
        return bass.ds(self.i * (2 * GU * n) + (self.c * GU * n + first), GU * n)


def groups(eng, body):
    with eng.Fori(0, NG // 2) as i:
        body(Group(i, 0))
        body(Group(i, 1))


def staggered(eng, *parts):
    def round_(group, k=None):
        for delay, do in parts:
            if k is None or 0 <= k - delay < NG:
                do(group(delay))
    for k in (0, 1):
        round_(lambda delay: Group(0, k - delay), k)
    with eng.Fori(0, NG // 2 - 1) as i:
        for c in range(2):
            round_(lambda delay: Group(i, c + 2 - delay))
    for k in (NG, NG + 1):
        round_(lambda delay: Group(0, k - delay), k)


def layer_norm(nc, step, own, src, dst, stats, mv, rs, eps, tag):
    V = nc.vector
    for j in range(GU):
        step(V.bn_stats(stats[:, j, :], src(j)))
    own(f"{tag}bn{GU - 1}")
    mean2, diff, m2, var = (mv[:, k, :] for k in range(4))
    step(V.tensor_tensor(mean2, stats[:, :, 1], stats[:, :, 4], ALU.add))
    step(V.tensor_tensor(diff, stats[:, :, 1], stats[:, :, 4], ALU.subtract))
    step(V.tensor_tensor(m2, stats[:, :, 2], stats[:, :, 5], ALU.add))
    own(f"{tag}m2")
    step(V.scalar_tensor_tensor(diff, diff, 0.25, diff, ALU.mult, ALU.mult))
    own(f"{tag}between")
    step(V.scalar_tensor_tensor(var, m2, 1.0 / W, diff, ALU.mult, ALU.add))
    own(f"{tag}var")
    rsqrt(nc, step, own, rs[:, 0, :], rs[:, 1, :], rs[:, 2, :], var, eps, tag)
    step(V.scalar_tensor_tensor(rs[:, 3, :], mean2, -0.5, rs[:, 0, :], ALU.mult, ALU.mult))
    own(f"{tag}shift")
    for j in range(GU):
        step(V.tensor_scalar(dst(j), src(j), rs[:, 0, j:j + 1], rs[:, 3, j:j + 1], ALU.mult, ALU.add))
    own(f"{tag}norm{GU - 1}")


def attention_out(nc, A, hT, attn, q_dram, h2_dram, H2TA, H2TB, ident):
    with ExitStack() as ctx:
        sb = lambda name, shape: ctx.enter_context(nc.sbuf_tensor(name, shape, F32))
        two = lambda name, shape: [sb(f"{name}_{i}", shape) for i in range(2)]
        sem = lambda name: ctx.enter_context(nc.semaphore(name))
        WgA, WgB = sb("WgA", [P, W]), sb("WgB", [WB, W])
        WoA, WoB = sb("WoA", [P, W]), sb("WoB", [WB, W])
        pw, pb_ = sb("pw", [P, W]), sb("pb", [P, W])
        lnw, lnb = sb("lnw3", [P, W]), sb("lnb3", [P, W])
        O, Qr, hA, hB = two("O", [P, GU, W]), two("Qr", [P, GU, W]), two("ghA", [P, GU, P]), two("ghB", [WB, GU, P])
        sq, ist = sb("sq3", [P, GU, W]), two("ist", [P, 5, GU * NH])
        gate, gate_w, gate_b = sb("gate", [P, GU, W]), two("gate_w", [P, GU, W]), two("gate_b", [P, GU, W])
        normed = sb("normed", [P, GU, W])
        oTA, oTB = sb("oTA", [P, GU * P]), sb("oTB", [WB, GU * P])
        h2 = two("h2", [P, GU, W])
        stats, mv, rs = sb("stats", [P, GU, 6]), sb("mv", [P, 4, GU]), sb("rs", [P, 4, GU])
        bank = [ctx.enter_context(nc.psum_tensor(f"out_bank{i}", [P, BANK], F32)) for i in range(NBANK)]
        weights_loaded = sem("out_weights_loaded")
        rows_loaded = [sem("rows_loaded0"), sem("rows_loaded1")]
        hT_loaded = [sem("hT_loaded0"), sem("hT_loaded1")]
        h2_stored = [sem("h2_stored0"), sem("h2_stored1")]
        gate_filled, oT_filled, h_filled, hT_filled = (sem(f"o_{n}_filled") for n in ("gate", "oT", "h", "hT"))
        gate_done, square_done, oT_done, hT_done = (sem(f"o_{n}_done") for n in ("gate", "square", "oT", "hT"))
        heads_done, normed_done, final_done = (sem(f"o_{n}_done") for n in ("heads", "normed", "final"))
        pool_done = sem("o_pool_done")
        gate_bank, T_bank, h_bank = bank[0:2], bank[2:4], [bank[4:6], bank[6:8]]
        unit_pair = lambda pb: pb[:, 0:2 * W].rearrange("p (j n) -> p j n", j=2)
        heads = lambda t: t[:].rearrange("p u k -> p (u k)").rearrange("p (g d) -> p g d", d=D)
        stat = lambda s, k: bcast(ist[s.par][:, k, :], 2, D)

        with nc.Block() as block:
            @block.sync
            def _(sp):
                def load_rows(s, ahead):
                    r = s.i * (2 * GU) + (s.c + ahead) * GU
                    for dst, src in ((O[s.par], attn[bass.ds(r + 1, GU), :, :].rearrange("u p k -> p u k")),
                                     (Qr[s.par], q_dram[bass.ds(r, GU), :, :].rearrange("u p k -> p u k"))):
                        sp.dma_start(dst[:], src).then_inc(rows_loaded[s.par], 16)

                def load_hT(s, ahead):
                    r = s.i * (2 * GU) + (s.c + ahead) * GU
                    for dst, src in ((hA[s.par], hT[bass.ds(r, GU), 0:P, :].rearrange("u f k -> f u k")),
                                     (hB[s.par], hT[bass.ds(r, GU), P:W, :].rearrange("u f k -> f u k"))):
                        sp.dma_start(dst[:], src).then_inc(hT_loaded[s.par], 16)

                def body(s):
                    sp.wait_ge(normed_done, s.at(NORMED, f"o_norm{GU - 1}"))
                    load_rows(s, 2)
                    sp.wait_ge(h_filled, s.at(TWO, "1"))
                    load_hT(s, 2)

                for c in range(2):
                    sp.sem_inc(h2_stored[c], 16)
                    load_rows(Group(0, c), 0)
                    load_hT(Group(0, c), 0)
                for dst, src in ((WgA, A["Wg"][0:P, :]), (WgB, A["Wg"][P:W, :]), (WoA, A["Wo"][0:P, :]),
                                 (WoB, A["Wo"][P:W, :]), (pw, A["pw"].broadcast_to([P, W])),
                                 (pb_, A["pb"].broadcast_to([P, W])),
                                 (lnw, A["lnw"].broadcast_to([P, W])), (lnb, A["lnb"].broadcast_to([P, W]))):
                    sp.dma_start(dst[:], src).then_inc(weights_loaded, 16)
                with sp.Fori(0, NG // 2 - 1) as i:
                    body(Group(i, 0))
                    body(Group(i, 1))
                for c in range(2):
                    sp.wait_ge(h2_stored[c], 16 * (NG // 2 + 1))

            @block.tensor
            def _(pe):
                for filled in (gate_filled, oT_filled, h_filled, hT_filled):
                    pe.sem_inc(filled, len(TWO))
                pe.wait_ge(weights_loaded, 16 * 8)

                def transposes(src, filled):
                    for k, (f0, f1) in enumerate(((0, P), (P, W))):
                        for j in range(GU):
                            q = nc.tensor.transpose(T_bank[k][0:f1 - f0, j * P:(j + 1) * P], src[:, j, f0:f1], ident[:])
                        q.then_inc(filled, 1)

                def gates(s):
                    pe.wait_ge(hT_loaded[s.par], s.loads(2))
                    for k in range(2):
                        pe.wait_ge(gate_done, s.at(TWO, str(k), 1))
                        for m in range(2):
                            j = 2 * k + m
                            o = gate_bank[k][:, m * W:(m + 1) * W]
                            nc.tensor.matmul(o, hA[s.par][:, j, :], WgA[:], start=True, stop=False)
                            q = nc.tensor.matmul(o, hB[s.par][:, j, :], WgB[:], start=False, stop=True)
                        q.then_inc(gate_filled, 1)

                def residual(s):
                    pe.wait_ge(normed_done, s.at(NORMED, "bias"))
                    pe.wait_ge(oT_done, s.at(TWO, "1", 1))
                    if not isinstance(s.i, int) or s.c >= 2:
                        pe.wait_ge(hT_done, s.at(TWO, "1", 2))
                    transposes(normed, oT_filled)
                    pe.wait_ge(oT_done, s.at(TWO, "1"))
                    for k in range(2):
                        if not isinstance(s.i, int) or s.c >= 2:
                            pe.wait_ge(final_done, s.at(FINAL, f"h_norm{GU - 1}", 2))
                        for m in range(2):
                            j = 2 * k + m
                            c = slice(j * P, (j + 1) * P)
                            o = h_bank[s.par][k][:, m * W:(m + 1) * W]
                            nc.tensor.matmul(o, oTA[:, c], WoA[:], start=True, stop=False)
                            nc.tensor.matmul(o, oTB[:, c], WoB[:], start=False, stop=False)
                            nc.tensor.matmul(o[:, 0:P], hA[s.par][:, j, :], ident[:], start=False, stop=False)
                            q = nc.tensor.matmul(o[:, P:W], hB[s.par][:, j, :], ident[0:WB, 0:WB], start=False, stop=True)
                        q.then_inc(h_filled, 1)

                def h2T(s):
                    pe.wait_ge(final_done, s.at(FINAL, f"h_norm{GU - 1}"))
                    if isinstance(s.i, int) and s.c == NG - 1:
                        pe.wait_ge(hT_done, s.at(TWO, "1", 1))
                    else:
                        pe.wait_ge(oT_done, s.at(TWO, "1", -1))
                    transposes(h2[s.par], hT_filled)
                staggered(pe, (0, gates), (1, residual), (2, h2T))

            @block.scalar
            def _(act):
                for done in (gate_done, oT_done, hT_done):
                    act.sem_inc(done, len(TWO))

                def evac(s, filled, done, k, dst, src, func=ACT.Copy):
                    act.wait_ge(filled, s.at(TWO, str(k)))
                    nc.scalar.activation(dst, src, func).then_inc(done, 1)

                def square(s):
                    act.wait_ge(heads_done, s.at(HEADS, "i_center"))
                    nc.scalar.activation(sq[:], O[s.par][:], ACT.Square).then_inc(square_done, 1)

                def gates(s):
                    if not isinstance(s.i, int) or s.c >= 1:
                        act.wait_ge(pool_done, s.at(GPOOL, "gate_bias", 1))
                    for k in range(2):
                        evac(s, gate_filled, gate_done, k, gate[:, 2 * k:2 * k + 2, :], unit_pair(gate_bank[k]),
                             ACT.Gelu_apprx_tanh)

                def oT(s):
                    evac(s, oT_filled, oT_done, 0, oTA[:], T_bank[0][:, :])
                    evac(s, oT_filled, oT_done, 1, oTB[:], T_bank[1][0:WB, :])

                def h2T(s):
                    act.wait_ge(final_done, s.at(FINAL, f"h_norm{GU - 1}"))
                    act.dma_start(h2_dram[s.row(1), :, :].rearrange("u p k -> p u k"), h2[s.par][:]).then_inc(h2_stored[s.par], 16)
                    evac(s, hT_filled, hT_done, 0, H2TA[:, s.row(P)], T_bank[0][:, :])
                    evac(s, hT_filled, hT_done, 1, H2TB[0:WB, s.row(P)], T_bank[1][0:WB, :])
                staggered(act, (0, square), (0, gates), (1, oT), (2, h2T))

            @block.gpsimd
            def _(pool):
                pool.sem_inc(pool_done, len(GPOOL))
                pool.wait_ge(weights_loaded, 16 * 8)

                def body(s):
                    def op(out, a, b, kind):
                        nc.gpsimd.tensor_tensor(out, a, b, kind).then_inc(pool_done, 1)
                    pool.wait_ge(rows_loaded[s.par], s.loads(2))
                    op(Qr[s.par][:], Qr[s.par][:], bcast(lnb[:, :], 1, GU), ALU.add)
                    pool.wait_ge(gate_done, s.at(TWO, "1"))
                    if not isinstance(s.i, int) or s.c >= 2:
                        pool.wait_ge(normed_done, s.at(NORMED, "bias", 2))
                    op(gate_w[s.par][:], gate[:], bcast(pw[:, :], 1, GU), ALU.mult)
                    op(gate_b[s.par][:], gate[:], bcast(pb_[:, :], 1, GU), ALU.mult)
                    pool.wait_ge(heads_done, s.at(HEADS, HEADS[-1]))
                    op(heads(O[s.par]), heads(O[s.par]), stat(s, 2), ALU.mult)
                    pool.wait_ge(pool_done, s.at(GPOOL, "xhat"))
                    op(O[s.par][:], O[s.par][:], bcast(lnw[:, :], 1, GU), ALU.mult)
                    pool.wait_ge(pool_done, s.at(GPOOL, "scale"))
                    op(O[s.par][:], O[s.par][:], Qr[s.par][:], ALU.add)
                staggered(pool, (0, body))

            @block.vector
            def _(dve):
                V = nc.vector
                dve.sem_inc(heads_done, len(HEADS))
                dve.sem_inc(normed_done, len(NORMED))
                dve.sem_inc(final_done, len(FINAL))
                dve.wait_ge(weights_loaded, 16 * 8)

                def center(s):
                    step = lambda ins: ins.then_inc(heads_done, 1)
                    dve.wait_ge(rows_loaded[s.par], s.loads(2))
                    if not isinstance(s.i, int) or s.c >= 2:
                        dve.wait_ge(pool_done, s.at(GPOOL, "xhat", 2))
                    st = ist[s.par]
                    step(V.tensor_reduce(st[:, 0, :], heads(O[s.par]), AX, ALU.add))
                    dve.wait_ge(heads_done, s.at(HEADS, "i_mean"))
                    step(V.scalar_tensor_tensor(heads(O[s.par]), stat(s, 0), -1.0 / D, heads(O[s.par]), ALU.mult, ALU.add))

                def deviation(s):
                    step = lambda ins: ins.then_inc(heads_done, 1)
                    own = lambda name: dve.wait_ge(heads_done, s.at(HEADS, name))
                    st = ist[s.par]
                    dve.wait_ge(square_done, s.i * 2 + (s.c + 1))
                    step(V.tensor_reduce(st[:, 1, :], heads(sq), AX, ALU.add))
                    own("i_var")
                    rsqrt(nc, step, own, st[:, 2, :], st[:, 3, :], st[:, 4, :], st[:, 1, :], D * EPS_INNER, "i_",
                          float(D) ** 0.5)

                def norm_and_gate(s):
                    step = lambda ins: ins.then_inc(normed_done, 1)
                    own = lambda name: dve.wait_ge(normed_done, s.at(NORMED, name))
                    dve.wait_ge(pool_done, s.at(GPOOL, "attention"))
                    if not isinstance(s.i, int) or s.c >= 1:
                        dve.wait_ge(oT_filled, s.at(TWO, "1", 1))
                    layer_norm(nc, step, own, lambda j: O[s.par][:, j, :], lambda j: normed[:, j, :], stats, mv, rs,
                               EPS_INNER, "o_")
                    step(V.tensor_tensor(normed[:], normed[:], gate_w[s.par][:], ALU.mult))
                    own("weight")
                    step(V.tensor_tensor(normed[:], normed[:], gate_b[s.par][:], ALU.add))

                def final_norm(s):
                    step = lambda ins: ins.then_inc(final_done, 1)
                    own = lambda name: dve.wait_ge(final_done, s.at(FINAL, name))
                    dve.wait_ge(h_filled, s.at(TWO, "1"))
                    dve.wait_ge(h2_stored[s.par], s.i * 16 + 16 * (s.c // 2 + 1))
                    layer_norm(nc, step, own, lambda j: unit_pair(h_bank[s.par][j // 2])[:, j % 2, :],
                               lambda j: h2[s.par][:, j, :], stats, mv, rs, EPS_LN, "h_")
                staggered(dve, (0, center), (1, norm_and_gate), (0, deviation), (2, final_norm))


def experts(nc, A, out_dram, h2_dram, H2TA, H2TB):
    with ExitStack() as ctx:
        sb = lambda name, shape: ctx.enter_context(nc.sbuf_tensor(name, shape, F32))
        two = lambda name, shape: [sb(f"{name}_{i}", shape) for i in range(2)]
        sem = lambda name: ctx.enter_context(nc.semaphore(name))
        HR = W // 2
        gamma, beta = sb("gamma", [P, W]), sb("beta", [P, W])
        w1A, w1B, w2r = sb("w1A", [P, HR]), sb("w1B", [WB + 1, HR]), sb("w2r", [HR + 1, E])
        downA, downB = sb("downA", [P, E * DE]), sb("downB", [WB + 1, E * DE])
        up = sb("up", [P, EC, W])
        rank = sb("rank", [P, E])
        router = two("router", [HR + 1, GU * P])
        gates, logit, picked = sb("gates", [P, NU * E]), sb("logit", [P, NU * E]), sb("picked", [P, NU * E])
        eq, score = sb("eq", [P, NU * E]), sb("score", [P, NU * E])
        col = sb("col", [P, 8, NU])
        Z = sb("Z", [P, 4, GU * P])
        h2, acc = two("mh2", [P, GU, W]), two("acc", [P, GU, W])
        stats, mv, rs = sb("mstats", [P, GU, 6]), sb("mmv", [P, 4, GU]), sb("mrs", [P, 4, GU])
        bank = [ctx.enter_context(nc.psum_tensor(f"moe_bank{i}", [P, BANK], F32)) for i in range(NBANK)]
        router_loaded, weights_loaded, ones_set = sem("router_loaded"), sem("moe_weights_loaded"), sem("moe_ones_set")
        in_loaded = [sem("h2_loaded0"), sem("h2_loaded1")]
        out_stored = [sem("y_stored0"), sem("y_stored1")]
        r_filled, r_act, r_dve = sem("router_filled"), sem("router_act"), sem("router_dve")
        pe_filled, act_done, dve_done = sem("m_pe_filled"), sem("m_act_done"), sem("m_dve_done")
        z_bank = lambda c: bank[c % 4]
        y_bank = lambda e, k: bank[4 + 2 * (e % 2) + k]

        with nc.Block() as block:
            @block.sync
            def _(sp):
                for dst, src in ((w1A[:], A["fw1"][0:P, :]), (w1B[0:WB, :], A["fw1"][P:W, :]), (w1B[WB:WB + 1, :], A["fb1"]),
                                 (w2r[0:HR, :], A["fw2"]), (w2r[HR:HR + 1, :], A["fb2"]),
                                 (rank[:], A["rank"].broadcast_to([P, E]))):
                    sp.dma_start(dst, src).then_inc(router_loaded, 16)
                dn = A["down"].rearrange("e h d -> h e d")
                for dst, src in ((downA[:].rearrange("p (e d) -> p e d", e=E), dn[0:P]),
                                 (downB[0:WB, :].rearrange("p (e d) -> p e d", e=E), dn[P:W]),
                                 (downB[WB:WB + 1, :], A["downb"]),
                                 (up[:], A["up"].rearrange("(c p) h -> p c h", p=P)),
                                 (gamma[:], A["gamma"].broadcast_to([P, W])), (beta[:], A["beta"].broadcast_to([P, W]))):
                    sp.dma_start(dst, src).then_inc(weights_loaded, 16)

                def load(s, ahead):
                    sp.dma_start(h2[s.c][:], h2_dram[bass.ds(s.i * (2 * GU) + (s.c + ahead) * GU, GU), :, :].rearrange(
                        "u p k -> p u k")).then_inc(in_loaded[s.c], 16)

                def store(s):
                    sp.wait_ge(dve_done, s.at(MDVE, f"f_norm{GU - 1}"))
                    sp.dma_start(out_dram[s.row(1), :, :].rearrange("u p k -> p u k"), acc[s.c][:]).then_inc(out_stored[s.c], 16)

                for c in range(2):
                    sp.sem_inc(out_stored[c], 16)
                load(Group(0, 0), 0)
                load(Group(0, 1), 0)
                with sp.Fori(0, NG // 2 - 1) as i:
                    for c in range(2):
                        store(Group(i, c))
                        load(Group(i, c), 2)
                for c in range(2):
                    store(Group(NG // 2 - 1, c))
                for c in range(2):
                    sp.wait_ge(out_stored[c], 16 * (NG // 2 + 1))

            @block.gpsimd
            def _(pool):
                nc.gpsimd.memset(H2TB[WB:WB + 1, :], 1.0).then_inc(ones_set, 1)
                for k in range(2):
                    nc.gpsimd.memset(router[k][HR:HR + 1, :], 1.0).then_inc(ones_set, 1)

            @block.tensor
            def _(pe):
                pe.wait_ge(router_loaded, 16 * 6)
                pe.wait_ge(ones_set, 3)

                def hidden(g):
                    c = slice(g * GU * P, (g + 1) * GU * P)
                    if g >= 2:
                        pe.wait_ge(r_act, g - 1)
                    nc.tensor.matmul(bank[g % 2][0:HR, :], w1A[:], H2TA[:, c], start=True, stop=False)
                    nc.tensor.matmul(bank[g % 2][0:HR, :], w1B[:], H2TB[:, c], start=False, stop=True).then_inc(r_filled, 1)

                def logits(g):
                    pe.wait_ge(r_act, g + 1)
                    for j in range(GU):
                        u = g * GU + j
                        q = nc.tensor.matmul(bank[2][:, u * E:(u + 1) * E], router[g % 2][:, j * P:(j + 1) * P], w2r[:],
                                             start=True, stop=True)
                    q.then_inc(r_filled, 1)
                hidden(0)
                for g in range(NG):
                    if g + 1 < NG:
                        hidden(g + 1)
                    logits(g)

                pe.wait_ge(weights_loaded, 16 * 6)
                pe.wait_ge(r_dve, 1)
                pe.sem_inc(pe_filled, len(MPE))

                def body(s):
                    def z(c):
                        prev = c - 4 if c >= 4 else c - 4 + EC
                        pe.wait_ge(act_done, s.at(MACT, f"z{prev}", 0 if c >= 4 else 1))
                        o, w = z_bank(c)[:, :], slice(c * P, (c + 1) * P)
                        nc.tensor.matmul(o, downA[:, w], H2TA[:, s.row(P)], start=True, stop=False)
                        nc.tensor.matmul(o, downB[:, w], H2TB[:, s.row(P)], start=False, stop=True).then_inc(pe_filled, 1)

                    def y(e):
                        pe.wait_ge(act_done, s.at(MACT, f"z{2 * e + 1}"))
                        for k in range(2):
                            prev = e - 2 if e >= 2 else e - 2 + E
                            pe.wait_ge(dve_done, s.at(MDVE, f"y{prev}_{2 * k + 1}", 0 if e >= 2 else 1))
                            for m in range(2):
                                j = 2 * k + m
                                o = y_bank(e, k)[:, m * W:(m + 1) * W]
                                for d in range(2):
                                    c = 2 * e + d
                                    q = nc.tensor.matmul(o, Z[:, c % 4, j * P:(j + 1) * P], up[:, c, :],
                                                         start=(d == 0), stop=(d == 1))
                            q.then_inc(pe_filled, 1)
                    for e in range(E + 1):
                        if e < E:
                            z(2 * e)
                            z(2 * e + 1)
                        if e > 0:
                            y(e - 1)
                groups(pe, body)

            @block.scalar
            def _(act):
                for g in range(NG):
                    act.wait_ge(r_filled, max(2 * g, 1))
                    nc.scalar.activation(router[g % 2][0:HR, :], bank[g % 2][0:HR, :], ACT.Gelu).then_inc(r_act, 1)
                act.wait_ge(r_dve, 3)
                nc.scalar.activation(picked[:], logit[:], ACT.Exp).then_inc(r_act, 1)
                act.sem_inc(act_done, len(MACT))

                def body(s):
                    for c in range(EC):
                        act.wait_ge(pe_filled, s.at(MPE, f"z{c}"))
                        prev = c // 2 - 2
                        act.wait_ge(pe_filled, s.at(MPE, f"y{prev}_1") if prev >= 0 else s.at(MPE, f"y{prev + E}_1", 1))
                        nc.scalar.activation(Z[:, c % 4, :], z_bank(c)[:, :], ACT.Gelu).then_inc(act_done, 1)
                groups(act, body)

            @block.vector
            def _(dve):
                V = nc.vector
                n = [0]

                def link(ins):
                    n[0] += 1
                    ins.then_inc(r_dve, 1)
                    dve.wait_ge(r_dve, n[0])
                ue = lambda t: t[:].rearrange("p (u e) -> p u e", e=E)
                c_ = lambda k: bcast(col[:, k, :], 2, E)
                dve.wait_ge(r_filled, 2 * NG)
                dve.wait_ge(router_loaded, 16 * 6)
                link(V.tensor_copy(logit[:], bank[2][:, 0:NU * E]))
                link(V.tensor_reduce(col[:, 0, :], ue(logit), AX, ALU.max))
                link(V.tensor_tensor(ue(logit), ue(logit), c_(0), ALU.subtract))
                dve.wait_ge(r_act, NG + 1)
                link(V.tensor_reduce(col[:, 1, :], ue(picked), AX, ALU.add))
                link(V.reciprocal(col[:, 1, :], col[:, 1, :]))
                link(V.tensor_tensor(ue(gates), ue(picked), c_(1), ALU.mult))
                link(V.tensor_copy(picked[:], gates[:]))
                for k in range(2):
                    link(V.tensor_reduce(col[:, 2, :], ue(picked), AX, ALU.max))
                    link(V.tensor_tensor(ue(eq), ue(picked), c_(2), ALU.is_equal))
                    link(V.tensor_tensor(ue(score), ue(eq), bcast(rank[:, :], 1, NU), ALU.mult))
                    link(V.tensor_reduce(col[:, 3, :], ue(score), AX, ALU.max))
                    link(V.tensor_tensor(ue(eq), ue(score), c_(3), ALU.is_equal))
                    link(V.scalar_tensor_tensor(picked[:], eq[:], -2.0, picked[:], ALU.mult, ALU.add))
                link(V.tensor_scalar(eq[:], picked[:], 0.0, None, ALU.is_lt))
                link(V.tensor_tensor(gates[:], gates[:], eq[:], ALU.mult))
                link(V.tensor_reduce(col[:, 4, :], ue(gates), AX, ALU.add))
                link(V.tensor_scalar(col[:, 4, :], col[:, 4, :], EPS_GATE, None, ALU.add))
                link(V.reciprocal(col[:, 4, :], col[:, 4, :]))
                link(V.tensor_tensor(ue(gates), ue(gates), c_(4), ALU.mult))
                dve.wait_ge(weights_loaded, 16 * 6)
                dve.sem_inc(dve_done, len(MDVE))

                def body(s):
                    step = lambda ins: ins.then_inc(dve_done, 1)
                    own = lambda name: dve.wait_ge(dve_done, s.at(MDVE, name))
                    a, h = acc[s.c], h2[s.c]
                    dve.wait_ge(in_loaded[s.c], s.i * 16 + 16)
                    dve.wait_ge(out_stored[s.c], s.i * 16 + 16)
                    for e in range(E):
                        for j in range(GU):
                            if j % 2 == 0:
                                dve.wait_ge(pe_filled, s.at(MPE, f"y{e}_{j // 2}"))
                            if e > 0:
                                own(f"y{e - 1}_{j}")
                            gate = gates[:, bass.ds(s.i * (2 * GU * E) + ((s.c * GU + j) * E + e), 1)]
                            step(V.scalar_tensor_tensor(a[:, j, :], y_bank(e, j // 2)[:, (j % 2) * W:(j % 2 + 1) * W], gate,
                                                        (h if e == 0 else a)[:, j, :], ALU.mult, ALU.add))
                    own(f"y{E - 1}_{GU - 1}")
                    one = lambda j: a[:, j, :]
                    layer_norm(nc, step, own, one, one, stats, mv, rs, EPS_LN, "m_")
                    step(V.tensor_tensor(a[:], a[:], bcast(gamma[:, :], 1, GU), ALU.mult))
                    own("gamma")
                    step(V.tensor_tensor(a[:], a[:], bcast(beta[:, :], 1, GU), ALU.add))
                    own("beta")
                    step(V.tensor_tensor(a[:], a[:], h[:], ALU.add))
                    own("residual")
                    layer_norm(nc, step, own, one, one, stats, mv, rs, EPS_LN, "f_")
                groups(dve, body)


def build(nc, A, out):
    dram = lambda name, shape: nc.dram_tensor(name, shape, F32, kind="Internal").ap()
    hT = dram("hT", (NU + SPARE, W, P))
    attn = dram("attn", (NU + 1, P, W))
    q_dram = dram("q", (NU + 2, P, W))
    h2_dram = dram("h2", (NU, P, W))
    with ExitStack() as ctx:
        ident = ctx.enter_context(nc.sbuf_tensor("ident_sb", [P, P], F32))
        with nc.sbuf_tensor("LR", [P, NU * NH], F32) as LR:
            tokenizer(nc, A, hT, LR, ident)
            scan(nc, A, hT, attn, q_dram, LR, ident)
        H2TA = ctx.enter_context(nc.sbuf_tensor("H2TA", [P, NU * P], F32))
        H2TB = ctx.enter_context(nc.sbuf_tensor("H2TB", [WB + 1, NU * P], F32))
        attention_out(nc, A, hT, attn, q_dram, h2_dram, H2TA, H2TB, ident)
        experts(nc, A, out, h2_dram, H2TA, H2TB)


def layouts(v):
    def patches(x, side):
        p = 64 // side
        t = x.reshape(B, CH, side, p, side, p).transpose(2, 4, 3, 5, 1, 0)
        return t.reshape(side * side, B * p * p * CH)
    a = {"x0": patches(v["x"], 64), "x1": patches(v["x"], 32), "x2": patches(v["x"], 16)}
    for k in range(3):
        a[f"idx{k}"] = v[f"L0_tok_idx{k}"].reshape(GROUPS[k], GP)
        a[f"W{k}T"] = v[f"L0_tok_W{k}"].T
        a[f"b{k}"] = v[f"L0_tok_b{k}"].reshape(EMB, 1)
    a["WfT"], a["bf"] = v["L0_tok_Wf"].T, v["L0_tok_bf"].reshape(1, W)
    t = lambda n: v["L0_attn_" + n]
    a["lrT"], a["lrb"] = t("lr_weight").reshape(NH, W).T, t("lr_bias").reshape(1, NH)
    a["Wqkv"] = np.concatenate([t("Wq"), t("Wk"), t("Wv")], axis=1)
    a["learn"] = t("learnable_token_idx").reshape(1, MB)
    a["lnw"], a["lnb"] = t("norm_weight").reshape(1, W), t("norm_bias").reshape(1, W)
    a["ab1"], a["ab2"] = t("b1").reshape(1, NH * F), t("b2").reshape(1, NH * D)
    a["W1"], a["W2"], a["Wg"], a["Wo"] = t("W1"), t("W2"), t("Wg"), t("Wo")
    a["pw"], a["pb"] = t("post_norm_weight").reshape(1, W), t("post_norm_bias").reshape(1, W)
    f = lambda n: v["L0_ffn_" + n]
    a["fw1"], a["fb1"], a["fw2"], a["fb2"] = f("w1"), f("b1").reshape(1, W // 2), f("w2"), f("b2").reshape(1, E)
    a["down"], a["downb"], a["up"] = f("down_w"), f("down_b").reshape(1, E * DE), f("up_w").reshape(E * DE, W)
    a["gamma"], a["beta"] = f("gamma").reshape(1, W), f("beta").reshape(1, W)
    i = np.arange(P)
    same = (i[:, None] // MB) == (i[None, :] // MB)
    a["ident"] = np.eye(P, dtype=np.float32)
    a["block_mask"] = same.astype(np.float32)
    a["triu_mask"] = (same & (i[:, None] <= i[None, :])).astype(np.float32)
    a["recip"] = np.tile(np.float32(1) / np.arange(1, MB + 1, dtype=np.float32), (P, 1))
    a["rank"] = np.arange(E, 0, -1, dtype=np.float32).reshape(1, E)
    return {k: np.ascontiguousarray(x) for k, x in a.items()}


def kernel(**inputs):
    import concourse.bacc as bacc
    from concourse.bass_utils import run_bass_kernel_spmd
    nc = bacc.Bacc("TRN2", target_bir_lowering=False, num_devices=1)
    arrays = layouts({k: np.asarray(x) for k, x in inputs.items()})
    aps = {k: nc.dram_tensor(f"in_{k}", x.shape, mybir.dt.from_np(x.dtype), kind="ExternalInput").ap()
           for k, x in arrays.items()}
    out = nc.dram_tensor("out", (NU, P, W), F32, kind="ExternalOutput").ap()
    build(nc, aps, out)
    r = run_bass_kernel_spmd(nc, [{f"in_{k}": x for k, x in arrays.items()}], core_ids=[0])
    y = r.results[0]["out"].reshape(NS, B // BH, BH, MB, W)
    return y.transpose(1, 2, 0, 3, 4).reshape(B, T, W)
```

```python
import numpy as np
import concourse.bass as bass
from concourse import mybir
from contextlib import ExitStack

F32 = mybir.dt.float32
U32 = mybir.dt.uint32
ALU = mybir.AluOpType
ACT = mybir.ActivationFunctionType
AX = mybir.AxisListType.X

P = 128
B, T, W = 16, 256, 192
NH, D, F = 12, 16, 64
MB = 16
NS = T // MB
BH = P // MB
NU = NS * B // BH
WB = W - P
GP, CH, EMB = 16, 3, 64
SIDES = (64, 32, 16)
DIN = tuple(CH * (64 // s) ** 2 for s in SIDES)
GROUPS = tuple(s * s // GP for s in SIDES)
E, DE = 8, 256
EC = E * DE // P
BANK = 512
NBANK = 8
EPS_INNER, EPS_LN, EPS_GATE = 1e-6, 1e-5, 1e-8
GELU_C, GELU_A, GELU_D = 0.79788456, 0.044715, 0.1070322243


def bcast(ap, axis, n):
    ap = ap.unsqueeze(axis)
    shape = list(ap.shape)
    shape[axis] = n
    return ap.broadcast_to(shape)


def inverse_root_steps(tag):
    return [f"{tag}half", f"{tag}seed"] + [f"{tag}newton{k}" for k in range(9)]


def inverse_root(nc, step, own, y, a, x, tag):
    V = nc.vector
    I32 = mybir.dt.int32
    names = inverse_root_steps(tag)
    step(V.tensor_scalar(y.bitcast(I32), x.bitcast(I32), 1, None, ALU.logical_shift_right))
    own(names[0])
    step(V.tensor_scalar(y.bitcast(I32), y.bitcast(I32), -1.0, float(0x5F3759DF), ALU.mult, ALU.add))
    own(names[1])
    for k in range(3):
        step(V.tensor_tensor(a, y, y, ALU.mult))
        own(names[2 + 3 * k])
        step(V.scalar_tensor_tensor(a, a, -0.5, x, ALU.mult, ALU.mult))
        own(names[3 + 3 * k])
        step(V.scalar_tensor_tensor(y, a, 1.5, y, ALU.add, ALU.mult))
        own(names[4 + 3 * k])


def rsqrt_steps(tag):
    return [f"{tag}eps"] + inverse_root_steps(tag)


def rsqrt(nc, step, own, y, a, x, var, eps, tag):
    step(nc.vector.tensor_scalar(x, var, eps, None, ALU.add))
    own(f"{tag}eps")
    inverse_root(nc, step, own, y, a, x, tag)


def previous_jobs(readers):
    n = len(readers)
    out = []
    for k, r in enumerate(readers):
        j = k - NBANK
        while readers[j % n] is None:
            j -= NBANK
        out.append((j // n, j % n))
    return out


def tokenizer(nc, A, hT, LR, ident, later):
    NCOL = B * T
    T1, T2 = GROUPS[1], GROUPS[2]
    jobs = ["dve"] + ["act"] * 4 + ["act"] * 4 + ["dve"] * 2 + ["dve"] + ["act"] * 8 + ["act"] * 8
    J_RATE, J_T1, J_T2, J_Y1, J_Y2, J_T0, J_Y0 = 0, 1, 5, 9, 11, 12, 20
    J_H = len(jobs)
    for _ in range(NS // 2):
        jobs += ["act", "dve"]
    J_LR = len(jobs)
    jobs += ["dve"]
    emptied_by = []
    n = {"act": 0, "dve": 0}
    for r in jobs:
        n[r] += 1
        emptied_by.append(n[r])

    with ExitStack() as ctx:
        sb = lambda name, shape, dt=F32: ctx.enter_context(nc.sbuf_tensor(name, shape, dt))
        sem = lambda name: ctx.enter_context(nc.semaphore(name))
        idx0 = sb("idx0_sb", [P, 2 * GP], U32)
        J1, J2 = P // T1, P // T2
        idx1 = sb("idx1_sb", [P, GP // J1], U32)
        idx2 = sb("idx2_sb", [P, GP // J2], U32)
        G0 = sb("G0", [P, 2 * GP * B * DIN[0]])
        G1 = sb("G1", [P, GP // J1 * B * DIN[1]])
        G2 = sb("G2", [P, GP // J2 * B * DIN[2]])
        K0, K1, K2 = GP * DIN[0], GP * DIN[1] // J1, GP * DIN[2] // J2
        X0T = sb("X0T", [K0, NCOL])
        X1T = sb("X1T", [K1, 2, B * T1])
        X2T = sb("X2T", [K2, GP // 2, B * T2])
        W0 = sb("W0_sb", [K0, EMB])
        W1 = sb("W1_sb", [K1, 2, EMB])
        W2 = sb("W2_sb", [K2, GP // 2, EMB])
        bias01 = sb("bias01", [P, 1])
        bias2 = sb("bias2", [EMB, 1])
        WfA = sb("WfA", [P, W + NH])
        WfB = sb("WfB", [WB + 1, W + NH])
        WrA, WrB = sb("WrA", [P, W + 1]), sb("WrB", [WB, W + 1])
        lrA = sb("lrA", [P, NH])
        lrB = sb("lrB", [WB + 1, NH])
        Y1 = sb("Y1", [P, B, T1 + 2])
        D1 = sb("D1", [P, B, T1 + 1])
        Y2 = sb("Y2", [EMB, B, T2 + 2])
        D2 = sb("D2", [EMB, B, T2 + 1])
        YA = sb("YA", [P, NCOL])
        YB = sb("YB", [WB + 1, NCOL])
        HA = sb("HA", [P, 2, BANK])
        HB = sb("HB", [WB, 2, BANK])
        LE = sb("LE", [WB + NH, NCOL])
        bank = [ctx.enter_context(nc.psum_tensor(f"tok_bank{i}", [P, BANK], F32)) for i in range(NBANK)]

        idx_loaded, weights_loaded = sem("tok_idx_loaded"), sem("tok_weights_loaded")
        gathered = [sem(f"gathered{i}") for i in range(3)]
        filled, act_emptied, dve_emptied = sem("tok_filled"), sem("tok_act_emptied"), sem("tok_dve_emptied")
        padded, levels_done, ones_set = sem("tok_padded"), sem("tok_levels_done"), sem("tok_ones_set")
        h_stored, lr_steps = [sem("h_stored0"), sem("h_stored1")], sem("lr_steps")
        rates_emptied, rate_weights = sem("rates_emptied"), sem("rate_weights")
        emptied = {"act": act_emptied, "dve": dve_emptied}
        NLOAD = 16

        with nc.Block() as block:
            @block.sync
            def _(sp):
                sp.dma_start(idx1[:], A["idx1"].bitcast(U32)).then_inc(idx_loaded, 16)
                sp.dma_start(idx2[:], A["idx2"].bitcast(U32)).then_inc(idx_loaded, 16)
                sp.dma_start(idx0[:].rearrange("p (t g) -> p t g", t=2),
                             A["idx0"].bitcast(U32).rearrange("(t p) g -> p t g", t=2)).then_inc(idx_loaded, 16)
                loads = [
                    (ident[:], A["ident"]),
                    (W1[:], A["W1T"].rearrange("(j k) e -> k j e", j=2)),
                    (W2[:], A["W2T"].rearrange("(j k) e -> k j e", k=K2)),
                    (W0[:], A["W0T"]),
                    (bias01[0:EMB, :], A["b0"]), (bias01[EMB:P, :], A["b1"]), (bias2[:], A["b2"]),
                    (WfA[:, 0:W], A["WfT"][0:P, :]), (WfB[0:WB, 0:W], A["WfT"][P:W, :]), (WfB[WB:WB + 1, 0:W], A["bf"]),
                    (WrA[:, 0:W], A["Wf"][0:P, :]), (WrB[:, 0:W], A["Wf"][P:W, :]),
                    (WrA[:, W:W + 1], A["bf_col"][0:P, :]), (WrB[:, W:W + 1], A["bf_col"][P:W, :]),
                    (lrA[:], A["lrT"][0:P, :]), (lrB[0:WB, :], A["lrT"][P:W, :]), (lrB[WB:WB + 1, :], A["lrb"]),
                ]
                for dst, src in loads:
                    sp.dma_start(dst, src).then_inc(weights_loaded, 16)
                for dst, src in later["loads"]:
                    sp.dma_start(dst, src).then_inc(later["loaded"], 16)
                for i in range(NS // 2):
                    sp.wait_ge(act_emptied, emptied_by[J_H + 2 * i])
                    sp.dma_start(hT[4 * i:4 * i + 4, 0:P, :].rearrange("u f k -> f u k"),
                                 HA[:, i % 2, :].rearrange("p (u k) -> p u k", u=4)).then_inc(h_stored[i % 2], 16)
                    sp.wait_ge(dve_emptied, emptied_by[J_H + 2 * i + 1])
                    sp.dma_start(hT[4 * i:4 * i + 4, P:W, :].rearrange("u f k -> f u k"),
                                 HB[0:WB, i % 2, :].rearrange("p (u k) -> p u k", u=4)).then_inc(h_stored[i % 2], 16)
                for u in range(SPARE):
                    sp.dma_start(hT[NU + u, 0:P, :], HA[:, 1, u * P:(u + 1) * P]).then_inc(h_stored[u % 2], 16)
                    sp.dma_start(hT[NU + u, P:W, :], HB[0:WB, 1, u * P:(u + 1) * P]).then_inc(h_stored[u % 2], 16)
                for k in range(2):
                    sp.wait_ge(h_stored[k], 16 * (NS // 2) + 32 * len(range(k, SPARE, 2)))

            @block.gpsimd
            def _(pool):
                pool.wait_ge(idx_loaded, 48)
                n1, n2 = B * DIN[1], B * DIN[2]
                for g in range(GP // J1):
                    nc.gpsimd.indirect_dma_start(
                        G1[:, g * n1:(g + 1) * n1], None, A["x1"],
                        bass.IndirectOffsetOnAxis(idx1[:, g:g + 1], 0)).then_inc(gathered[1], 16)
                for g in range(GP // J2):
                    nc.gpsimd.indirect_dma_start(
                        G2[:, g * n2:(g + 1) * n2], None, A["x2"],
                        bass.IndirectOffsetOnAxis(idx2[:, g:g + 1], 0)).then_inc(gathered[2], 16)
                for j in range(2 * GP):
                    n0 = B * DIN[0]
                    nc.gpsimd.indirect_dma_start(
                        G0[:, j * n0:(j + 1) * n0], None, A["x0"],
                        bass.IndirectOffsetOnAxis(idx0[:, j:j + 1], 0)).then_inc(gathered[0], 16)

            @block.tensor
            def _(pe):
                def bank_free(k):
                    if k >= NBANK:
                        pe.wait_ge(emptied[jobs[k - NBANK]], emptied_by[k - NBANK])
                        if J_H <= k - NBANK < J_LR and (k - NBANK - J_H) % 2:
                            pe.wait_ge(rates_emptied, (k - NBANK - J_H) // 2 + 1)
                    return bank[k % NBANK]

                pe.wait_ge(weights_loaded, 16 * 17)
                pb = bank_free(J_RATE)
                for n, (k0, k1) in enumerate(((0, P), (P, W + 1))):
                    o = pb[0:k1 - k0, n * NH:(n + 1) * NH]
                    nc.tensor.matmul(o, WrA[:, k0:k1], lrA[:], start=True, stop=False)
                    q = nc.tensor.matmul(o, WrB[:, k0:k1], lrB[0:WB, :], start=False, stop=True)
                q.then_inc(filled, 1)
                for level, (G, job) in enumerate(((G1, J_T1), (G2, J_T2)), 1):
                    pe.wait_ge(gathered[level], 16 * (GP // (J1 if level == 1 else J2)))
                    v = G[:].rearrange("t (n b) -> t b n", b=B)
                    for k in range(4):
                        pb = bank_free(job + k)
                        for m in range(4):
                            q = nc.tensor.transpose(pb[0:v.shape[2], m * P:(m + 1) * P], v[:, 4 * k + m], ident[:])
                        q.then_inc(filled, 1)
                pe.wait_ge(act_emptied, emptied_by[J_T1 + 3])
                for k in range(2):
                    pb = bank_free(J_Y1 + k)
                    for j in range(2):
                        q = nc.tensor.matmul(pb[EMB:P, :], W1[:, j, :], X1T[:, j, k * BANK:(k + 1) * BANK],
                                             start=(j == 0), stop=(j == 1))
                    q.then_inc(filled, 1)
                pe.wait_ge(act_emptied, emptied_by[J_T2 + 3])
                pb = bank_free(J_Y2)
                for j in range(GP // 2):
                    q = nc.tensor.matmul(pb[0:EMB, 0:B * T2], W2[:, j, :], X2T[:, j, :],
                                         start=(j == 0), stop=(j == GP // 2 - 1))
                q.then_inc(filled, 1)
                pe.wait_ge(gathered[0], 16 * 2 * GP)
                v0 = G0[:].rearrange("t (j n b) -> t j b n", j=2, b=B)
                for k in range(8):
                    pb = bank_free(J_T0 + k)
                    for m in range(4):
                        q = nc.tensor.transpose(pb[0:K0, m * P:(m + 1) * P], v0[:, k % 2, 4 * (k // 2) + m], ident[:])
                    q.then_inc(filled, 1)
                for k in range(8):
                    pb = bank_free(J_Y0 + k)
                    pe.wait_ge(act_emptied, emptied_by[J_T0 + (k // 2) * 2 + 1])
                    nc.tensor.matmul(pb[0:EMB, :], W0[:], X0T[:, k * BANK:(k + 1) * BANK],
                                     start=True, stop=True).then_inc(filled, 1)
                pe.wait_ge(act_emptied, emptied_by[J_Y0 + 7])
                pe.wait_ge(levels_done, 2)
                pe.wait_ge(ones_set, 1)
                yA = YA[:].rearrange("p (b s k) -> p s b k", b=B, s=NS)
                yB = YB[:].rearrange("p (b s k) -> p s b k", b=B, s=NS)

                pe.wait_ge(dve_emptied, emptied_by[J_RATE])
                for i in range(NS // 2):
                    for half, (m0, m1) in enumerate(((0, P), (P, W + NH))):
                        pb = bank_free(J_H + 2 * i + half)
                        nc.tensor.matmul(pb[0:m1 - m0, :], WfA[:, m0:m1], yA[:, 2 * i:2 * i + 2], start=True, stop=False)
                        nc.tensor.matmul(pb[0:m1 - m0, :], WfB[:, m0:m1], yB[:, 2 * i:2 * i + 2],
                                         start=False, stop=True).then_inc(filled, 1)
                pb = bank_free(J_LR)
                pe.wait_ge(rates_emptied, NS // 2)
                for u in range(NU):
                    q = nc.tensor.transpose(pb[:, u * NH:(u + 1) * NH], LE[WB:, u * P:(u + 1) * P],
                                            ident[WB:WB + NH, WB:WB + NH])
                q.then_inc(filled, 1)

            @block.scalar
            def _(act):
                def job(k, out, in_, func=ACT.Copy, **kw):
                    act.wait_ge(filled, k + 1)
                    nc.scalar.activation(out, in_, func, **kw).then_inc(act_emptied, 1)

                x1 = X1T[:].rearrange("p j (b t) -> p b j t", b=B)
                x2 = X2T[:].rearrange("p j (b t) -> p b j t", b=B)
                for x, K, parts, first in ((x1, K1, J1, J_T1), (x2, K2, J2, J_T2)):
                    for k in range(4):
                        job(first + k, x[:, 4 * k:4 * k + 4], bank[(first + k) % NBANK][0:K, :].rearrange(
                            "p (b j t) -> p b j t", b=4, j=parts))
                x0 = X0T[:].rearrange("p (b t n) -> p b t n", b=B, t=2)
                for k in range(8):
                    job(J_T0 + k, x0[:, 4 * (k // 2):4 * (k // 2) + 4, k % 2, :],
                        bank[(J_T0 + k) % NBANK][0:K0, :].rearrange("p (b n) -> p b n", b=4))
                act.wait_ge(weights_loaded, 16 * 17)
                for k in range(8):
                    job(J_Y0 + k, YA[0:EMB, k * BANK:(k + 1) * BANK], bank[(J_Y0 + k) % NBANK][0:EMB, :],
                        ACT.Identity, bias=bias01[0:EMB, 0:1])
                for i in range(NS // 2):
                    if i >= 2:
                        act.wait_ge(h_stored[i % 2], 32 * (i // 2))
                    k = J_H + 2 * i
                    job(k, HA[:, i % 2, :], bank[k % NBANK][:, :])
                    act.wait_ge(filled, k + 2)
                    nc.scalar.activation(LE[WB:, i * BANK:(i + 1) * BANK], bank[(k + 1) % NBANK][WB:WB + NH, :], ACT.Exp,
                                         scale=-1.0).then_inc(rates_emptied, 1)

            @block.vector
            def _(dve):
                nc.vector.memset(YB[WB:WB + 1, :], 1.0).then_inc(ones_set, 1)
                dve.wait_ge(weights_loaded, 16 * 17)
                dve.wait_ge(filled, J_RATE + 1)
                pb = bank[J_RATE % NBANK]
                nc.vector.tensor_copy(WfA[:, W:], pb[:, 0:NH]).then_inc(rate_weights, 1)
                nc.vector.tensor_copy(WfB[0:WB, W:], pb[0:WB, NH:2 * NH]).then_inc(rate_weights, 1)
                nc.vector.tensor_tensor(WfB[WB:WB + 1, W:], pb[WB:WB + 1, NH:2 * NH], lrB[WB:WB + 1, :],
                                        ALU.add).then_inc(dve_emptied, 1)
                for k in range(2):
                    dve.wait_ge(filled, J_Y1 + k + 1)
                    nc.vector.tensor_scalar(Y1[EMB:P, 8 * k:8 * k + 8, 1:T1 + 1],
                                            bank[(J_Y1 + k) % NBANK][EMB:P, :].rearrange("p (b t) -> p b t", b=8),
                                            bias01[EMB:P, 0:1], None, ALU.add).then_inc(dve_emptied, 1)
                dve.wait_ge(filled, J_Y2 + 1)
                nc.vector.tensor_scalar(Y2[:, :, 1:T2 + 1],
                                        bank[J_Y2 % NBANK][0:EMB, 0:B * T2].rearrange("p (b t) -> p b t", b=B),
                                        bias2[:, 0:1], None, ALU.add).then_inc(dve_emptied, 1)
                for Y, rows, t in ((Y1, slice(EMB, P), T1), (Y2, slice(0, EMB), T2)):
                    if t == T1:
                        dve.wait_ge(dve_emptied, 4)
                    nc.vector.tensor_copy(Y[rows, :, 0:1], Y[rows, :, 1:2]).then_inc(padded, 1)
                    nc.vector.tensor_copy(Y[rows, :, t + 1:t + 2], Y[rows, :, t:t + 1]).then_inc(padded, 1)
                dve.wait_ge(padded, 4)
                nc.vector.tensor_tensor(D1[EMB:P], Y1[EMB:P, :, 1:T1 + 2], Y1[EMB:P, :, 0:T1 + 1],
                                        ALU.subtract).then_inc(padded, 1)
                nc.vector.tensor_tensor(D2[:], Y2[:, :, 1:T2 + 2], Y2[:, :, 0:T2 + 1], ALU.subtract).then_inc(padded, 1)
                dve.wait_ge(padded, 6)
                for Y, Df, rows, t, out in ((Y1, D1, slice(EMB, P), T1, YA), (Y2, D2, slice(0, EMB), T2, YB)):
                    R = T // t
                    o = out[rows, :].rearrange("p (b k r) -> p b k r", b=B, r=R)
                    for r in range(R):
                        w = (r + 0.5) / R - 0.5
                        first = 0 if w < 0 else 1
                        w = w + 1.0 if w < 0 else w
                        q = nc.vector.scalar_tensor_tensor(o[:, :, :, r], Df[rows, :, first:first + t], w,
                                                           Y[rows, :, first:first + t], ALU.mult, ALU.add)
                    q.then_inc(levels_done, 1)
                for i in range(NS // 2):
                    k = J_H + 2 * i + 1
                    if i >= 2:
                        dve.wait_ge(h_stored[i % 2], 32 * (i // 2))
                    dve.wait_ge(filled, k + 1)
                    nc.vector.tensor_copy(HB[0:WB, i % 2, :], bank[k % NBANK][0:WB, :]).then_inc(dve_emptied, 1)
                dve.wait_ge(filled, J_LR + 1)
                nc.vector.tensor_scalar(LR[:], bank[J_LR % NBANK][:, 0:NU * NH], float(D), float(D),
                                        ALU.mult, ALU.add).then_inc(lr_steps, 1)
                dve.wait_ge(lr_steps, 1)
                nc.vector.reciprocal(LR[:], LR[:]).then_inc(lr_steps, 1)
                dve.wait_ge(lr_steps, 2)


QUARTER = P // 4
SPARE = 3
JOBS = [("z2", 4, "dve"), ("attn", 4, "dve"), ("kqT", 6, "act"), ("z2b", 4, "act"), ("m2", 1, "act"), ("w2", 2, "dve"),
        ("m2T", 1, "act"), ("m1", 3, "dve"),
        ("gT", 3, "act"), ("z1", 2, "dve"), ("gx", 2, "dve"), ("proj", 2, "act"), ("g1", 2, "act"), ("w2T", 2, "act"),
        ("z1b", 2, "dve"), ("w1", 2, "dve"), ("x2", 2, "act")]
SLOTS = [f"{n}{i}" for n, k, _ in JOBS for i in range(k)]
READER = {f"{n}{i}": r for n, k, r in JOBS for i in range(k)}
NJ = len(SLOTS)
PADDED = SLOTS + [None] * (-NJ % 4)
NP = len(PADDED)
SLOT_OF = {s: i for i, s in enumerate(PADDED) if s}
PREV = previous_jobs([READER[s] if s else None for s in PADDED])
ACT_STEPS = ([f"kqT{i}" for i in range(6)] + ["z2b0", "z2b1", "z2b2", "z2b3", "m20", "m2T0"]
             + ["gT0", "gT1", "gT2", "proj0", "proj1", "g10", "g11", "w2T0", "w2T1", "sq", "cube", "half", "slope", "tanh", "gelu_b", "x20", "x21"])
DVE_STEPS = (["z20", "z21", "z22", "z23", "z2_fold", "attn0", "z2_bias", "attn1", "mean", "attn2", "center", "attn3", "square", "var"] + rsqrt_steps("r_")
             + ["xhat", "gxh0", "gxh", "s1", "gx_xh", "s2", "lr_rstd", "s2_xh", "sub1", "sub2", "g2", "g2_bd", "w20", "w21", "b2"]
             + ["m10", "m11", "m12", "db", "dc", "dgelu", "gx0", "gx1", "z10", "z11", "arg"]
             + ["z1b0", "z1b1", "gelu", "b1_sum", "b1", "w10", "w11"])
POOL_STEPS = ["q_bd", "t0", "t1", "t2", "b2_copy", "k_bd", "zb_mask", "zb_half", "zb_quarter", "zb_fold", "zb_own", "out"]
DVE_OF = {"w21": "b2"}


def count_of(engine, job):
    if engine == "act":
        return ACT_STEPS.index(job) + 1
    return DVE_STEPS.index(DVE_OF.get(job, job)) + 1


def scan_constants(nc, A, ctx):
    sb = lambda name, shape: ctx.enter_context(nc.sbuf_tensor(name, shape, F32))
    two = lambda name, shape: [sb(f"{name}_{i}", shape) for i in range(2)]
    HD, HF = NH * D, NH * F
    block_mask = sb("block_mask", [P, P])
    neg_tril = sb("neg_tril", [P, P])
    tok, recip = sb("tok", [P, MB]), sb("recip", [P, MB])
    lnw, lnb = sb("lnw", [P, HD]), sb("lnb", [P, HD])
    w2_small, b1_small = sb("w2_small", [P, NH // 2, D]), sb("b1_small", [P, NH // 2])
    b2s = two("b2s", [P, HD])
    W1s = two("W1s", [P, HF])
    WqkvA, WqkvB = sb("WqkvA", [P, 3 * W]), sb("WqkvB", [WB, 3 * W])
    w2v = A["W2"].rearrange("(q two) f d -> two f q d", two=2)
    loads = [(block_mask[:], A["block_mask"]), (neg_tril[:], A["triu_mask"]), (recip[:], A["recip"]),
             (tok[:], A["learn"].broadcast_to([P, MB])),
             (lnw[:], A["lnw"].broadcast_to([P, HD])), (lnb[:], A["lnb"].broadcast_to([P, HD])),
             (b1_small[:], A["ab1"]),
             (b2s[0][:], A["ab2"].broadcast_to([P, HD])), (b2s[1][:], A["ab2"].broadcast_to([P, HD])),
             (WqkvA[:], A["Wqkv"][0:P, :]), (WqkvB[:], A["Wqkv"][P:W, :]),
             (w2_small[0:F], w2v[0]), (w2_small[F:P], w2v[1])]
    for k in range(2):
        for b in range(BH):
            loads.append((W1s[k][b * D:(b + 1) * D, :].rearrange("p (h f) -> p h f", f=F),
                          A["W1"].rearrange("h d f -> d h f")))
    return {"tensors": (block_mask, neg_tril, tok, recip, lnw, lnb, w2_small, b1_small, b2s, W1s, WqkvA, WqkvB),
            "loads": loads, "loaded": ctx.enter_context(nc.semaphore("consts_loaded"))}


def scan(nc, A, hT, attn, q_dram, LR, ident, C, later):
    with ExitStack() as ctx:
        sb = lambda name, shape: ctx.enter_context(nc.sbuf_tensor(name, shape, F32))
        two = lambda name, shape: [sb(f"{name}_{i}", shape) for i in range(2)]
        sem = lambda name: ctx.enter_context(nc.semaphore(name))
        HD, HF, HP = NH * D, NH * F, NH * P
        (block_mask, neg_tril, tok, recip, lnw, lnb, w2_small, b1_small, b2s, W1s, WqkvA, WqkvB) = C["tensors"]
        consts_loaded, n_consts = C["loaded"], 16 * len(C["loads"])
        neg_last = sb("neg_last", [P, P])
        last_col = sb("last_col", [P, 1])
        lnw2 = sb("lnw2", [P, HD])
        b1s = two("b1s", [P, NH // 2 * BH])
        W2s = two("W2s", [P, HP // 2])
        W2T = two("W2T", [P, HF])
        hA, hB = two("hA", [P, P]), two("hB", [WB, P])
        QKV = sb("QKV", [P, 3 * W])
        K_bd, Q_bd = two("K_bd", [P, HP]), sb("Q_bd", [P, HP])
        KT, QT = sb("KT", [P, HP]), two("QT", [P, HP])
        M1T, M2T = two("M1T", [P, HP]), sb("M2T", [P, HP])
        target, tt = two("target", [P, HD]), sb("tt", [P, HD])
        x, x_sq, arg, th = sb("x", [P, HF]), sb("x_sq", [P, HF]), sb("arg", [P, HF]), sb("th", [P, HF])
        cube, slope = sb("cube", [P, HF]), sb("slope", [P, HF])
        tmp, dg = sb("tmp", [P, HF]), sb("dg", [P, HF])
        x_half, X2T = sb("x_half", [P, HF]), two("X2Tr", [P, HF])
        X2 = two("X2", [P, HF])
        xb, XbT = sb("xb", [P, HF]), sb("XbT", [P, HF])
        Zm, Zb, b2_copy = sb("Zm", [P, HP]), sb("Zb", [P, HP]), sb("b2_copy", [P, HD])
        z, zc, zs, xh, g = sb("z", [P, HD]), sb("zc", [P, HD]), sb("zs", [P, HD]), sb("xh", [P, HD]), sb("g", [P, HD])
        st = sb("st", [P, 8, NH])
        G2, G2bd, GT = two("G2v", [P, HD + QUARTER - D]), two("G2bd", [P, HP]), sb("GT", [P, HP])
        G1T, G1 = sb("G1T", [P, HF]), sb("G1v", [P, HF])
        b1_sum = sb("b1_sum", [P, NH // 2 * BH])
        own_T, own_part = sb("own_T", [P, NH // 4 * P]), sb("own_part", [P, HD])
        out = two("scan_out", [P, HD])
        bank = [ctx.enter_context(nc.psum_tensor(f"scan_bank{i}", [P, BANK], F32)) for i in range(NBANK)]

        consts_made, state_made, last_made = sem("consts_made"), sem("state_made"), sem("last_made")
        pe_filled, act_done, dve_done, pool_done = sem("pe_filled"), sem("act_done"), sem("dve_done"), sem("pool_done")
        h_loaded = [sem("h_loaded0"), sem("h_loaded1")]
        out_stored = [sem("out_stored0"), sem("out_stored1")]
        q_stored, first_projected, first_copied = sem("q_stored"), sem("first_projected"), sem("first_copied")
        done = {"act": act_done, "dve": dve_done}
        per = {"act": len(ACT_STEPS), "dve": len(DVE_STEPS), "pool": len(POOL_STEPS), "pe": NJ}

        class Step:
            def __init__(self, i, c):
                self.i, self.c = i, c
                self.n, self.u, self.p = c % 2, (c - 1) % 2, c % 2

            def at(self, each, k, back=0):
                const = each * (self.c - back) + k
                return const if isinstance(self.i, int) else self.i * (2 * each) + const

        def bank_of(s, job):
            return bank[(s.c * NP + SLOT_OF[job]) % NBANK]

        def act_at(s, name, back=0):
            return s.at(per["act"], ACT_STEPS.index(name) + 1, back)

        def dve_at(s, name, back=0):
            return s.at(per["dve"], DVE_STEPS.index(name) + 1, back)

        def pool_at(s, name, back=0):
            return s.at(per["pool"], POOL_STEPS.index(name) + 1, back)

        def pe_at(s, job, back=0):
            return s.at(NJ, SLOTS.index(job) + 1, back)

        def steps(eng, first, body, last, sign_off=None):
            first(Step(0, 0))
            with eng.Fori(0, NU // 2) as i:
                body(Step(i, 1))
                body(Step(i, 2))
            last(Step(0, NU + 1))

        head = lambda ap, h, n: ap[:, h * n:(h + 1) * n]
        SPLIT = [(0, 2, 4, 6), (1, 3, 5, 7), (8, 10), (9, 11)]
        PLACE = {h: n for n, h in enumerate(h for hs in SPLIT for h in hs)}
        rows_of = lambda h: slice(F * (h % 2), F * (h % 2) + F)
        heads4 = lambda ap: ap.rearrange("p (h n) -> p h n", n=P)

        def split_view(ap, k):
            part = ap[:, 0:8 * P] if k < 2 else ap[:, 8 * P:]
            return part.rearrange("p (h two n) -> p two h n", two=2, n=P)[:, k % 2]

        def split_bank(pb, k):
            return pb[:, 0:len(SPLIT[k]) * P].rearrange("p (h n) -> p h n", n=P)

        def split_mask(m, k):
            return bcast(m[:, :], 1, len(SPLIT[k]))

        with nc.Block() as block:
            @block.sync
            def _(sp):
                def load_h(row, par):
                    sp.dma_start(hA[par][:], hT[row, 0:P, :].rearrange("u f k -> (u f) k")).then_inc(h_loaded[par], 16)
                    sp.dma_start(hB[par][:], hT[row, P:W, :].rearrange("u f k -> (u f) k")).then_inc(h_loaded[par], 16)

                def store_q(row):
                    sp.dma_start(q_dram[row, :, :].rearrange("u p k -> (u p) k"), QKV[:, 0:W]).then_inc(q_stored, 16)

                def first(s):
                    for par in range(2):
                        sp.sem_inc(out_stored[par], 16)
                    load_h(slice(0, 1), 0)
                    load_h(slice(1, 2), 1)
                    sp.wait_ge(first_projected, 2)
                    load_h(slice(2, 3), 0)
                    sp.wait_ge(first_copied, 2)
                    store_q(slice(0, 1))
                    sp.wait_ge(act_done, act_at(s, "proj1"))
                    store_q(slice(1, 2))
                    for dst, src in later["loads"]:
                        sp.dma_start(dst, src).then_inc(later["loaded"], 16)

                def body(s):
                    sp.wait_ge(pe_filled, pe_at(s, "proj1", 1))
                    load_h(bass.ds(s.i * 2 + (s.c + 2), 1), s.n)
                    sp.wait_ge(act_done, act_at(s, "proj1"))
                    store_q(bass.ds(s.i * 2 + (s.c + 1), 1))
                    sp.wait_ge(pool_done, pool_at(s, "out"))
                    sp.dma_start(attn[bass.ds(s.i * 2 + (s.c - 1), 1), :, :].rearrange("u p k -> (u p) k"),
                                 out[s.p][:]).then_inc(out_stored[s.p], 16)

                def last(s):
                    sp.wait_ge(last_made, 7)
                    sp.dma_start(attn[NU, :, :], out[s.p][:]).then_inc(out_stored[s.p], 16)
                    sp.wait_ge(q_stored, 16 * (NU + 2))
                    sp.wait_ge(out_stored[0], 16 * (NU // 2 + 1))
                    sp.wait_ge(out_stored[1], 16 * (NU // 2 + 2))
                    for par in range(2):
                        sp.wait_ge(h_loaded[par], 32 * len(range(par, NU + SPARE, 2)))

                steps(sp, first, body, last)

            @block.tensor
            def _(pe):
                def free(s, job):
                    step, slot = PREV[SLOT_OF[job]]
                    prev = PADDED[slot]
                    r = READER[prev]
                    if not (isinstance(s.i, int) and s.c + step < 0):
                        pe.wait_ge(done[r], s.at(per[r], count_of(r, prev), -step))
                    return bank_of(s, job)

                def projection(pb, k, par):
                    c = slice(k * 288, (k + 1) * 288)
                    nc.tensor.matmul(pb[:, 0:288], hA[par][:], WqkvA[:, c], start=True, stop=False)
                    return nc.tensor.matmul(pb[:, 0:288], hB[par][:], WqkvB[:, c], start=False, stop=True)

                def proj(s):
                    pe.wait_ge(h_loaded[1 - s.n], s.i * 32 + 32 * ((s.c + 1) // 2 + 1))
                    for k in range(2):
                        projection(free(s, f"proj{k}"), k, 1 - s.n).then_inc(pe_filled, 1)

                def transposes(s, job, k, src, blocks):
                    pb = free(s, f"{job}{k}")
                    for m, h in enumerate(blocks):
                        q = nc.tensor.transpose(head(pb, m, P), head(src, h, P), ident[:])
                    q.then_inc(pe_filled, 1)

                def kq(s):
                    pe.wait_ge(pool_done, pool_at(s, "k_bd"))
                    for k in range(3):
                        transposes(s, "kqT", k, K_bd[s.n], range(4 * k, 4 * k + 4))
                    pe.wait_ge(pool_done, pool_at(s, "q_bd"))
                    for k in range(3):
                        transposes(s, "kqT", 3 + k, Q_bd, range(4 * k, 4 * k + 4))

                def w2T(s):
                    transposes(s, "w2T", 0, W2s[s.p], range(4))
                    transposes(s, "w2T", 1, W2s[s.p], range(4, 6))

                def m1(s):
                    pe.wait_ge(act_done, act_at(s, "kqT5"))
                    for k in range(3):
                        pb = free(s, f"m1{k}")
                        for m in range(4):
                            h = 4 * k + m
                            q = nc.tensor.matmul(head(pb, m, P), head(KT, h, P), head(QT[s.n], h, P), start=True, stop=True)
                        q.then_inc(pe_filled, 1)

                def z1(s):
                    if not (isinstance(s.i, int) and s.c == 0):
                        pe.wait_ge(dve_done, dve_at(s, "w11", 1))
                    in_pairs(s, "z1", lambda o, h, **kw: nc.tensor.matmul(o, head(W1s[s.n], h, F), head(KT, h, P), **kw))

                def in_pairs(s, job, *products):
                    for k, qs in enumerate((range(4), range(4, 6))):
                        pb = free(s, f"{job}{k}")
                        for m, q2 in enumerate(qs):
                            for n, product in enumerate(products):
                                for par in range(2):
                                    q = product(pb[rows_of(par), m * P:(m + 1) * P], 2 * q2 + par,
                                                start=(n == 0), stop=(n == len(products) - 1))
                        q.then_inc(pe_filled, 1)

                def by64(s, job, product):
                    for k, hs in enumerate((range(8), range(8, 12))):
                        pb = free(s, f"{job}{k}")
                        for m, h in enumerate(hs):
                            q = product(head(pb, m, F), h)
                        q.then_inc(pe_filled, 1)

                def x2(s):
                    pe.wait_ge(dve_done, dve_at(s, "gelu"))
                    transposes(s, "x2", 0, X2T[s.n], range(4))
                    transposes(s, "x2", 1, X2T[s.n], range(4, 6))

                def split_jobs(s, job, product):
                    for k in range(4):
                        pb = free(s, f"{job}{k}")
                        for m, h in enumerate(SPLIT[k]):
                            q = product(head(pb, m, P), h)
                        q.then_inc(pe_filled, 1)

                def attn2(s):
                    pe.wait_ge(act_done, act_at(s, "gelu_b", 1))
                    split_jobs(s, "attn", lambda o, h: nc.tensor.matmul(
                        o, head(X2T[s.p][rows_of(h)], h // 2, P), head(XbT[rows_of(h)], h // 2, P), start=True, stop=True))

                def z2b(s):
                    split_jobs(s, "z2b", lambda o, h: nc.tensor.matmul(
                        o, head(XbT[rows_of(h)], h // 2, P), head(W2s[s.p][rows_of(h)], h // 2, P), start=True, stop=True))

                def m2(s):
                    pe.wait_ge(dve_done, dve_at(s, "attn3"))
                    pb = free(s, "m20")
                    for h in range(NH):
                        r = QUARTER * (h % 4)
                        q = nc.tensor.matmul(pb[r:r + QUARTER, (h // 4) * P:(h // 4 + 1) * P],
                                             G2[s.p][:, h * D:h * D + QUARTER], head(M2T, PLACE[h], P), start=True, stop=True)
                    q.then_inc(pe_filled, 1)

                def m2T(s):
                    pe.wait_ge(act_done, act_at(s, "m20"))
                    transposes(s, "m2T", 0, own_T, range(NH // 4))

                def w2(s):
                    for k, qs in enumerate((range(4), range(4, 6))):
                        pb = free(s, f"w2{k}")
                        for m, q2 in enumerate(qs):
                            for par in range(2):
                                h = 2 * q2 + par
                                q = nc.tensor.matmul(pb[rows_of(par), m * P:(m + 1) * P], head(X2[s.p], h, F),
                                                     head(G2bd[s.p], h, P), start=True, stop=True)
                        if k == 1:
                            q = nc.tensor.matmul(pb[:, 2 * P:2 * P + HD], neg_last[:], G2[s.p][:, 0:HD], start=True, stop=True)
                        q.then_inc(pe_filled, 1)

                def skip(s, a, b=None):
                    pe.wait_ge(pe_filled, s.at(NJ, SLOTS.index(a)))
                    pe.sem_inc(pe_filled, (SLOTS.index(b) if b else NJ) - SLOTS.index(a))

                def first(s):
                    skip(s, "z20", "kqT0")
                    kq(s)
                    skip(s, "z2b0", "m10")
                    m1(s)
                    skip(s, "gT0", "z10")
                    z1(s)
                    skip(s, "gx0", "proj0")
                    proj(s)
                    skip(s, "g10", "w2T0")
                    w2T(s)
                    skip(s, "z1b0", "x20")
                    x2(s)

                def body(s):
                    split_jobs(s, "z2", lambda o, h: nc.tensor.matmul(
                        o, head(X2T[s.u][rows_of(h)], h // 2, P), head(W2s[s.u][rows_of(h)], h // 2, P), start=True, stop=True))
                    attn2(s)
                    kq(s)
                    z2b(s)
                    m2(s)
                    w2(s)
                    m2T(s)
                    m1(s)
                    pe.wait_ge(dve_done, dve_at(s, "g2_bd"))
                    for k in range(3):
                        transposes(s, "gT", k, G2bd[s.u], range(4 * k, 4 * k + 4))
                    z1(s)
                    pe.wait_ge(act_done, act_at(s, "gT2"))
                    in_pairs(s, "gx", lambda o, h, **kw: nc.tensor.matmul(o, head(W2T[s.u], h, F), head(GT, h, P), **kw))
                    proj(s)
                    pe.wait_ge(dve_done, dve_at(s, "gx1"))
                    transposes(s, "g1", 0, G1T, range(4))
                    transposes(s, "g1", 1, G1T, range(4, 6))
                    pe.wait_ge(dve_done, dve_at(s, "w21"))
                    w2T(s)
                    pe.wait_ge(act_done, act_at(s, "g11"))
                    in_pairs(s, "z1b", lambda o, h, **kw: nc.tensor.matmul(o, head(W1s[s.u], h, F), head(QT[s.u], h, P), **kw),
                             lambda o, h, **kw: nc.tensor.matmul(o, head(G1, h, F), head(M1T[s.u], h, P), **kw))
                    by64(s, "w1", lambda o, h: nc.tensor.matmul(o, head(K_bd[s.u], h, P), head(G1, h, F), start=True, stop=True))
                    x2(s)

                def last(s):
                    skip(s, "z20", "attn0")
                    attn2(s)
                    skip(s, "kqT0", "z2b0")
                    z2b(s)
                    m2(s)
                    skip(s, "w20", "m2T0")
                    m2T(s)

                pe.wait_ge(consts_loaded, n_consts)
                pe.wait_ge(h_loaded[0], 32)
                for k in range(2):
                    projection(bank[k], k, 0).then_inc(first_projected, 1)
                pe.wait_ge(consts_made, 4)
                pe.wait_ge(state_made, 12)
                pe.wait_ge(first_copied, 3)
                steps(pe, first, body, last)

            @block.scalar
            def _(act):
                def skip(s, a, b=None):
                    act.wait_ge(act_done, s.at(per["act"], ACT_STEPS.index(a)))
                    act.sem_inc(act_done, (ACT_STEPS.index(b) if b else len(ACT_STEPS)) - ACT_STEPS.index(a))

                def evac(s, job, dst, width=BANK, **kw):
                    act.wait_ge(pe_filled, pe_at(s, job))
                    nc.scalar.activation(dst, bank_of(s, job)[:, 0:width], ACT.Copy, **kw).then_inc(act_done, 1)

                def proj(s):
                    act.wait_ge(pool_done, pool_at(s, "k_bd"))
                    act.wait_ge(q_stored, s.at(16, 16))
                    for k in range(2):
                        evac(s, f"proj{k}", QKV[:, k * 288:(k + 1) * 288], 288)

                def kq(s):
                    for k in range(3):
                        evac(s, f"kqT{k}", KT[:, k * BANK:(k + 1) * BANK])
                    for k in range(3):
                        evac(s, f"kqT{3 + k}", QT[s.n][:, k * BANK:(k + 1) * BANK])

                def wide(s, job, dst, **kw):
                    evac(s, f"{job}0", dst[:, 0:BANK], **kw)
                    evac(s, f"{job}1", dst[:, BANK:HF], HF - BANK, **kw)

                def square(s):
                    act.wait_ge(dve_done, dve_at(s, "z11"))
                    nc.scalar.activation(x_sq[:], x[:], ACT.Square).then_inc(act_done, 1)
                    act.wait_ge(act_done, act_at(s, "sq"))
                    nc.scalar.activation(cube[:], x_sq[:], ACT.Copy, bias=1.0, scale=GELU_A).then_inc(act_done, 1)
                    nc.scalar.activation(x_half[:], x[:], ACT.Copy, scale=0.5).then_inc(act_done, 1)
                    nc.scalar.activation(slope[:], x_sq[:], ACT.Copy, bias=2 * GELU_C, scale=2 * GELU_D).then_inc(act_done, 1)

                def tanh(s):
                    act.wait_ge(dve_done, dve_at(s, "arg"))
                    nc.scalar.activation(th[:], arg[:], ACT.Tanh, scale=GELU_C).then_inc(act_done, 1)

                def z2b(s):
                    if not (isinstance(s.i, int) and s.c == 1):
                        act.wait_ge(pool_done, pool_at(s, "zb_own", 1))
                    for k in range(4):
                        act.wait_ge(pe_filled, pe_at(s, f"z2b{k}"))
                        nc.scalar.activation(split_view(Zb[:], k), split_bank(bank_of(s, f"z2b{k}"), k),
                                             ACT.Copy).then_inc(act_done, 1)

                def own_product(s):
                    evac(s, "m20", own_T[:], NH // 4 * P)
                    act.wait_ge(pe_filled, pe_at(s, "m2T0"))
                    quarters = bank_of(s, "m2T0")[:, 0:NH // 4 * P].rearrange("p (h r) -> p h r", r=QUARTER)
                    nc.scalar.activation(own_part[:].rearrange("p (h d) -> p h d", d=D), quarters[:, :, 0:D],
                                         ACT.Copy).then_inc(act_done, 1)

                def first(s):
                    kq(s)
                    skip(s, "z2b0", "proj0")
                    proj(s)
                    skip(s, "g10", "w2T0")
                    wide(s, "w2T", W2T[s.p])
                    square(s)
                    tanh(s)
                    skip(s, "gelu_b", "x20")
                    wide(s, "x2", X2[s.n])

                def body(s):
                    kq(s)
                    z2b(s)
                    own_product(s)
                    for k in range(3):
                        evac(s, f"gT{k}", GT[:, k * BANK:(k + 1) * BANK])
                    proj(s)
                    wide(s, "g1", G1)
                    wide(s, "w2T", W2T[s.p])
                    square(s)
                    tanh(s)
                    act.wait_ge(dve_done, dve_at(s, "z1b1"))
                    nc.scalar.activation(XbT[:], xb[:], ACT.Gelu_apprx_tanh).then_inc(act_done, 1)
                    wide(s, "x2", X2[s.n])

                def last(s):
                    skip(s, "kqT0", "m20")
                    act.wait_ge(pool_done, pool_at(s, "zb_own", 1))
                    own_product(s)

                for k in range(2):
                    act.wait_ge(first_projected, k + 1)
                    nc.scalar.activation(QKV[:, k * 288:(k + 1) * 288], bank[k][:, 0:288], ACT.Copy).then_inc(first_copied, 1)
                act.wait_ge(state_made, 12)
                nc.scalar.activation(XbT[:], xb[:], ACT.Gelu_apprx_tanh).then_inc(first_copied, 1)
                steps(act, first, body, last)

            @block.gpsimd
            def _(pool):
                TT = nc.gpsimd.tensor_tensor

                def skip(s, a, b=None):
                    pool.wait_ge(pool_done, s.at(per["pool"], POOL_STEPS.index(a)))
                    pool.sem_inc(pool_done, (POOL_STEPS.index(b) if b else len(POOL_STEPS)) - POOL_STEPS.index(a))

                def step(ins):
                    ins.then_inc(pool_done, 1)

                def masked(dst, src):
                    step(TT(dst[:].rearrange("p (h b d) -> p h b d", h=NH, b=BH),
                            bcast(src.rearrange("p (h d) -> p h d", h=NH), 2, BH),
                            bcast(block_mask[:].rearrange("p (b d) -> p b d", b=BH), 1, NH), ALU.mult))

                def inputs(s):
                    Q, K, V = (QKV[:, k * W:(k + 1) * W] for k in range(3))
                    masked(Q_bd, Q)
                    step(TT(tt[:], K, V, ALU.subtract))
                    pool.wait_ge(pool_done, pool_at(s, "t0"))
                    step(TT(tt[:], tt[:], lnb[:], ALU.add))
                    pool.wait_ge(pool_done, pool_at(s, "t1"))
                    step(TT(target[s.n][:], tt[:], lnw[:], ALU.mult))
                    step(nc.gpsimd.tensor_copy(b2_copy[:], b2s[s.p][:]))
                    if not (isinstance(s.i, int) and s.c == 0):
                        pool.wait_ge(pe_filled, pe_at(s, "w11", 1))
                    masked(K_bd[s.n], K)

                def output(s):
                    pool.wait_ge(act_done, act_at(s, "z2b3"))
                    step(TT(Zb[:].rearrange("p (h n) -> p h n", n=P), Zb[:].rearrange("p (h n) -> p h n", n=P),
                            bcast(block_mask[:, :], 1, NH), ALU.mult))
                    by_image = Zb[:].rearrange("p (h b d) -> p h b d", h=NH, b=BH)
                    n = BH
                    for name in ("zb_mask", "zb_half", "zb_quarter"):
                        pool.wait_ge(pool_done, pool_at(s, name))
                        n //= 2
                        if n > 1:
                            step(TT(by_image[:, :, 0:n], by_image[:, :, 0:n], by_image[:, :, n:2 * n], ALU.add))
                        else:
                            step(TT(out[s.p][:].rearrange("p (h d) -> p h d", h=NH), by_image[:, :, 0], by_image[:, :, 1],
                                    ALU.add))
                    pool.wait_ge(pool_done, pool_at(s, "zb_fold"))
                    pool.wait_ge(act_done, act_at(s, "m2T0"))
                    step(TT(out[s.p][:], out[s.p][:], own_part[:], ALU.add))
                    pool.wait_ge(pool_done, pool_at(s, "zb_own"))
                    step(TT(out[s.p][:], out[s.p][:], b2_copy[:], ALU.add))

                def first(s):
                    pool.wait_ge(first_copied, 2)
                    inputs(s)
                    skip(s, "zb_mask")

                def body(s):
                    pool.wait_ge(act_done, act_at(s, "proj1", 1))
                    pool.wait_ge(pe_filled, pe_at(s, "kqT5", 1))
                    pool.wait_ge(dve_done, dve_at(s, "g2", 1))
                    inputs(s)
                    pool.wait_ge(out_stored[s.p], s.i * 16 + 16)
                    output(s)

                def last(s):
                    pass

                pool.wait_ge(consts_loaded, n_consts)
                for t in (X2T[1], X2[1], G2bd[1]):
                    nc.gpsimd.memset(t[:], 0.0).then_inc(state_made, 1)
                steps(pool, first, body, last)

            @block.vector
            def _(dve):
                def skip(s, a, b=None):
                    dve.wait_ge(dve_done, s.at(per["dve"], DVE_STEPS.index(a)))
                    dve.sem_inc(dve_done, (DVE_STEPS.index(b) if b else len(DVE_STEPS)) - DVE_STEPS.index(a))

                def own(s, name):
                    dve.wait_ge(dve_done, dve_at(s, name))

                def step(ins):
                    ins.then_inc(dve_done, 1)

                V = nc.vector
                by_head = lambda ap: ap.rearrange("p (h d) -> p h d", h=NH)
                stat = lambda k: bcast(st[:, k, :], 2, D)

                def halves(s, job, emit):
                    for k, c in enumerate((slice(0, BANK), slice(BANK, HF))):
                        dve.wait_ge(pe_filled, pe_at(s, f"{job}{k}"))
                        step(emit(c, bank_of(s, f"{job}{k}")[:, 0:c.stop - c.start]))

                def attention(s, k):
                    dve.wait_ge(pe_filled, pe_at(s, f"attn{k}"))
                    n0 = PLACE[SPLIT[k][0]] * P
                    step(V.scalar_tensor_tensor(heads4(M2T[:, n0:n0 + len(SPLIT[k]) * P]),
                                                split_bank(bank_of(s, f"attn{k}"), k), 1.0,
                                                split_mask(neg_tril, k), ALU.add, ALU.mult))

                def first(s):
                    skip(s, "z20", "m10")
                    m1(s)
                    skip(s, "db", "z10")
                    hidden(s)
                    argument(s)
                    skip(s, "z1b0", "gelu")
                    gelu(s)
                    skip(s, "b1_sum")

                def m1(s):
                    for k in range(3):
                        dve.wait_ge(pe_filled, pe_at(s, f"m1{k}"))
                        step(V.scalar_tensor_tensor(heads4(M1T[s.n][:, k * BANK:(k + 1) * BANK]),
                                                    heads4(bank_of(s, f"m1{k}")[:, :]), 1.0,
                                                    bcast(neg_tril[:, :], 1, 4), ALU.add, ALU.mult))

                def with_bias(s, job, dst, par):
                    def add(c, pb):
                        pair = lambda ap: ap.rearrange("p (n k) -> p n k", k=MB)
                        n = slice(c.start // MB, c.stop // MB)
                        return V.tensor_tensor(pair(dst[:, c]), pair(pb), bcast(b1s[par][:, n], 2, MB), ALU.add)
                    halves(s, job, add)

                def hidden(s):
                    with_bias(s, "z1", x, s.n)

                def argument(s):
                    dve.wait_ge(act_done, act_at(s, "cube"))
                    step(V.tensor_tensor(arg[:], cube[:], x[:], ALU.mult))

                def gelu(s):
                    dve.wait_ge(act_done, act_at(s, "tanh"))
                    step(V.scalar_tensor_tensor(X2T[s.n][:], th[:], 1.0, x_half[:], ALU.add, ALU.mult))

                def body(s):
                    for k in range(4):
                        dve.wait_ge(pe_filled, pe_at(s, f"z2{k}"))
                        step(V.tensor_tensor(split_view(Zm[:], k), split_bank(bank_of(s, f"z2{k}"), k),
                                             split_mask(block_mask, k), ALU.mult))
                    own(s, "z23")
                    step(V.tensor_reduce(z[:], Zm[:].rearrange("p (h b d) -> p h d b", h=NH, b=BH), AX, ALU.add))
                    attention(s, 0)
                    own(s, "z2_fold")
                    step(V.tensor_tensor(z[:], z[:], b2s[s.u][:], ALU.add))
                    attention(s, 1)
                    own(s, "z2_bias")
                    step(V.tensor_reduce(st[:, 0, :], by_head(z[:]), AX, ALU.add))
                    attention(s, 2)
                    own(s, "mean")
                    step(V.scalar_tensor_tensor(by_head(zc[:]), stat(0), -1.0 / D, by_head(z[:]), ALU.mult, ALU.add))
                    attention(s, 3)
                    own(s, "center")
                    step(V.tensor_tensor(zs[:], zc[:], zc[:], ALU.mult))
                    own(s, "square")
                    step(V.tensor_reduce(st[:, 1, :], by_head(zs[:]), AX, ALU.add))
                    own(s, "var")
                    rsqrt(nc, step, lambda name: own(s, name), st[:, 2, :], st[:, 6, :], st[:, 7, :], st[:, 1, :],
                          D * EPS_INNER, "r_")
                    step(V.scalar_tensor_tensor(by_head(xh[:]), by_head(zc[:]), float(D) ** 0.5, stat(2), ALU.mult, ALU.mult))
                    own(s, "xhat")
                    step(V.tensor_tensor(zs[:], xh[:], lnw2[:], ALU.mult))
                    own(s, "gxh0")
                    dve.wait_ge(pool_done, pool_at(s, "t2", 1))
                    step(V.tensor_tensor(g[:], zs[:], target[s.u][:], ALU.add))
                    own(s, "gxh")
                    step(V.tensor_reduce(st[:, 3, :], by_head(g[:]), AX, ALU.add))
                    step(V.tensor_tensor(zs[:], g[:], xh[:], ALU.mult))
                    own(s, "gx_xh")
                    step(V.tensor_reduce(st[:, 4, :], by_head(zs[:]), AX, ALU.add))
                    unit = s.i * (2 * NH) + (s.c - 1) * NH
                    step(V.scalar_tensor_tensor(st[:, 5, :], st[:, 2, :], float(D) ** 0.5, LR[:, bass.ds(unit, NH)],
                                                ALU.mult, ALU.mult))
                    own(s, "s2")
                    step(V.tensor_tensor(by_head(zc[:]), by_head(xh[:]), stat(4), ALU.mult))
                    step(V.scalar_tensor_tensor(by_head(g[:]), stat(3), -1.0 / D, by_head(g[:]), ALU.mult, ALU.add))
                    own(s, "sub1")
                    step(V.scalar_tensor_tensor(g[:], zc[:], -1.0 / D, g[:], ALU.mult, ALU.add))
                    own(s, "sub2")
                    step(V.tensor_tensor(by_head(G2[s.u][:, 0:HD]), by_head(g[:]), stat(5), ALU.mult))
                    own(s, "g2")
                    step(V.tensor_tensor(G2bd[s.u][:].rearrange("p (h b d) -> p h b d", h=NH, b=BH),
                                         bcast(by_head(G2[s.u][:, 0:HD]), 2, BH),
                                         bcast(block_mask[:].rearrange("p (b d) -> p b d", b=BH), 1, NH), ALU.mult))
                    halves(s, "w2", lambda c, pb: V.scalar_tensor_tensor(
                        W2s[s.p][:, c], pb, last_col[:, 0:1], W2s[s.p][:, c], ALU.mult, ALU.add))
                    dve.wait_ge(pool_done, pool_at(s, "b2_copy"))
                    step(V.tensor_tensor(b2s[s.p][:], bank_of(s, "w21")[:, 2 * P:2 * P + HD], b2s[s.p][:], ALU.add))
                    m1(s)
                    step(V.scalar_tensor_tensor(tmp[:], th[:], 1.0, slope[:], ALU.subtract, ALU.mult))
                    own(s, "db")
                    step(V.tensor_tensor(tmp[:], tmp[:], X2T[s.u][:], ALU.mult))
                    own(s, "dc")
                    step(V.scalar_tensor_tensor(dg[:], th[:], 1.0, tmp[:], ALU.add, ALU.subtract))
                    own(s, "dgelu")
                    halves(s, "gx", lambda c, pb: V.scalar_tensor_tensor(G1T[:, c], pb, 0.5, dg[:, c], ALU.mult, ALU.mult))
                    hidden(s)
                    argument(s)
                    dve.wait_ge(act_done, act_at(s, "gelu_b", 1))
                    with_bias(s, "z1b", xb, s.u)
                    gelu(s)
                    step(V.tensor_reduce(b1_sum[:], G1T[:].rearrange("p (n k) -> p n k", k=MB), AX, ALU.add))
                    own(s, "b1_sum")
                    step(V.scalar_tensor_tensor(b1s[s.u][:], b1_sum[:], last_col[:, 0:1], b1s[s.u][:], ALU.mult, ALU.add))
                    halves(s, "w1", lambda c, pb: V.scalar_tensor_tensor(
                        W1s[s.u][:, c], pb, last_col[:, 0:1], W1s[s.u][:, c], ALU.mult, ALU.add))

                def last(s):
                    for k, (before, after) in enumerate((("z20", "attn0"), ("z2_bias", "attn1"), ("mean", "attn2"),
                                                         ("center", "attn3"))):
                        skip(s, before, after)
                        attention(s, k)
                    skip(s, "square")
                    for k in range(4):
                        dve.wait_ge(pe_filled, pe_at(s, f"z2b{k}"))
                        V.tensor_tensor(split_view(Zm[:], k), split_bank(bank_of(s, f"z2b{k}"), k),
                                        split_mask(block_mask, k), ALU.mult).then_inc(last_made, 1)
                    dve.wait_ge(last_made, 4)
                    V.tensor_reduce(z[:], Zm[:].rearrange("p (h b d) -> p h d b", h=NH, b=BH), AX, ALU.add).then_inc(last_made, 1)
                    dve.wait_ge(last_made, 5)
                    V.tensor_tensor(z[:], z[:], b2s[s.p][:], ALU.add).then_inc(last_made, 1)
                    dve.wait_ge(last_made, 6)
                    dve.wait_ge(act_done, act_at(s, "m2T0"))
                    dve.wait_ge(out_stored[s.p], 16 * (NU // 2 + 1))
                    V.tensor_tensor(out[s.p][:], z[:], own_part[:], ALU.add).then_inc(last_made, 1)

                dve.wait_ge(consts_loaded, n_consts)
                made = [0]

                def make(ins, wait=True):
                    ins.then_inc(consts_made, 1)
                    made[0] += 1
                    if wait:
                        dve.wait_ge(consts_made, made[0])
                make(V.tensor_tensor(tok[:], tok[:], recip[:], ALU.add))
                make(V.tensor_scalar(tok[:], tok[:], 0.0, None, ALU.max))
                make(V.scalar_tensor_tensor(neg_tril[:].rearrange("p (b k) -> p b k", b=BH),
                                            neg_tril[:].rearrange("p (b k) -> p b k", b=BH), -1.0,
                                            bcast(tok[:, :], 1, BH), ALU.mult, ALU.mult))
                make(V.tensor_scalar(last_col[:], tok[:, MB - 1:MB], -1.0, None, ALU.mult))
                V.tensor_scalar(neg_last[:], block_mask[:], last_col[:, 0:1], None, ALU.mult).then_inc(state_made, 1)
                for k in range(2):
                    V.tensor_copy(W2s[k][:].rearrange("p (q b d) -> p q b d", q=NH // 2, b=BH),
                                  bcast(w2_small[:], 2, BH)).then_inc(state_made, 1)
                    V.tensor_copy(b1s[k][:].rearrange("p (q b) -> p q b", b=BH),
                                  bcast(b1_small[:], 2, BH)).then_inc(state_made, 1)
                V.tensor_tensor(lnw2[:], lnw[:], lnw[:], ALU.mult).then_inc(state_made, 1)
                for t in (xb, G2[0], G2[1]):
                    V.memset(t[:], 0.0).then_inc(state_made, 1)
                dve.wait_ge(state_made, 12)
                steps(dve, first, body, last)


GU = 4
NG = NU // GU
SIDE_PE = ["gate0", "gate1", "h2T0", "h2T1", "hidden", "oT0", "oT1", "logits", "h0", "h1"]
SIDE_ACT = ["square", "gate0", "gate1", "h2T0", "h2T1", "hidden", "oT0", "oT1", "exp"]
SIDE_POOL = ["query_beta", "xhat", "scale", "attention", "gate_weight", "gate_bias"]
ROUTER = (["r_copy", "r_max", "r_shift", "r_sum", "r_inverse", "r_softmax", "r_left"]
          + [f"r_{n}{k}" for k in range(2) for n in ("best", "equal", "rank", "first", "chosen", "drop")]
          + ["r_picked", "r_gates", "r_total", "r_guard", "r_scale", "r_final"])
SIDE_DVE = (["i_mean", "i_center"] + [f"o_bn{j}" for j in range(GU)] + [f"h_bn{j}" for j in range(GU)] + ["i_var"]
            + ["sum", "diff", "m2", "between", "eps_i", "eps_o", "eps_h", "s_var"] + inverse_root_steps("s_") + ["shift"]
            + [f"h_norm{j}" for j in range(GU)] + [f"o_norm{j}" for j in range(GU)] + ["weight", "bias"] + ROUTER)


def ln_steps(tag):
    return ([f"{tag}bn{j}" for j in range(GU)] + [f"{tag}{x}" for x in ("sum", "diff", "m2", "between", "var")] + rsqrt_steps(tag) + [f"{tag}shift"]
            + [f"{tag}norm{j}" for j in range(GU)])


MDVE = [f"y{e}_{j}" for e in range(E) for j in range(GU)]
FINAL = ln_steps("m_") + ["gamma", "beta", "residual"] + ln_steps("f_")
MPE = []
for _e in range(E + 1):
    if _e < E:
        MPE += [f"z{2 * _e}", f"z{2 * _e + 1}"]
    if _e > 0:
        MPE += [f"y{_e - 1}_0", f"y{_e - 1}_1"]
MACT = [f"z{c}" for c in range(EC)]


class Group:
    def __init__(self, i, c):
        self.i, self.c, self.par = i, c, c % 2

    def before(self, d):
        return Group(self.i, self.c - d)

    def loads(self, each):
        return self.i * (16 * each) + 16 * each * (self.c // 2 + 1)

    def at(self, names, name, back=0):
        each = len(names)
        return self.i * (2 * each) + each * (self.c + 1 - back) + names.index(name) + 1

    def row(self, n, first=0):
        return bass.ds(self.i * (2 * GU * n) + (self.c * GU * n + first), GU * n)


DELAYS = 5


def rounds(eng, body):
    assert NG % 2 == 0 and NG > DELAYS - 1
    peeled = lambda k: body(Group(0, k), [0 <= k - d < NG for d in range(DELAYS)])
    for k in range(DELAYS - 1):
        peeled(k)
    with eng.Fori(0, (NG - DELAYS + 1) // 2) as i:
        for c in range(2):
            body(Group(i, DELAYS - 1 + c), [True] * DELAYS)
    for k in range(NG, NG + DELAYS - 1):
        peeled(k)


def layer_norm(nc, step, own, src, dst, stats, mv, rs, eps, tag):
    V = nc.vector
    for j in range(GU):
        step(V.bn_stats(stats[:, j, :], src(j)))
    own(f"{tag}bn{GU - 1}")
    mean2, diff, m2, var = (mv[:, k, :] for k in range(4))
    step(V.tensor_tensor(mean2, stats[:, :, 1], stats[:, :, 4], ALU.add))
    step(V.tensor_tensor(diff, stats[:, :, 1], stats[:, :, 4], ALU.subtract))
    step(V.tensor_tensor(m2, stats[:, :, 2], stats[:, :, 5], ALU.add))
    own(f"{tag}m2")
    step(V.scalar_tensor_tensor(diff, diff, 0.25, diff, ALU.mult, ALU.mult))
    own(f"{tag}between")
    step(V.scalar_tensor_tensor(var, m2, 1.0 / W, diff, ALU.mult, ALU.add))
    own(f"{tag}var")
    rsqrt(nc, step, own, rs[:, 0, :], rs[:, 1, :], rs[:, 2, :], var, eps, tag)
    step(V.scalar_tensor_tensor(rs[:, 3, :], mean2, -0.5, rs[:, 0, :], ALU.mult, ALU.mult))
    own(f"{tag}shift")
    for j in range(GU):
        step(V.tensor_scalar(dst(j), src(j), rs[:, 0, j:j + 1], rs[:, 3, j:j + 1], ALU.mult, ALU.add))
    own(f"{tag}norm{GU - 1}")


def output_weights(nc, A, ctx):
    sb = lambda name, shape: ctx.enter_context(nc.sbuf_tensor(name, shape, F32))
    tensors = (sb("WgA", [P, W]), sb("WgB", [WB, W]), sb("WoA", [P, W]), sb("WoB", [WB, W]),
               sb("pw", [P, W]), sb("pb", [P, W]), sb("lnw3", [P, W]), sb("lnb3", [P, W]))
    sources = (A["Wg"][0:P, :], A["Wg"][P:W, :], A["Wo"][0:P, :], A["Wo"][P:W, :],
               A["pw"].broadcast_to([P, W]), A["pb"].broadcast_to([P, W]),
               A["lnw"].broadcast_to([P, W]), A["lnb"].broadcast_to([P, W]))
    return {"tensors": tensors, "loads": [(t[:], src) for t, src in zip(tensors, sources)],
            "loaded": ctx.enter_context(nc.semaphore("out_weights_loaded"))}


def outputs(nc, A, hT, attn, q_dram, out_dram, ident, weights):
    with ExitStack() as ctx:
        sb = lambda name, shape: ctx.enter_context(nc.sbuf_tensor(name, shape, F32))
        two = lambda name, shape: [sb(f"{name}_{i}", shape) for i in range(2)]
        sem = lambda name: ctx.enter_context(nc.semaphore(name))
        HR, GH, NS_ = W // 2, GU * NH, 2 * GU
        (WgA, WgB, WoA, WoB, pw, pb_, lnw, lnb), weights_loaded = weights["tensors"], weights["loaded"]
        gamma, beta = sb("gamma", [P, W]), sb("beta", [P, W])
        w1A, w1B, w2r = sb("w1A", [P, HR]), sb("w1B", [WB + 1, HR]), sb("w2r", [HR + 1, E])
        downA, downB = sb("downA", [P, E * DE]), sb("downB", [WB + 1, E * DE])
        up = sb("up", [P, EC, W])
        rank = sb("rank", [P, E])
        O, Qr, hA, hB = two("O", [P, GU, W]), two("Qr", [P, GU, W]), two("ghA", [P, GU, P]), two("ghB", [WB, GU, P])
        sq, head_sum = sb("sq3", [P, GU, W]), sb("head_sum", [P, 2, GH])
        gate, gate_w, gate_b = sb("gate", [P, GU, W]), two("gate_w", [P, GU, W]), two("gate_b", [P, GU, W])
        normed = sb("normed", [P, GU, W])
        oTA, oTB = sb("oTA", [P, GU * P]), sb("oTB", [WB, GU * P])
        side_stats, side_mv, shift = sb("side_stats", [P, NS_, 6]), sb("side_mv", [P, 3, NS_]), sb("shift", [P, NS_])
        var, rstd, root_tmp = sb("var", [P, GH + NS_]), sb("rstd", [P, GH + NS_]), sb("root_tmp", [P, GH + NS_])
        h2 = two("h2", [P, GU, W])
        H2TA, H2TB = two("H2TA", [P, GU * P]), two("H2TB", [WB + 1, GU * P])
        router = sb("router", [HR + 1, GU * P])
        gates, logit, picked, eq, score = (sb(n, [P, GU * E]) for n in ("gates", "logit", "picked", "eq", "score"))
        col = sb("col", [P, 5, GU])
        Z, acc = sb("Z", [P, 4, GU * P]), two("acc", [P, GU, W])
        stats, mv, rs = sb("mstats", [P, GU, 6]), sb("mmv", [P, 4, GU]), sb("mrs", [P, 4, GU])

        bank = [ctx.enter_context(nc.psum_tensor(f"out_bank{i}", [P, BANK], F32)) for i in range(NBANK)]
        z_bank = lambda c: bank[c % 2]
        y_bank = bank[2:4]
        h_bank = bank[4:6]
        turn = {"gate0": bank[6], "gate1": bank[7], "h2T0": bank[6], "h2T1": bank[7], "hidden": bank[6],
                "oT0": bank[7], "oT1": bank[6], "logits": bank[7]}

        router_loaded, experts_loaded = sem("router_loaded"), sem("experts_loaded")
        ones_set, stats_cleared = sem("out_ones_set"), sem("stats_cleared")
        rows_loaded = [sem("rows_loaded0"), sem("rows_loaded1")]
        hT_loaded = [sem("hT_loaded0"), sem("hT_loaded1")]
        out_stored = [sem("y_stored0"), sem("y_stored1")]
        side_pe, side_act, side_dve, side_pool = sem("side_pe"), sem("side_act"), sem("side_dve"), sem("side_pool")
        pe_filled, act_done, dve_done, final_done = sem("m_pe_filled"), sem("m_act_done"), sem("m_dve_done"), sem("final_done")
        unit_pair = lambda pb: pb[:, 0:2 * W].rearrange("p (j n) -> p j n", j=2)
        heads = lambda t: t[:].rearrange("p u k -> p (u k)").rearrange("p (g d) -> p g d", d=D)

        def skipper(eng, counter, names):
            def skip(s, a, b):
                n = (names.index(b) if b else len(names)) - names.index(a)
                eng.wait_ge(counter, s.at(names, a) - 1)
                eng.sem_inc(counter, n)
            return skip

        with nc.Block() as block:
            @block.sync
            def _(sp):
                def load_rows(s):
                    for dst, src in ((O[s.par], attn[s.row(1, 1), :, :].rearrange("u p k -> p u k")),
                                     (Qr[s.par], q_dram[s.row(1), :, :].rearrange("u p k -> p u k"))):
                        sp.dma_start(dst[:], src).then_inc(rows_loaded[s.par], 16)

                def load_hT(s):
                    for dst, src in ((hA[s.par], hT[s.row(1), 0:P, :].rearrange("u f k -> f u k")),
                                     (hB[s.par], hT[s.row(1), P:W, :].rearrange("u f k -> f u k"))):
                        sp.dma_start(dst[:], src).then_inc(hT_loaded[s.par], 16)

                for c in range(2):
                    sp.sem_inc(out_stored[c], 16)
                load_rows(Group(0, 0))
                load_hT(Group(0, 0))
                load_rows(Group(0, 1))
                load_hT(Group(0, 1))
                for dst, src in ((w1A[:], A["fw1"][0:P, :]), (w1B[0:WB, :], A["fw1"][P:W, :]), (w1B[WB:WB + 1, :], A["fb1"]),
                                 (w2r[0:HR, :], A["fw2"]), (w2r[HR:HR + 1, :], A["fb2"]),
                                 (rank[:], A["rank"].broadcast_to([P, E]))):
                    sp.dma_start(dst, src).then_inc(router_loaded, 16)
                dn = A["down"].rearrange("e h d -> h e d")
                for dst, src in ((downA[:].rearrange("p (e d) -> p e d", e=E), dn[0:P]),
                                 (downB[0:WB, :].rearrange("p (e d) -> p e d", e=E), dn[P:W]),
                                 (downB[WB:WB + 1, :], A["downb"]),
                                 (up[:], A["up"].rearrange("(c p) h -> p c h", p=P)),
                                 (gamma[:], A["gamma"].broadcast_to([P, W])), (beta[:], A["beta"].broadcast_to([P, W]))):
                    sp.dma_start(dst, src).then_inc(experts_loaded, 16)

                def body(s, has):
                    if has[0] and not (isinstance(s.i, int) and s.c < 2):
                        sp.wait_ge(side_dve, s.at(SIDE_DVE, f"o_norm{GU - 1}", 1))
                        load_rows(s)
                        sp.wait_ge(side_pe, s.at(SIDE_PE, "h1", 1))
                        load_hT(s)
                    if has[4]:
                        x = s.before(4)
                        sp.wait_ge(final_done, x.at(FINAL, f"f_norm{GU - 1}"))
                        sp.dma_start(out_dram[x.row(1), :, :].rearrange("u p k -> p u k"), acc[x.par][:]).then_inc(
                            out_stored[x.par], 16)
                rounds(sp, body)
                for c in range(2):
                    sp.wait_ge(out_stored[c], 16 * (NG // 2 + 1))

            @block.tensor
            def _(pe):
                skip = skipper(pe, side_pe, SIDE_PE)
                pe.sem_inc(side_pe, len(SIDE_PE))
                pe.sem_inc(pe_filled, len(MPE))
                pe.wait_ge(weights_loaded, 16 * 8)

                def transposes(src, names):
                    for name, (f0, f1) in zip(names, ((0, P), (P, W))):
                        for j in range(GU):
                            q = nc.tensor.transpose(turn[name][0:f1 - f0, j * P:(j + 1) * P], src[:, j, f0:f1], ident[:])
                        q.then_inc(side_pe, 1)

                def gate(s):
                    pe.wait_ge(hT_loaded[s.par], s.loads(2))
                    pe.wait_ge(side_act, s.at(SIDE_ACT, "oT1", 1))
                    pe.wait_ge(side_dve, s.at(SIDE_DVE, "r_copy", 1))
                    for k in range(2):
                        for m in range(2):
                            j = 2 * k + m
                            o = turn[f"gate{k}"][:, m * W:(m + 1) * W]
                            nc.tensor.matmul(o, hA[s.par][:, j, :], WgA[:], start=True, stop=False)
                            q = nc.tensor.matmul(o, hB[s.par][:, j, :], WgB[:], start=False, stop=True)
                        q.then_inc(side_pe, 1)

                def h2T(s):
                    pe.wait_ge(side_dve, s.at(SIDE_DVE, f"h_norm{GU - 1}"))
                    pe.wait_ge(side_act, s.at(SIDE_ACT, "gate1"))
                    transposes(h2[s.par], ("h2T0", "h2T1"))

                def hidden(s):
                    pe.wait_ge(side_act, s.at(SIDE_ACT, "h2T1"))
                    o = turn["hidden"][0:HR, :]
                    nc.tensor.matmul(o, w1A[:], H2TA[s.par][:], start=True, stop=False)
                    nc.tensor.matmul(o, w1B[:], H2TB[s.par][:], start=False, stop=True).then_inc(side_pe, 1)

                def oT(s):
                    pe.wait_ge(side_dve, s.at(SIDE_DVE, "bias"))
                    pe.wait_ge(side_act, s.at(SIDE_ACT, "hidden"))
                    transposes(normed, ("oT0", "oT1"))

                def logits(s):
                    pe.wait_ge(side_act, s.at(SIDE_ACT, "oT0"))
                    for j in range(GU):
                        q = nc.tensor.matmul(turn["logits"][:, j * E:(j + 1) * E], router[:, j * P:(j + 1) * P], w2r[:],
                                             start=True, stop=True)
                    q.then_inc(side_pe, 1)

                def h(s):
                    g = s.before(1)
                    pe.wait_ge(side_act, s.at(SIDE_ACT, "oT1"))
                    pe.wait_ge(side_dve, s.at(SIDE_DVE, f"h_norm{GU - 1}"))
                    for k in range(2):
                        for m in range(2):
                            j = 2 * k + m
                            c = slice(j * P, (j + 1) * P)
                            o = h_bank[k][:, m * W:(m + 1) * W]
                            nc.tensor.matmul(o, oTA[:, c], WoA[:], start=True, stop=False)
                            nc.tensor.matmul(o, oTB[:, c], WoB[:], start=False, stop=False)
                            nc.tensor.matmul(o[:, 0:P], hA[g.par][:, j, :], ident[:], start=False, stop=False)
                            q = nc.tensor.matmul(o[:, P:W], hB[g.par][:, j, :], ident[0:WB, 0:WB], start=False, stop=True)
                        q.then_inc(side_pe, 1)

                def z(x, c):
                    prev = c - 2 if c >= 2 else c - 2 + EC
                    pe.wait_ge(act_done, x.at(MACT, f"z{prev}", 0 if c >= 2 else 1))
                    o, w = z_bank(c)[:, :], slice(c * P, (c + 1) * P)
                    nc.tensor.matmul(o, downA[:, w], H2TA[x.par][:], start=True, stop=False)
                    nc.tensor.matmul(o, downB[:, w], H2TB[x.par][:], start=False, stop=True).then_inc(pe_filled, 1)

                def y(x, e):
                    pe.wait_ge(act_done, x.at(MACT, f"z{2 * e + 1}"))
                    for k in range(2):
                        prev = e - 1 if e >= 1 else e - 1 + E
                        pe.wait_ge(dve_done, x.at(MDVE, f"y{prev}_{2 * k + 1}", 0 if e >= 1 else 1))
                        for m in range(2):
                            j = 2 * k + m
                            o = y_bank[k][:, m * W:(m + 1) * W]
                            for d in range(2):
                                c = 2 * e + d
                                q = nc.tensor.matmul(o, Z[:, c % 4, j * P:(j + 1) * P], up[:, c, :],
                                                     start=(d == 0), stop=(d == 1))
                        q.then_inc(pe_filled, 1)

                def body(s, has):
                    if isinstance(s.i, int) and s.c == 2:
                        pe.wait_ge(router_loaded, 16 * 6)
                        pe.wait_ge(experts_loaded, 16 * 6)
                        pe.wait_ge(ones_set, 3)
                    side = {0: [(0, gate, "gate0")], 5: [(2, h2T, "h2T0")], 6: [(2, hidden, "hidden")], 7: [(1, oT, "oT0")],
                            8: [(2, logits, "logits"), (1, h, "h0")]}
                    starts = [part[2] for e in sorted(side) for part in side[e]] + [None]
                    for e in range(E + 1):
                        if has[3]:
                            if e < E:
                                z(s.before(3), 2 * e)
                                z(s.before(3), 2 * e + 1)
                            if e > 0:
                                y(s.before(3), e - 1)
                        for d, do, name in side.get(e, ()):
                            if has[d]:
                                do(s)
                            else:
                                skip(s, name, starts[starts.index(name) + 1])
                rounds(pe, body)

            @block.scalar
            def _(act):
                skip = skipper(act, side_act, SIDE_ACT)
                act.sem_inc(side_act, len(SIDE_ACT))
                act.sem_inc(act_done, len(MACT))

                def evac(s, name, dst, src, func=ACT.Copy):
                    act.wait_ge(side_pe, s.at(SIDE_PE, name))
                    nc.scalar.activation(dst, src, func).then_inc(side_act, 1)

                def square(s):
                    act.wait_ge(side_dve, s.at(SIDE_DVE, "i_center"))
                    nc.scalar.activation(sq[:], O[s.par][:], ACT.Square).then_inc(side_act, 1)

                def gates_(s):
                    act.wait_ge(side_pool, s.at(SIDE_POOL, "gate_bias", 1))
                    for k in range(2):
                        evac(s, f"gate{k}", gate[:, 2 * k:2 * k + 2, :], unit_pair(turn[f"gate{k}"]), ACT.Gelu_apprx_tanh)

                def h2T(s):
                    evac(s, "h2T0", H2TA[s.par][:], turn["h2T0"][:, :])
                    evac(s, "h2T1", H2TB[s.par][0:WB, :], turn["h2T1"][0:WB, :])

                def hidden(s):
                    evac(s, "hidden", router[0:HR, :], turn["hidden"][0:HR, :], ACT.Gelu)

                def oT(s):
                    evac(s, "oT0", oTA[:], turn["oT0"][:, :])
                    evac(s, "oT1", oTB[:], turn["oT1"][0:WB, :])

                def exp(s):
                    act.wait_ge(side_dve, s.at(SIDE_DVE, "r_shift"))
                    nc.scalar.activation(picked[:], logit[:], ACT.Exp).then_inc(side_act, 1)

                def body(s, has):
                    side = {1: [(0, square, "square"), (0, gates_, "gate0")], 5: [(2, h2T, "h2T0")],
                            6: [(2, hidden, "hidden")], 7: [(1, oT, "oT0"), (2, exp, "exp")]}
                    starts = [part[2] for e in sorted(side) for part in side[e]] + [None]
                    for e in range(E):
                        if has[3]:
                            x = s.before(3)
                            for c in (2 * e, 2 * e + 1):
                                act.wait_ge(pe_filled, x.at(MPE, f"z{c}"))
                                prev = c // 2 - 2
                                act.wait_ge(pe_filled, x.at(MPE, f"y{prev}_1") if prev >= 0 else x.at(MPE, f"y{prev + E}_1", 1))
                                nc.scalar.activation(Z[:, c % 4, :], z_bank(c)[:, :], ACT.Gelu).then_inc(act_done, 1)
                        for d, do, name in side.get(e, ()):
                            if has[d]:
                                do(s)
                            else:
                                skip(s, name, starts[starts.index(name) + 1])
                rounds(act, body)

            @block.gpsimd
            def _(pool):
                skip = skipper(pool, side_pool, SIDE_POOL)
                for k in range(2):
                    nc.gpsimd.memset(H2TB[k][WB:WB + 1, :], 1.0).then_inc(ones_set, 1)
                nc.gpsimd.memset(router[HR:HR + 1, :], 1.0).then_inc(ones_set, 1)
                pool.wait_ge(ones_set, 3)
                pool.sem_inc(side_pool, len(SIDE_POOL))
                pool.wait_ge(weights_loaded, 16 * 8)

                def body(s, has):
                    if not has[0]:
                        skip(s, "query_beta", None)
                        return

                    def op(out, a, b, kind):
                        nc.gpsimd.tensor_tensor(out, a, b, kind).then_inc(side_pool, 1)
                    pool.wait_ge(rows_loaded[s.par], s.loads(2))
                    op(Qr[s.par][:], Qr[s.par][:], bcast(lnb[:, :], 1, GU), ALU.add)
                    pool.wait_ge(side_dve, s.at(SIDE_DVE, "s_newton8"))
                    op(heads(O[s.par]), heads(O[s.par]), bcast(rstd[:, 0:GH], 2, D), ALU.mult)
                    pool.wait_ge(side_pool, s.at(SIDE_POOL, "xhat"))
                    op(O[s.par][:], O[s.par][:], bcast(lnw[:, :], 1, GU), ALU.mult)
                    pool.wait_ge(side_pool, s.at(SIDE_POOL, "scale"))
                    op(O[s.par][:], O[s.par][:], Qr[s.par][:], ALU.add)
                    pool.wait_ge(side_act, s.at(SIDE_ACT, "gate1"))
                    pool.wait_ge(side_dve, s.at(SIDE_DVE, "bias", 1))
                    op(gate_w[s.par][:], gate[:], bcast(pw[:, :], 1, GU), ALU.mult)
                    op(gate_b[s.par][:], gate[:], bcast(pb_[:, :], 1, GU), ALU.mult)
                rounds(pool, body)

            @block.vector
            def _(dve):
                V = nc.vector
                skip = skipper(dve, side_dve, SIDE_DVE)
                V.memset(side_stats[:], 0.0).then_inc(stats_cleared, 1)
                dve.wait_ge(stats_cleared, 1)
                dve.sem_inc(side_dve, len(SIDE_DVE))
                dve.sem_inc(dve_done, len(MDVE))
                dve.sem_inc(final_done, len(FINAL))
                dve.wait_ge(weights_loaded, 16 * 8)
                step = lambda ins: ins.then_inc(side_dve, 1)

                def own(s, name):
                    dve.wait_ge(side_dve, s.at(SIDE_DVE, name))

                def center(s):
                    dve.wait_ge(rows_loaded[s.par], s.loads(2))
                    step(V.tensor_reduce(head_sum[:, 0, :], heads(O[s.par]), AX, ALU.add))
                    own(s, "i_mean")
                    step(V.scalar_tensor_tensor(heads(O[s.par]), bcast(head_sum[:, 0, :], 2, D), -1.0 / D, heads(O[s.par]),
                                                ALU.mult, ALU.add))

                def o_stats(s):
                    dve.wait_ge(side_pool, s.at(SIDE_POOL, "attention", 1))
                    for j in range(GU):
                        step(V.bn_stats(side_stats[:, j, :], O[1 - s.par][:, j, :]))

                def h_stats(s):
                    dve.wait_ge(side_pe, s.at(SIDE_PE, "h1", 1))
                    for j in range(GU):
                        step(V.bn_stats(side_stats[:, GU + j, :], unit_pair(h_bank[j // 2])[:, j % 2, :]))

                def head_var(s):
                    dve.wait_ge(side_act, s.at(SIDE_ACT, "square"))
                    step(V.tensor_reduce(head_sum[:, 1, :], heads(sq), AX, ALU.add))

                def deviations(s, has):
                    own(s, "i_var")
                    mean2, diff, m2 = (side_mv[:, k, :] for k in range(3))
                    step(V.tensor_tensor(mean2, side_stats[:, :, 1], side_stats[:, :, 4], ALU.add))
                    step(V.tensor_tensor(diff, side_stats[:, :, 1], side_stats[:, :, 4], ALU.subtract))
                    step(V.tensor_tensor(m2, side_stats[:, :, 2], side_stats[:, :, 5], ALU.add))
                    own(s, "m2")
                    step(V.scalar_tensor_tensor(diff, diff, 0.25, diff, ALU.mult, ALU.mult))
                    if has[0] or has[1]:
                        dve.wait_ge(side_pool, s.at(SIDE_POOL, "xhat", 1))
                    step(V.tensor_scalar(var[:, 0:GH], head_sum[:, 1, :], 1.0 / D, EPS_INNER, ALU.mult, ALU.add))
                    step(V.tensor_scalar(m2[:, 0:GU], m2[:, 0:GU], 1.0 / W, EPS_INNER, ALU.mult, ALU.add))
                    step(V.tensor_scalar(m2[:, GU:NS_], m2[:, GU:NS_], 1.0 / W, EPS_LN, ALU.mult, ALU.add))
                    own(s, "eps_h")
                    step(V.tensor_tensor(var[:, GH:], m2, diff, ALU.add))
                    own(s, "s_var")
                    inverse_root(nc, step, lambda name: own(s, name), rstd[:], root_tmp[:], var[:], "s_")
                    step(V.scalar_tensor_tensor(shift[:], mean2, -0.5, rstd[:, GH:], ALU.mult, ALU.mult))
                    own(s, "shift")

                def h_norm(s):
                    for j in range(GU):
                        n = GU + j
                        step(V.tensor_scalar(h2[s.par][:, j, :], unit_pair(h_bank[j // 2])[:, j % 2, :],
                                             rstd[:, GH + n:GH + n + 1], shift[:, n:n + 1], ALU.mult, ALU.add))

                def o_norm(s):
                    dve.wait_ge(side_pe, s.at(SIDE_PE, "oT1", 1))
                    for j in range(GU):
                        step(V.tensor_scalar(normed[:, j, :], O[1 - s.par][:, j, :], rstd[:, GH + j:GH + j + 1],
                                             shift[:, j:j + 1], ALU.mult, ALU.add))
                    own(s, f"o_norm{GU - 1}")
                    dve.wait_ge(side_pool, s.at(SIDE_POOL, "gate_bias", 1))
                    step(V.tensor_tensor(normed[:], normed[:], gate_w[1 - s.par][:], ALU.mult))
                    own(s, "weight")
                    step(V.tensor_tensor(normed[:], normed[:], gate_b[1 - s.par][:], ALU.add))

                def route(s):
                    names = iter(ROUTER)

                    def link(ins):
                        step(ins)
                        own(s, next(names))
                    ue = lambda t: t[:].rearrange("p (u e) -> p u e", e=E)
                    c_ = lambda k: bcast(col[:, k, :], 2, E)
                    dve.wait_ge(side_pe, s.at(SIDE_PE, "logits"))
                    link(V.tensor_copy(logit[:], turn["logits"][:, 0:GU * E]))
                    link(V.tensor_reduce(col[:, 0, :], ue(logit), AX, ALU.max))
                    link(V.tensor_tensor(ue(logit), ue(logit), c_(0), ALU.subtract))
                    dve.wait_ge(side_act, s.at(SIDE_ACT, "exp"))
                    link(V.tensor_reduce(col[:, 1, :], ue(picked), AX, ALU.add))
                    link(V.reciprocal(col[:, 1, :], col[:, 1, :]))
                    link(V.tensor_tensor(ue(gates), ue(picked), c_(1), ALU.mult))
                    link(V.tensor_copy(picked[:], gates[:]))
                    for k in range(2):
                        link(V.tensor_reduce(col[:, 2, :], ue(picked), AX, ALU.max))
                        link(V.tensor_tensor(ue(eq), ue(picked), c_(2), ALU.is_equal))
                        link(V.tensor_tensor(ue(score), ue(eq), bcast(rank[:, :], 1, GU), ALU.mult))
                        link(V.tensor_reduce(col[:, 3, :], ue(score), AX, ALU.max))
                        link(V.tensor_tensor(ue(eq), ue(score), c_(3), ALU.is_equal))
                        link(V.scalar_tensor_tensor(picked[:], eq[:], -2.0, picked[:], ALU.mult, ALU.add))
                    link(V.tensor_scalar(eq[:], picked[:], 0.0, None, ALU.is_lt))
                    link(V.tensor_tensor(gates[:], gates[:], eq[:], ALU.mult))
                    link(V.tensor_reduce(col[:, 4, :], ue(gates), AX, ALU.add))
                    link(V.tensor_scalar(col[:, 4, :], col[:, 4, :], EPS_GATE, None, ALU.add))
                    link(V.reciprocal(col[:, 4, :], col[:, 4, :]))
                    link(V.tensor_tensor(ue(gates), ue(gates), c_(4), ALU.mult))

                def expert(x, e):
                    a, h = acc[x.par], h2[x.par]
                    if e == 0:
                        dve.wait_ge(out_stored[x.par], x.i * 16 + 16 * (x.c // 2 + 1))
                    for j in range(GU):
                        if j % 2 == 0:
                            dve.wait_ge(pe_filled, x.at(MPE, f"y{e}_{j // 2}"))
                        if e > 0:
                            dve.wait_ge(dve_done, x.at(MDVE, f"y{e - 1}_{j}"))
                        V.scalar_tensor_tensor(a[:, j, :], y_bank[j // 2][:, (j % 2) * W:(j % 2 + 1) * W],
                                               gates[:, j * E + e:j * E + e + 1], (h if e == 0 else a)[:, j, :],
                                               ALU.mult, ALU.add).then_inc(dve_done, 1)

                one = lambda x: lambda j: acc[x.par][:, j, :]
                fstep = lambda ins: ins.then_inc(final_done, 1)
                fown = lambda x: lambda name: dve.wait_ge(final_done, x.at(FINAL, name))

                def moe_norm(x):
                    dve.wait_ge(dve_done, x.at(MDVE, MDVE[-1]))
                    layer_norm(nc, fstep, fown(x), one(x), one(x), stats, mv, rs, EPS_LN, "m_")

                def residual(x):
                    a = acc[x.par]
                    fstep(V.tensor_tensor(a[:], a[:], bcast(gamma[:, :], 1, GU), ALU.mult))
                    fown(x)("gamma")
                    fstep(V.tensor_tensor(a[:], a[:], bcast(beta[:, :], 1, GU), ALU.add))
                    fown(x)("beta")
                    fstep(V.tensor_tensor(a[:], a[:], h2[x.par][:], ALU.add))

                def final_norm(x):
                    fown(x)("residual")
                    layer_norm(nc, fstep, fown(x), one(x), one(x), stats, mv, rs, EPS_LN, "f_")

                def part(s, present, do, first, after):
                    if present:
                        do(s)
                    else:
                        skip(s, first, after)

                def body(s, has):
                    if isinstance(s.i, int) and s.c == 2:
                        dve.wait_ge(router_loaded, 16 * 6)
                        dve.wait_ge(experts_loaded, 16 * 6)
                    x = s.before(3)
                    experts = lambda *es: [expert(x, e) for e in es if has[3]]
                    part(s, has[0], center, "i_mean", "o_bn0")
                    experts(0)
                    if has[4]:
                        moe_norm(s.before(4))
                    experts(1)
                    if has[4]:
                        residual(s.before(4))
                    part(s, has[1], o_stats, "o_bn0", "h_bn0")
                    part(s, has[2], h_stats, "h_bn0", "i_var")
                    experts(2)
                    part(s, has[0], head_var, "i_var", "sum")
                    part(s, has[0] or has[1] or has[2], lambda s: deviations(s, has), "sum", "h_norm0")
                    experts(3)
                    part(s, has[2], h_norm, "h_norm0", "o_norm0")
                    experts(4)
                    part(s, has[1], o_norm, "o_norm0", "r_copy")
                    experts(5)
                    if has[4]:
                        final_norm(s.before(4))
                    experts(6, 7)
                    part(s, has[2], route, "r_copy", None)
                rounds(dve, body)


def build(nc, A, out):
    dram = lambda name, shape: nc.dram_tensor(name, shape, F32, kind="Internal").ap()
    hT = dram("hT", (NU + SPARE, W, P))
    attn = dram("attn", (NU + 1, P, W))
    q_dram = dram("q", (NU + 2, P, W))
    with ExitStack() as ctx:
        ident = ctx.enter_context(nc.sbuf_tensor("ident_sb", [P, P], F32))
        weights = output_weights(nc, A, ctx)
        with ExitStack() as scan_ctx:
            LR = scan_ctx.enter_context(nc.sbuf_tensor("LR", [P, NU * NH], F32))
            constants = scan_constants(nc, A, scan_ctx)
            tokenizer(nc, A, hT, LR, ident, constants)
            scan(nc, A, hT, attn, q_dram, LR, ident, constants, weights)
        outputs(nc, A, hT, attn, q_dram, out, ident, weights)


def layouts(v):
    def patches(x, side):
        p = 64 // side
        t = x.reshape(B, CH, side, p, side, p).transpose(2, 4, 3, 5, 1, 0)
        return t.reshape(side * side, B * p * p * CH)
    a = {"x0": patches(v["x"], 64), "x1": patches(v["x"], 32), "x2": patches(v["x"], 16)}
    for k in range(3):
        parts = max(1, P // GROUPS[k])
        a[f"idx{k}"] = v[f"L0_tok_idx{k}"].reshape(GROUPS[k], parts, GP // parts).transpose(1, 0, 2).reshape(
            parts * GROUPS[k], GP // parts)
        a[f"W{k}T"] = v[f"L0_tok_W{k}"].T
        a[f"b{k}"] = v[f"L0_tok_b{k}"].reshape(EMB, 1)
    a["WfT"], a["bf"] = v["L0_tok_Wf"].T, v["L0_tok_bf"].reshape(1, W)
    a["Wf"], a["bf_col"] = v["L0_tok_Wf"], v["L0_tok_bf"].reshape(W, 1)
    t = lambda n: v["L0_attn_" + n]
    a["lrT"], a["lrb"] = t("lr_weight").reshape(NH, W).T, t("lr_bias").reshape(1, NH)
    a["Wqkv"] = np.concatenate([t("Wq"), t("Wk"), t("Wv")], axis=1)
    a["learn"] = t("learnable_token_idx").reshape(1, MB)
    a["lnw"], a["lnb"] = t("norm_weight").reshape(1, W), t("norm_bias").reshape(1, W)
    a["ab1"], a["ab2"] = t("b1").reshape(NH // 2, 2 * F).T, t("b2").reshape(1, NH * D)
    a["W1"], a["W2"], a["Wg"], a["Wo"] = t("W1"), t("W2"), t("Wg"), t("Wo")
    a["pw"], a["pb"] = t("post_norm_weight").reshape(1, W), t("post_norm_bias").reshape(1, W)
    f = lambda n: v["L0_ffn_" + n]
    a["fw1"], a["fb1"], a["fw2"], a["fb2"] = f("w1"), f("b1").reshape(1, W // 2), f("w2"), f("b2").reshape(1, E)
    a["down"], a["downb"], a["up"] = f("down_w"), f("down_b").reshape(1, E * DE), f("up_w").reshape(E * DE, W)
    a["gamma"], a["beta"] = f("gamma").reshape(1, W), f("beta").reshape(1, W)
    i = np.arange(P)
    same = (i[:, None] // MB) == (i[None, :] // MB)
    a["ident"] = np.eye(P, dtype=np.float32)
    a["block_mask"] = same.astype(np.float32)
    a["triu_mask"] = (same & (i[:, None] <= i[None, :])).astype(np.float32)
    a["recip"] = np.tile(np.float32(1) / np.arange(1, MB + 1, dtype=np.float32), (P, 1))
    a["rank"] = np.arange(E, 0, -1, dtype=np.float32).reshape(1, E)
    return {k: np.ascontiguousarray(x) for k, x in a.items()}


def kernel(**inputs):
    import concourse.bacc as bacc
    from concourse.bass_utils import run_bass_kernel_spmd
    nc = bacc.Bacc("TRN2", target_bir_lowering=False, num_devices=1)
    arrays = layouts({k: np.asarray(x) for k, x in inputs.items()})
    aps = {k: nc.dram_tensor(f"in_{k}", x.shape, mybir.dt.from_np(x.dtype), kind="ExternalInput").ap()
           for k, x in arrays.items()}
    out = nc.dram_tensor("out", (NU, P, W), F32, kind="ExternalOutput").ap()
    build(nc, aps, out)
    r = run_bass_kernel_spmd(nc, [{f"in_{k}": x for k, x in arrays.items()}], core_ids=[0])
    y = r.results[0]["out"].reshape(NS, B // BH, BH, MB, W)
    return y.transpose(1, 2, 0, 3, 4).reshape(B, T, W)
```
